# Optimizing a Trainium2 kernel written in Bass

```python
import numpy as np
import jax
import jax.numpy as jnp

def _softmax(x, axis=-1):
    return jax.nn.softmax(x, axis=axis)

def _gelu(x):
    return jax.nn.gelu(x, approximate=True)

def _silu(x):
    return jax.nn.silu(x)

def _sigmoid(x):
    return jax.nn.sigmoid(x)

def _layernorm(x, axis=-1, eps=1e-05):
    m = jnp.mean(x, axis=axis, keepdims=True)
    v = jnp.var(x, axis=axis, keepdims=True)
    return (x - m) / jnp.sqrt(v + eps)

def _scatter_add(tgt, idx, src, axis=0):
    return tgt.at[idx].add(src)

def _segment_sum(src, seg, n):
    return jax.ops.segment_sum(src, seg, n)
kernel_name = 'mk_flamingo_gated_d2_seqx_r8_f6f84d'

def setup_inputs(seed: int=0):
    np.random.seed(seed)
    _w = jnp.asarray

    def _rec_inputs():
        import jax
        import jax.numpy as jnp
        _rk = jax.random.key(seed)
        x = -0.0002928 + 1 * jax.random.normal(jax.random.fold_in(_rk, 1), (32, 100, 128), jnp.float32)
        _lenS = 100 - jax.random.randint(jax.random.fold_in(_rk, 7), (32,), 0, max(1, 100 // 4) + 1, jnp.int32)
        _lenS2 = 1444 - jax.random.randint(jax.random.fold_in(_rk, 8), (32,), 0, max(1, 1444 // 4) + 1, jnp.int32)
        _ctx_1024P = jax.random.normal(jax.random.fold_in(_rk, 11), (32, 16, 128), jnp.float32)
        _ctx_1024c = jax.random.dirichlet(jax.random.fold_in(_rk, 511), 0.3 * jnp.ones((16,), jnp.float32), (32, 1444))
        _ctx_1024t = jnp.einsum('bsk,bkd->bsd', _ctx_1024c, _ctx_1024P)
        _ctx_1024t = _ctx_1024t * jax.lax.rsqrt(jnp.mean(jnp.square(_ctx_1024t)) + 1e-12) * 0.953939
        ctx_1024 = -1.39393e-06 + 0.999914 * (_ctx_1024t + 0.3 * jax.random.normal(jax.random.fold_in(_rk, 611), (32, 1444, 128), jnp.float32))
        _validS = jnp.arange(100)[None, :] < _lenS[:, None]
        _validS2 = jnp.arange(1444)[None, :] < _lenS2[:, None]
        _causal = jnp.tril(jnp.ones((100, 100), dtype=bool))
        mask_SxS2_bk0 = jnp.logical_not(jnp.broadcast_to(_validS2[0:1, :], (100, 1444)))
        _g = jax.random.normal(jax.random.fold_in(_rk, 9001), (2, 2), jnp.float32)
        _g = jnp.sign(_g) * jnp.maximum(jnp.abs(_g), 1.0) + (_g == 0) * 1.0
        g_xattn = _g[0]
        g_ffn = _g[1]
        return (x, ctx_1024, mask_SxS2_bk0, g_xattn, g_ffn)
    x, ctx_1024, mask_SxS2_bk0, g_xattn, g_ffn = _rec_inputs()

    def _L0_xattn_setup():
        import jax, jax.numpy as jnp
        import numpy as np
        DIM = 128
        HEADS = 16
        HEAD_DIM = DIM // HEADS
        SCALE = HEAD_DIM ** (-0.5)
        key = jax.random.key(seed)
        ks = jax.random.split(key, 7)
        b, n = (2, 256)
        x1 = jax.random.normal(ks[0], (b, n, DIM), dtype=jnp.float32)
        x2 = jax.random.normal(ks[1], (b, n, DIM), dtype=jnp.float32)
        s = DIM ** (-0.5)
        wq = jax.random.normal(ks[2], (DIM, DIM), dtype=jnp.float32) * s
        wk = jax.random.normal(ks[3], (DIM, DIM), dtype=jnp.float32) * s
        wv = jax.random.normal(ks[4], (DIM, DIM), dtype=jnp.float32) * s
        wo = jax.random.normal(ks[5], (DIM, DIM), dtype=jnp.float32) * s
        bo = jax.random.normal(ks[6], (DIM,), dtype=jnp.float32) * 0.01
        return {'x1': x1, 'x2': x2, 'wq': wq, 'wk': wk, 'wv': wv, 'wo': wo, 'bo': bo}
    _L0_xattn_all = _L0_xattn_setup()
    _L0_xattn_in = {k: v for k, v in _L0_xattn_all.items() if k in ('wq', 'wk', 'wv', 'wo', 'bo')}
    del _L0_xattn_all

    def _L0_ffn_setup():
        import jax, jax.numpy as jnp
        import numpy as np
        NUM_NOD = 6
        MAX_PREV = 5
        NUM_EDGE = 20
        D = 128
        H = 8
        LN_EPS = 1e-06

        def _layernorm(x, g, b):
            mu = jnp.mean(x, axis=-1, keepdims=True)
            var = jnp.mean(jnp.square(x - mu), axis=-1, keepdims=True)
            return (x - mu) * jax.lax.rsqrt(var + LN_EPS) * g + b

        def _mha(q, k, v, wq, wk, wv, wo):
            B, S, d = q.shape
            dh = d // H
            qh = (q @ wq).reshape(B, S, H, dh)
            kh = (k @ wk).reshape(B, S, H, dh)
            vh = (v @ wv).reshape(B, S, H, dh)
            scores = jnp.einsum('bqhd,bkhd->bhqk', qh, kh) / jnp.sqrt(jnp.asarray(dh, q.dtype))
            attn = jax.nn.softmax(scores, axis=-1)
            ctx = jnp.einsum('bhqk,bkhd->bqhd', attn, vh).reshape(B, S, d)
            return ctx @ wo
        key = jax.random.key(seed)
        ks = jax.random.split(key, 12)
        B, S = (8, 128)
        scale = 1.0 / np.sqrt(D)
        return {'inputs': jax.random.normal(ks[0], (B, S, D), jnp.float32), 'ew': jax.random.uniform(ks[1], (NUM_NOD, 3), jnp.float32), 'act_w': jax.random.uniform(ks[2], (NUM_NOD,), jnp.float32), 'We': jax.random.normal(ks[3], (NUM_EDGE, D, D), jnp.float32) * scale, 'be': jnp.zeros((NUM_EDGE, D), jnp.float32), 'Wq': jax.random.normal(ks[4], (NUM_NOD, D, D), jnp.float32) * scale, 'Wk': jax.random.normal(ks[5], (NUM_NOD, D, D), jnp.float32) * scale, 'Wv': jax.random.normal(ks[6], (NUM_NOD, D, D), jnp.float32) * scale, 'Wo': jax.random.normal(ks[7], (NUM_NOD, D, D), jnp.float32) * scale, 'ln_g': jnp.ones((D,), jnp.float32), 'ln_b': jnp.zeros((D,), jnp.float32)}
    _L0_ffn_all = _L0_ffn_setup()
    _L0_ffn_in = {k: v for k, v in _L0_ffn_all.items() if k in ('ew', 'act_w', 'We', 'be', 'Wq', 'Wk', 'Wv', 'Wo', 'ln_g', 'ln_b')}
    del _L0_ffn_all

    def _L1_xattn_setup():
        import jax, jax.numpy as jnp
        import numpy as np
        B, S, DIM, H = (4, 256, 128, 16)
        HD = DIM // H
        SCALE = HD ** (-0.5)

        def _heads(x):
            b, s, _ = x.shape
            return x.reshape(b, s, H, HD).transpose(0, 2, 1, 3)
        key = jax.random.key(seed)
        ks = jax.random.split(key, 7)
        init = 0.02
        return {'query': jax.random.normal(ks[0], (B, S, DIM), dtype=jnp.float32), 'key': jax.random.normal(ks[1], (B, S, DIM), dtype=jnp.float32), 'value': jax.random.normal(ks[2], (B, S, DIM), dtype=jnp.float32), 'attn_mask': jnp.tril(jnp.ones((S, S), dtype=bool)), 'Wq': jax.random.normal(ks[3], (DIM, DIM), dtype=jnp.float32) * init, 'Wk': jax.random.normal(ks[4], (DIM, DIM), dtype=jnp.float32) * init, 'Wv': jax.random.normal(ks[5], (DIM, DIM), dtype=jnp.float32) * init, 'Wo': jax.random.normal(ks[6], (DIM, DIM), dtype=jnp.float32) * init}
    _L1_xattn_all = _L1_xattn_setup()
    _L1_xattn_in = {k: v for k, v in _L1_xattn_all.items() if k in ('Wq', 'Wk', 'Wv', 'Wo')}
    del _L1_xattn_all

    def _L1_ffn_setup():
        import jax, jax.numpy as jnp
        import numpy as np
        H = 16
        TOP_K = 2
        EPS = 1e-05

        def _layer_norm(x, g, b):
            m = x.mean(-1, keepdims=True)
            v = ((x - m) ** 2).mean(-1, keepdims=True)
            return (x - m) * jax.lax.rsqrt(v + EPS) * g + b

        def _block(x, ln1_g, ln1_b, ln2_g, ln2_b, w_qkv, w_o, w_gate, w1, b1, w2, b2):
            B, S, D = x.shape
            hd = D // H
            h = _layer_norm(x, ln1_g, ln1_b)
            qkv = h @ w_qkv
            q, k, v = jnp.split(qkv, 3, axis=-1)
            q = q.reshape(B, S, H, hd)
            k = k.reshape(B, S, H, hd)
            v = v.reshape(B, S, H, hd)
            scores = jnp.einsum('bqhd,bkhd->bhqk', q, k) * hd ** (-0.5)
            causal = jnp.tril(jnp.ones((S, S), bool))
            scores = jnp.where(causal, scores, jnp.finfo(scores.dtype).min)
            attn = jax.nn.softmax(scores, axis=-1)
            o = jnp.einsum('bhqk,bkhd->bqhd', attn, v).reshape(B, S, D)
            x_resid = x + o @ w_o
            moe_in = _layer_norm(x_resid, ln2_g, ln2_b)
            N = B * S
            xf = moe_in.reshape(N, D)
            probs = jax.nn.softmax(xf @ w_gate, axis=-1)
            top_w, top_i = jax.lax.top_k(probs, TOP_K)
            top_w = top_w / top_w.sum(-1, keepdims=True)
            E = w1.shape[0]
            out = jnp.zeros_like(xf)
            for e in range(E):
                gate_e = jnp.sum(jnp.where(top_i == e, top_w, 0.0), axis=-1)
                he = jax.nn.gelu(xf @ w1[e] + b1[e])
                out = out + gate_e[:, None] * (he @ w2[e] + b2[e])
            return out.reshape(B, S, D) + x_resid
        key = jax.random.key(seed)
        ks = jax.random.split(key, 12)
        B, S, D, F, E = (8, 64, 128, 512, 8)
        inp = {'x': jax.random.normal(ks[0], (B, S, D), jnp.float32), 'ln1_g': jnp.ones((D,), jnp.float32), 'ln1_b': jnp.zeros((D,), jnp.float32), 'ln2_g': jnp.ones((D,), jnp.float32), 'ln2_b': jnp.zeros((D,), jnp.float32), 'w_qkv': jax.random.normal(ks[1], (D, 3 * D), jnp.float32) * D ** (-0.5), 'w_o': jax.random.normal(ks[2], (D, D), jnp.float32) * D ** (-0.5), 'w_gate': jax.random.normal(ks[3], (D, E), jnp.float32) * D ** (-0.5), 'w1': jax.random.normal(ks[4], (E, D, F), jnp.float32) * D ** (-0.5), 'b1': jnp.zeros((E, F), jnp.float32), 'w2': jax.random.normal(ks[5], (E, F, D), jnp.float32) * F ** (-0.5), 'b2': jnp.zeros((E, D), jnp.float32)}
        return inp
    _L1_ffn_all = _L1_ffn_setup()
    _L1_ffn_in = {k: v for k, v in _L1_ffn_all.items() if k in ('ln1_g', 'ln1_b', 'ln2_g', 'ln2_b', 'w_qkv', 'w_o', 'w_gate', 'w1', 'b1', 'w2', 'b2')}
    del _L1_ffn_all
    return {'x': x, 'ctx_1024': ctx_1024, 'mask_SxS2_bk0': mask_SxS2_bk0, 'g_xattn': g_xattn, 'g_ffn': g_ffn, 'L0_xattn_wq': _L0_xattn_in['wq'], 'L0_xattn_wk': _L0_xattn_in['wk'], 'L0_xattn_wv': _L0_xattn_in['wv'], 'L0_xattn_wo': _L0_xattn_in['wo'], 'L0_xattn_bo': _L0_xattn_in['bo'], 'L0_ffn_ew': _L0_ffn_in['ew'], 'L0_ffn_act_w': _L0_ffn_in['act_w'], 'L0_ffn_We': _L0_ffn_in['We'], 'L0_ffn_be': _L0_ffn_in['be'], 'L0_ffn_Wq': _L0_ffn_in['Wq'], 'L0_ffn_Wk': _L0_ffn_in['Wk'], 'L0_ffn_Wv': _L0_ffn_in['Wv'], 'L0_ffn_Wo': _L0_ffn_in['Wo'], 'L0_ffn_ln_g': _L0_ffn_in['ln_g'], 'L0_ffn_ln_b': _L0_ffn_in['ln_b'], 'L1_xattn_Wq': _L1_xattn_in['Wq'], 'L1_xattn_Wk': _L1_xattn_in['Wk'], 'L1_xattn_Wv': _L1_xattn_in['Wv'], 'L1_xattn_Wo': _L1_xattn_in['Wo'], 'L1_ffn_ln1_g': _L1_ffn_in['ln1_g'], 'L1_ffn_ln1_b': _L1_ffn_in['ln1_b'], 'L1_ffn_ln2_g': _L1_ffn_in['ln2_g'], 'L1_ffn_ln2_b': _L1_ffn_in['ln2_b'], 'L1_ffn_w_qkv': _L1_ffn_in['w_qkv'], 'L1_ffn_w_o': _L1_ffn_in['w_o'], 'L1_ffn_w_gate': _L1_ffn_in['w_gate'], 'L1_ffn_w1': _L1_ffn_in['w1'], 'L1_ffn_b1': _L1_ffn_in['b1'], 'L1_ffn_w2': _L1_ffn_in['w2'], 'L1_ffn_b2': _L1_ffn_in['b2']}

def reference(x, ctx_1024, mask_SxS2_bk0, g_xattn, g_ffn, L0_xattn_wq, L0_xattn_wk, L0_xattn_wv, L0_xattn_wo, L0_xattn_bo, L0_ffn_ew, L0_ffn_act_w, L0_ffn_We, L0_ffn_be, L0_ffn_Wq, L0_ffn_Wk, L0_ffn_Wv, L0_ffn_Wo, L0_ffn_ln_g, L0_ffn_ln_b, L1_xattn_Wq, L1_xattn_Wk, L1_xattn_Wv, L1_xattn_Wo, L1_ffn_ln1_g, L1_ffn_ln1_b, L1_ffn_ln2_g, L1_ffn_ln2_b, L1_ffn_w_qkv, L1_ffn_w_o, L1_ffn_w_gate, L1_ffn_w1, L1_ffn_b1, L1_ffn_w2, L1_ffn_b2):
    import jax
    import jax.numpy as jnp

    def _L0_xattn_ref(x1, x2, wq, wk, wv, wo, bo):
        import jax, jax.numpy as jnp
        import numpy as np
        DIM = 128
        HEADS = 16
        HEAD_DIM = DIM // HEADS
        SCALE = HEAD_DIM ** (-0.5)
        b, n, _ = x1.shape
        m = x2.shape[1]
        q = (x1 @ wq.T).reshape(b, n, HEADS, HEAD_DIM).transpose(0, 2, 1, 3)
        k = (x2 @ wk.T).reshape(b, m, HEADS, HEAD_DIM).transpose(0, 2, 1, 3)
        v = (x2 @ wv.T).reshape(b, m, HEADS, HEAD_DIM).transpose(0, 2, 1, 3)
        dots = jnp.einsum('bhnd,bhmd->bhnm', q, k) * SCALE
        attn = jax.nn.softmax(dots, axis=-1)
        out = jnp.einsum('bhnm,bhmd->bhnd', attn, v)
        out = out.transpose(0, 2, 1, 3).reshape(b, n, DIM)
        return out @ wo.T + bo

    def _L0_ffn_ref(inputs, ew, act_w, We, be, Wq, Wk, Wv, Wo, ln_g, ln_b):
        import jax, jax.numpy as jnp
        import numpy as np
        NUM_NOD = 6
        MAX_PREV = 5
        NUM_EDGE = 20
        D = 128
        H = 8
        LN_EPS = 1e-06

        def _layernorm(x, g, b):
            mu = jnp.mean(x, axis=-1, keepdims=True)
            var = jnp.mean(jnp.square(x - mu), axis=-1, keepdims=True)
            return (x - mu) * jax.lax.rsqrt(var + LN_EPS) * g + b

        def _mha(q, k, v, wq, wk, wv, wo):
            B, S, d = q.shape
            dh = d // H
            qh = (q @ wq).reshape(B, S, H, dh)
            kh = (k @ wk).reshape(B, S, H, dh)
            vh = (v @ wv).reshape(B, S, H, dh)
            scores = jnp.einsum('bqhd,bkhd->bhqk', qh, kh) / jnp.sqrt(jnp.asarray(dh, q.dtype))
            attn = jax.nn.softmax(scores, axis=-1)
            ctx = jnp.einsum('bhqk,bkhd->bqhd', attn, vh).reshape(B, S, d)
            return ctx @ wo
        nodes = {-1: inputs}
        lind = 0
        for c in range(NUM_NOD):
            nsrc = min(c + 1, MAX_PREV)
            snode = c - nsrc
            eq, ek, ev = (lind + nsrc - 1, lind, lind + nsrc // 2)
            in_q, in_k, in_v = (c - 1, snode, snode + nsrc // 2)
            q = ew[c, 0] * (nodes[in_q] @ We[eq] + be[eq])
            k = ew[c, 1] * (nodes[in_k] @ We[ek] + be[ek])
            v = ew[c, 2] * (nodes[in_v] @ We[ev] + be[ev])
            o = _mha(q, k, v, Wq[c], Wk[c], Wv[c], Wo[c])
            nodes[c] = act_w[c] * o + q
            lind += nsrc
        out = nodes[NUM_NOD - 1]
        return _layernorm(out, ln_g, ln_b)

    def _L1_xattn_ref(query, key, value, attn_mask, Wq, Wk, Wv, Wo):
        import jax, jax.numpy as jnp
        import numpy as np
        B, S, DIM, H = (4, 256, 128, 16)
        HD = DIM // H
        SCALE = HD ** (-0.5)

        def _heads(x):
            b, s, _ = x.shape
            return x.reshape(b, s, H, HD).transpose(0, 2, 1, 3)
        q = _heads(query @ Wq.T)
        k = _heads(key @ Wk.T)
        v = _heads(value @ Wv.T)
        logits = jnp.einsum('bhqd,bhkd->bhqk', q, k) * SCALE
        mask = attn_mask[None, None, :, :]
        masked = jnp.where(mask, logits, -1000000000.0)
        weights = jax.nn.softmax(masked, axis=-1)
        weights = weights * mask.astype(weights.dtype)
        denom = jnp.maximum(weights.sum(axis=-1, keepdims=True), 1e-09)
        weights = weights / denom
        out = jnp.einsum('bhqk,bhkd->bhqd', weights, v)
        out = out.transpose(0, 2, 1, 3).reshape(query.shape[0], query.shape[1], -1)
        return out @ Wo.T

    def _L1_ffn_ref(x, ln1_g, ln1_b, ln2_g, ln2_b, w_qkv, w_o, w_gate, w1, b1, w2, b2):
        import jax, jax.numpy as jnp
        import numpy as np
        H = 16
        TOP_K = 2
        EPS = 1e-05

        def _layer_norm(x, g, b):
            m = x.mean(-1, keepdims=True)
            v = ((x - m) ** 2).mean(-1, keepdims=True)
            return (x - m) * jax.lax.rsqrt(v + EPS) * g + b

        def _block(x, ln1_g, ln1_b, ln2_g, ln2_b, w_qkv, w_o, w_gate, w1, b1, w2, b2):
            B, S, D = x.shape
            hd = D // H
            h = _layer_norm(x, ln1_g, ln1_b)
            qkv = h @ w_qkv
            q, k, v = jnp.split(qkv, 3, axis=-1)
            q = q.reshape(B, S, H, hd)
            k = k.reshape(B, S, H, hd)
            v = v.reshape(B, S, H, hd)
            scores = jnp.einsum('bqhd,bkhd->bhqk', q, k) * hd ** (-0.5)
            causal = jnp.tril(jnp.ones((S, S), bool))
            scores = jnp.where(causal, scores, jnp.finfo(scores.dtype).min)
            attn = jax.nn.softmax(scores, axis=-1)
            o = jnp.einsum('bhqk,bkhd->bqhd', attn, v).reshape(B, S, D)
            x_resid = x + o @ w_o
            moe_in = _layer_norm(x_resid, ln2_g, ln2_b)
            N = B * S
            xf = moe_in.reshape(N, D)
            probs = jax.nn.softmax(xf @ w_gate, axis=-1)
            top_w, top_i = jax.lax.top_k(probs, TOP_K)
            top_w = top_w / top_w.sum(-1, keepdims=True)
            E = w1.shape[0]
            out = jnp.zeros_like(xf)
            for e in range(E):
                gate_e = jnp.sum(jnp.where(top_i == e, top_w, 0.0), axis=-1)
                he = jax.nn.gelu(xf @ w1[e] + b1[e])
                out = out + gate_e[:, None] * (he @ w2[e] + b2[e])
            return out.reshape(B, S, D) + x_resid
        return _block(x, ln1_g, ln1_b, ln2_g, ln2_b, w_qkv, w_o, w_gate, w1, b1, w2, b2)
    x = x + jnp.tanh(g_xattn[0]) * _L0_xattn_ref(_layernorm(x, axis=-1), ctx_1024, L0_xattn_wq, L0_xattn_wk, L0_xattn_wv, L0_xattn_wo, L0_xattn_bo)
    x = x + jnp.tanh(g_ffn[0]) * _L0_ffn_ref(_layernorm(x, axis=-1), L0_ffn_ew, L0_ffn_act_w, L0_ffn_We, L0_ffn_be, L0_ffn_Wq, L0_ffn_Wk, L0_ffn_Wv, L0_ffn_Wo, L0_ffn_ln_g, L0_ffn_ln_b)
    x = x + jnp.tanh(g_xattn[1]) * _L1_xattn_ref(_layernorm(x, axis=-1), ctx_1024, ctx_1024, mask_SxS2_bk0, L1_xattn_Wq, L1_xattn_Wk, L1_xattn_Wv, L1_xattn_Wo)
    x = x + jnp.tanh(g_ffn[1]) * _L1_ffn_ref(_layernorm(x, axis=-1), L1_ffn_ln1_g, L1_ffn_ln1_b, L1_ffn_ln2_g, L1_ffn_ln2_b, L1_ffn_w_qkv, L1_ffn_w_o, L1_ffn_w_gate, L1_ffn_w1, L1_ffn_b1, L1_ffn_w2, L1_ffn_b2)
    return x

_drawn_inputs = setup_inputs


def setup_inputs(seed=0):
    import zlib

    import numpy as np

    out = dict(_drawn_inputs(seed))
    spreads = {'g_ffn': (-1.0, 0.2),
     'L0_ffn_be': (0.0, 0.1),
     'L0_ffn_ln_g': (1.0, 0.2),
     'L0_ffn_ln_b': (0.0, 0.1),
     'L1_ffn_ln1_g': (1.0, 0.2),
     'L1_ffn_ln1_b': (0.0, 0.1),
     'L1_ffn_ln2_g': (1.0, 0.2),
     'L1_ffn_ln2_b': (0.0, 0.1),
     'L1_ffn_b1': (0.0, 0.1),
     'L1_ffn_b2': (0.0, 0.1)}
    factors = {'L0_ffn_Wq': 64.0, 'L0_ffn_Wk': 64.0, 'L1_xattn_Wq': 7.653, 'L1_xattn_Wk': 8.0}
    for name, (base, spread) in spreads.items():
        noise = np.random.default_rng([zlib.crc32(name.encode()), seed]).standard_normal(out[name].shape)
        drawn = base * np.exp(spread * noise) if base else spread * noise
        out[name] = jnp.asarray(drawn.astype(out[name].dtype))
    for name, factor in factors.items():
        out[name] = (out[name] * factor).astype(out[name].dtype)
    return out
```

```python
from contextlib import ExitStack

import concourse.bass as bass
from concourse import mybir

F32 = mybir.dt.float32
BF16 = mybir.dt.bfloat16
U8 = mybir.dt.uint8
ALU = mybir.AluOpType
ACT = mybir.ActivationFunctionType
AX_X = mybir.AxisListType.X

B, S, D = 32, 100, 128
SK = 1444
P = 128
XH, XD = 16, 8
CH = -(-SK // P)
LASTK = SK - (CH - 1) * P
COLS = [(0, 512), (512, 512), (1024, SK - 1024)]
PARTS = 5 * XH
NEG = -float(2 ** 30)
LN_EPS = 1e-5
L0_LN_EPS = 1e-6


def chunk_keys(c):
    return P if c < CH - 1 else LASTK


def col(ap, shape):
    for _ in range(len(shape) - 2):
        ap = ap.unsqueeze(1)
    return ap.to_broadcast(shape)


class Chain:

    def __init__(self, eng, sem, per, ahead=0):
        self.eng, self.sem, self.per, self.ahead, self.turn, self.k = eng, sem, per, ahead, 0, 0

    def begin(self, turn):
        self.turn, self.k = turn, 0

    def count(self, ins):
        self.k += 1
        ins.then_inc(self.sem, 1)

    def wait(self):
        self.eng.wait_ge(self.sem, self.turn * self.per + self.ahead + self.k)

    def link(self, ins):
        self.count(ins)
        self.wait()

    def end(self):
        assert self.k == self.per, (self.k, self.per)


class Shared:
    pass


class LayerNorm:

    def __init__(self, c, nc, name, rows, minus_half, n):
        def sb(what, shape):
            return c.enter_context(nc.sbuf_tensor(f"{name}_{what}", [rows] + shape, F32))

        self.n = n
        self.stats, self.mv, self.var, self.rstd = sb("stats", [n, 6]), sb("mv", [n, 2]), sb("var", [n]), sb("rstd", [n])
        self.held = sb("held", [1])
        self.minus_half = minus_half[0:rows, :].to_broadcast([rows, n])

    def inverse_root(self, nc):
        return nc.gpsimd.tensor_tensor(self.rstd[:, :], self.var[:, :], self.minus_half, ALU.pow)


def norm_stats(chain, nc, x, ln, eps, var_ready):
    for b in range(ln.n):
        chain.count(nc.vector.bn_stats(ln.stats[:, b, :], x[:, b, :]))
    chain.wait()
    chain.count(nc.vector.memset(ln.held[:, :], 0.0))
    for b in range(ln.n):
        chain.count(nc.vector.bn_aggr(ln.mv[:, b, :], ln.stats[:, b, :]))
    chain.wait()
    nc.vector.tensor_scalar(ln.var[:, :], ln.mv[:, :, 1], eps, None, ALU.add).then_inc(var_ready, 1)


def setup(nc, ctx, A):
    sh = Shared()

    def sb(name, shape, dt=F32):
        return ctx.enter_context(nc.sbuf_tensor(name, shape, dt))

    sh.x = sb("x_tokens", [S, B, D])
    sh.ident = sb("ident", [P, P])
    sh.ident_bf = sb("ident_bf", [P, P], BF16)
    sh.head16 = sb("head16", [P, 16])
    sh.head8 = sb("head8", [P, 8])
    sh.part_head = sb("part_head", [PARTS, 16])
    sh.ones_bf = sb("ones_bf", [PARTS, P], BF16)
    sh.minus_half = sb("minus_half", [P, 1])
    sh.tanh_g = sb("tanh_g", [P, 4])
    sh.cross_w = sb("cross_w", [P, 8, P])
    with ExitStack() as c:
        raw = c.enter_context(nc.sbuf_tensor("raw_w", [P, 8, P], F32))
        g = c.enter_context(nc.sbuf_tensor("g_raw", [P, 4], F32))
        ps = [c.enter_context(nc.psum_tensor(f"ps_w{i}", [P, 4, P], F32)) for i in range(2)]
        sem = {n: ctx.enter_context(nc.semaphore("setup_" + n)) for n in ("loaded", "x_loaded", "ident", "tp", "cp", "g")}
        names = ["L0_xattn_wq", "L0_xattn_wk", "L0_xattn_wv", "L0_xattn_wo", "L1_xattn_Wq", "L1_xattn_Wk", "L1_xattn_Wv", "L1_xattn_Wo"]
        with nc.Block() as block:
            @block.sync
            def _(sp):
                for n, name in enumerate(names):
                    sp.dma_start(raw[:, n, :], A[name]).then_inc(sem["loaded"], 16)
                sp.dma_start(sh.x[:, :, :], A["x"].rearrange("b s d -> s b d")).then_inc(sem["x_loaded"], 16)

            @block.gpsimd
            def _(pool):
                k = 0

                def link(ins):
                    nonlocal k
                    k += 1
                    ins.then_inc(sem["ident"], 1)
                    pool.wait_ge(sem["ident"], k)
                link(pool.memset(sh.ident[:, :], 0.0))
                link(pool.memset(sh.ident_bf[:, :], 0.0))
                link(pool.memset(sh.minus_half[:, :], -0.5))
                link(pool.memset(sh.part_head[:, :], 0.0))
                link(pool.memset(sh.head16[:, :], 1.0))
                link(pool.memset(sh.head8[:, :], 1.0))
                link(pool.memset(sh.ones_bf[:, :], 1.0))
                for m in (sh.ident, sh.ident_bf):
                    link(pool.affine_select(out=m[:, :], in_=m[:, :], compare_op=ALU.not_equal, fill=1.0, base=0,
                                            pattern=[[-1, P]], channel_multiplier=1))
                for part in range(3):
                    link(pool.affine_select(out=sh.part_head[:, :], in_=sh.part_head[:, :], compare_op=ALU.not_equal,
                                            fill=1.0, base=-16 * part, pattern=[[-1, 16]], channel_multiplier=1))
                for m, heads in ((sh.head16, 16), (sh.head8, 8)):
                    size = P // heads
                    link(pool.affine_select(out=m[:, :], in_=m[:, :], compare_op=ALU.is_ge, fill=0.0, base=0,
                                            pattern=[[-size, heads]], channel_multiplier=1))
                    link(pool.affine_select(out=m[:, :], in_=m[:, :], compare_op=ALU.is_ge, fill=0.0, base=size - 1,
                                            pattern=[[size, heads]], channel_multiplier=-1))

            @block.scalar
            def _(act):
                for n, name in enumerate(("g_xattn", "g_ffn")):
                    act.dma_start(g[:, 2 * n:2 * n + 2], A[name].partition_broadcast(P)).then_inc(sem["g"], 16)
                act.wait_ge(sem["g"], 32)
                nc.scalar.activation(sh.tanh_g[:, :], g[:, :], ACT.Tanh).then_inc(sem["g"], 1)
                for i in range(2):
                    act.wait_ge(sem["tp"], i + 1)
                    nc.scalar.copy(sh.cross_w[:, 4 * i:4 * i + 4, :], ps[i][:, :, :]).then_inc(sem["cp"], 1)

            @block.tensor
            def _(pe):
                pe.wait_ge(sem["loaded"], 128)
                pe.wait_ge(sem["ident"], 9)
                for i in range(2):
                    for j in range(4):
                        mm = nc.tensor.transpose(ps[i][:, j, :], raw[:, 4 * i + j, :], sh.ident[:, :])
                    mm.then_inc(sem["tp"], 1)

            @block.vector
            def _(dve):
                dve.wait_ge(sem["x_loaded"], 16)
                dve.wait_ge(sem["cp"], 2)
                dve.wait_ge(sem["g"], 33)
                dve.wait_ge(sem["ident"], 16)
    return sh


def cross_attention(nc, ctx, sh, A, layer):
    SCALE = float(XD) ** -0.5
    masked = layer == 1
    wqT, wkT, wvT, woT = (sh.cross_w[:, 4 * layer + n, :] for n in range(4))
    tanh_g = sh.tanh_g[0:S, layer:layer + 1]
    PIECES = XH * len(COLS)
    HALVES = 2 * CH
    PREP = 9
    MISC = 6

    c = ExitStack()
    with c:
        def sb(name, shape, dt=F32):
            return c.enter_context(nc.sbuf_tensor(f"x{layer}_{name}", shape, dt))

        def sem(name):
            return ctx.enter_context(nc.semaphore(f"x{layer}_{name}"))

        ctx_raw = [sb(f"ctx_raw{u}", [P, CH, D]) for u in range(2)]
        ctxT = sb("ctxT", [D, SK])
        kT = [sb(f"kT{u}", [D, SK]) for u in range(2)]
        v = [sb(f"v{u}", [P, CH, XH, XD + 1]) for u in range(2)]
        q_bd = [sb(f"q_bd{u}", [D, XH, S]) for u in range(2)]
        xn = sb("xn", [S, D])
        xnT = sb("xnT", [D, S])
        max_parts = sb("max_parts", [S, XH, len(COLS)])
        neg_max = sb("neg_max", [S, XH])
        rest = sb("rest", [S, 2, XH])
        parts = sb("parts", [S, 5, XH], BF16)
        max_bd = sb("max_bd", [PARTS, XH, S], BF16)
        probs = [sb(f"probs{r}", [P, 8 * S]) for r in range(3)]
        oT = sb("oT", [P, 4 * S])
        rden = sb("rden", [S, XH])
        o_n = sb("o_n", [S, D])
        o_nT = sb("o_nT", [D, S])
        ln = LayerNorm(c, nc, f"x{layer}_ln", S, sh.minus_half, 1)
        bo = None if masked else sb("bo", [S, D])
        if masked:
            mask_raw = sb("mask_raw", [S, SK], U8)
            mask_q = sb("mask_q", [S, SK], BF16)
            mask_k = sb("mask_k", [P, CH, S], BF16)

        ring = c.enter_context(nc.psum_tensor(f"x{layer}_ring", [P, 4, 512], F32))
        o_ps = c.enter_context(nc.psum_tensor(f"x{layer}_o_ps", [P, 512], F32))
        prep_ps = [c.enter_context(nc.psum_tensor(f"x{layer}_prep{r}", [P, 512], F32)) for r in range(2)]
        misc = c.enter_context(nc.psum_tensor(f"x{layer}_misc", [P, 512], F32))

        ctx_in = [sem(f"ctx_in{u}") for u in range(2)]
        prep_mm = sem("prep_mm")
        prep_out = sem("prep_out")
        piece_mm = sem("piece_mm")
        max_done = sem("max_done")
        half_mm = sem("half_mm")
        exp_done = sem("exp_done")
        pv_mm = sem("pv_mm")
        o_out = sem("o_out")
        pe_misc = sem("pe_misc")
        dve_misc = sem("dve_misc")
        dve_ready = sem("dve_ready")
        dve_chain = sem("dve_chain")
        tail_chain = sem("tail_chain")
        var_ready = sem("var_ready")
        rstd_ready = sem("rstd_ready")
        once = sem("once")
        bo_in = sem("bo_in")

        ONCE = 11 if masked else 10
        LINKS = 10 if masked else 11

        def batches(eng, body):
            with eng.Fori(0, B // 2 - 1) as i:
                body(i * 2, 0, False)
                body(i * 2 + 1, 1, False)
            body(B - 2, 0, False)
            body(B - 1, 1, True)

        with nc.Block() as block:
            @block.sync
            def _(sp):
                if masked:
                    sp.dma_start(mask_raw[:, :], A["mask_SxS2_bk0"]).then_inc(bo_in, 16)
                else:
                    sp.dma_start(bo[:, :], A["L0_xattn_bo"].partition_broadcast(S)).then_inc(bo_in, 16)

                def load(b, u):
                    body = (CH - 1) * P
                    sp.dma_start(ctx_raw[u][:, 0:CH - 1, :], A["ctx_1024"][b, 0:body, :].rearrange("(p c) d -> p c d", p=P)
                                 ).then_inc(ctx_in[u], 16)
                    sp.dma_start(ctx_raw[u][0:LASTK, CH - 1, :], A["ctx_1024"][b, body:SK, :]).then_inc(ctx_in[u], 16)
                load(0, 0)
                load(1, 1)
                with sp.Fori(1, B // 2) as i:
                    for u in range(2):
                        sp.wait_ge(prep_out, (i * 2 + u - 2) * PREP + 2 + 3)
                        load(i * 2 + u, u)

            @block.tensor
            def _(pe):
                pe.sem_inc(pv_mm, 3)

                def prep_kT(b, u):
                    for j, (c0, n) in enumerate(COLS):
                        m = j
                        r = (u * PREP + m) % 2
                        pe.wait_ge(prep_out, b * PREP + m + 1)
                        if j == 0:
                            pe.wait_ge(ctx_in[u], (b - u) * 16 + 32)
                        for ch in range(4 * j, min(4 * j + 4, CH)):
                            k = chunk_keys(ch)
                            mm = nc.tensor.transpose(prep_ps[r][:, (ch % 4) * P:(ch % 4) * P + k],
                                                     ctx_raw[u][0:k, ch, :], sh.ident[0:k, 0:k])
                        mm.then_inc(prep_mm, 1)
                    for j, (c0, n) in enumerate(COLS):
                        m = 3 + j
                        r = (u * PREP + m) % 2
                        pe.wait_ge(prep_out, b * PREP + m + 1)
                        pe.wait_ge(prep_out, b * PREP + 2 + j + 1)
                        nc.tensor.matmul(prep_ps[r][:, 0:n], wkT, ctxT[:, c0:c0 + n], start=True, stop=True
                                         ).then_inc(prep_mm, 1)

                def prep_v(b, u):
                    for j in range(3):
                        m = 6 + j
                        r = (u * PREP + m) % 2
                        pe.wait_ge(prep_out, b * PREP + m + 1)
                        for ch in range(4 * j, 4 * j + 4):
                            k = chunk_keys(ch)
                            mm = nc.tensor.matmul(prep_ps[r][0:k, (ch % 4) * P:(ch % 4) * P + P],
                                                  ctxT[:, ch * P:ch * P + k], wvT, start=True, stop=True)
                        mm.then_inc(prep_mm, 1)

                def xn_transpose(b, turn):
                    pe.wait_ge(dve_misc, turn)
                    pe.wait_ge(dve_ready, b * 2 + 1)
                    nc.tensor.transpose(misc[:, 0:S], xn[:, :], sh.ident[0:S, 0:S]).then_inc(pe_misc, 1)

                def q_product(b, turn):
                    pe.wait_ge(dve_misc, turn)
                    nc.tensor.matmul(misc[:, 0:S], wqT, xnT[:, :], start=True, stop=True).then_inc(pe_misc, 1)

                def batch(b, u, last):
                    turn = first + b * MISC
                    pe.wait_ge(prep_out, b * PREP + 2 + 6)
                    for h in range(XH):
                        for j, (c0, n) in enumerate(COLS):
                            i = h * len(COLS) + j
                            if i < 4:
                                pe.wait_ge(exp_done, 1 + b * HALVES)
                            else:
                                pe.wait_ge(max_done, b * PIECES + i - 3)
                            mm = nc.tensor.matmul(ring[0:S, i % 4, 0:n], q_bd[u][:, h, :], kT[u][:, c0:c0 + n],
                                                  start=True, stop=not masked)
                            if masked:
                                mm = nc.tensor.matmul(ring[0:S, i % 4, 0:n], sh.ident_bf[0:S, 0:S],
                                                      mask_q[:, c0:c0 + n], start=False, stop=True)
                            mm.then_inc(piece_mm, 1)
                    if not last:
                        prep_kT(b + 1, 1 - u)
                    pe.wait_ge(dve_ready, b * 2 + 2)
                    pe.wait_ge(dve_misc, turn)
                    nc.tensor.transpose(misc[0:PARTS, 0:S // 2].bitcast(BF16), parts[:, :, :].rearrange("q a h -> q (a h)"),
                                        sh.ident_bf[0:S, 0:S]).then_inc(pe_misc, 1)
                    if not last:
                        prep_v(b + 1, 1 - u)
                    pe.wait_ge(dve_misc, turn + 1)
                    pe.wait_ge(o_out, b + 1)

                    def values(i):
                        ch, half = i // 2, i % 2
                        pe.wait_ge(exp_done, 1 + b * HALVES + i + 1)
                        for j in range(4):
                            pair = 4 * half + j
                            mm = nc.tensor.matmul(o_ps[32 * j:32 * j + 2 * (XD + 1), half * 200:half * 200 + 200],
                                                  v[u][:, ch, 2 * pair:2 * pair + 2, :].rearrange("k h d -> k (h d)"),
                                                  probs[i % 3][:, j * 200:j * 200 + 200],
                                                  start=(i == 0), stop=(ch == CH - 1), skip_group_check=True)
                        mm.then_inc(pv_mm, 1)

                    for i in range(HALVES):
                        ch, half = i // 2, i % 2
                        k = chunk_keys(ch)
                        if i >= 2:
                            pe.wait_ge(exp_done, 1 + b * HALVES + i - 1)
                        for g in range(2):
                            h0 = 8 * half + 4 * g
                            bank = ring[0:k, 2 * (i % 2) + g, 0:4 * S]
                            nc.tensor.matmul(bank, kT[u][:, ch * P:ch * P + k],
                                             q_bd[u][:, h0:h0 + 4, :].rearrange("d h q -> d (h q)"), start=True, stop=False)
                            if masked:
                                nc.tensor.matmul(bank.rearrange("k (h q) -> k h q", h=4), sh.ident_bf[0:k, 0:k],
                                                 mask_k[0:k, ch, :].unsqueeze(1).to_broadcast([k, 4, S]),
                                                 start=False, stop=False)
                            mm = nc.tensor.matmul(bank, sh.ones_bf[:, 0:k],
                                                  max_bd[:, h0:h0 + 4, :].rearrange("p h q -> p (h q)"),
                                                  start=False, stop=True)
                        mm.then_inc(half_mm, 1)
                        if i >= 1:
                            values(i - 1)
                        if not last and i == 8:
                            xn_transpose(b + 1, turn + 1)
                        if not last and i == 12:
                            q_product(b + 1, turn + 2)
                    values(HALVES - 1)
                    turn += 1 if last else 3
                    pe.wait_ge(dve_misc, turn)
                    pe.wait_ge(o_out, b + 2)
                    for t in range(4):
                        mm = nc.tensor.transpose(misc[0:S, t * P:t * P + P], oT[:, t * S:t * S + S], sh.ident[:, :])
                    mm.then_inc(pe_misc, 1)
                    pe.wait_ge(dve_misc, turn + 1)
                    nc.tensor.transpose(misc[:, 0:S], o_n[:, :], sh.ident[0:S, 0:S]).then_inc(pe_misc, 1)
                    pe.wait_ge(dve_misc, turn + 2)
                    nc.tensor.matmul(misc[0:S, 0:D], o_nT[:, :], woT, start=True, stop=True).then_inc(pe_misc, 1)

                first = 2
                if masked:
                    first += 1
                    pe.wait_ge(once, ONCE)
                    mview, side = misc[:, :].bitcast(BF16), prep_ps[0][:, :].bitcast(BF16)
                    for ch in range(CH):
                        k = chunk_keys(ch)
                        dst = (mview[0:k, ch * S:ch * S + S] if ch < 10 else side[0:k, (ch - 10) * S:(ch - 10) * S + S])
                        mm = nc.tensor.transpose(dst, mask_q[:, ch * P:ch * P + k], sh.ident_bf[0:S, 0:S])
                    mm.then_inc(pe_misc, 1)
                    pe.wait_ge(dve_misc, 1)
                prep_kT(0, 0)
                prep_v(0, 0)
                xn_transpose(0, first - 2)
                q_product(0, first - 1)
                pe.wait_ge(dve_misc, first)
                batches(pe, batch)

            @block.gpsimd
            def _(pool):
                with pool.Fori(0, B) as b:
                    pool.wait_ge(var_ready, b + 1)
                    ln.inverse_root(nc).then_inc(rstd_ready, 1)

            @block.scalar
            def _(act):
                act.sem_inc(prep_out, 2)
                act.sem_inc(exp_done, 1)

                def prep(b, u):
                    for m in range(PREP):
                        r = (u * PREP + m) % 2
                        act.wait_ge(prep_mm, b * PREP + m + 1)
                        j = m % 3
                        c0, n = COLS[j]
                        if m < 3:
                            ins = nc.scalar.copy(ctxT[:, c0:c0 + n], prep_ps[r][:, 0:n])
                        elif m < 6:
                            ins = nc.scalar.copy(kT[u][:, c0:c0 + n], prep_ps[r][:, 0:n])
                        else:
                            whole = 4 if j < 2 else 3
                            ins = nc.scalar.copy(
                                v[u][:, 4 * j:4 * j + whole, :, 0:XD].rearrange("k c h d -> k (c h) d"),
                                prep_ps[r][:, 0:whole * P].rearrange("k (c d) -> k c d", d=XD))
                            if whole < 4:
                                ins = nc.scalar.copy(
                                    v[u][0:LASTK, CH - 1, :, 0:XD],
                                    prep_ps[r][0:LASTK, whole * P:4 * P].rearrange("k (h d) -> k h d", d=XD))
                        ins.then_inc(prep_out, 1)

                def batch(b, u, last):
                    if not last:
                        prep(b + 1, 1 - u)
                    for i in range(HALVES):
                        k = chunk_keys(i // 2)
                        act.wait_ge(half_mm, b * HALVES + i + 1)
                        act.wait_ge(pv_mm, b * HALVES + i + 1)
                        nc.scalar.activation(probs[i % 3][0:k, :].rearrange("k (g n) -> k g n", g=2),
                                             ring[0:k, 2 * (i % 2):2 * (i % 2) + 2, 0:4 * S], ACT.Exp, scale=SCALE
                                             ).then_inc(exp_done, 1)

                act.wait_ge(once, 6)
                prep(0, 0)
                batches(act, batch)

            @block.vector
            def _(dve):
                for u in range(2):
                    nc.vector.memset(v[u][:, :, :, :], 1.0).then_inc(once, 1)
                    dve.wait_ge(once, 3 * u + 1)
                    nc.vector.memset(v[u][:, CH - 1, :, :], 0.0).then_inc(once, 1)
                    dve.wait_ge(once, 3 * u + 2)
                    nc.vector.memset(v[u][0:LASTK, CH - 1, :, :], 1.0).then_inc(once, 1)
                nc.vector.memset(parts[:, :, :], 0.0).then_inc(once, 1)
                nc.vector.memset(o_ps[:, :], 0.0).then_inc(once, 1)
                nc.vector.memset(misc[:, :], 0.0).then_inc(once, 1)
                dve.wait_ge(bo_in, 16)
                if masked:
                    body = (CH - 1) * P
                    nc.vector.tensor_scalar(mask_q[:, 0:body].rearrange("q (c p) -> q c p", p=P),
                                            mask_raw[:, 0:body].rearrange("q (p c) -> q c p", p=P),
                                            0.0, NEG, ALU.is_equal, ALU.mult).then_inc(once, 1)
                    nc.vector.tensor_scalar(mask_q[:, body:SK], mask_raw[:, body:SK], 0.0, NEG, ALU.is_equal, ALU.mult
                                            ).then_inc(once, 1)
                    dve.wait_ge(pe_misc, 1)
                    nc.vector.tensor_copy(mask_k[:, 0:10, :].rearrange("k c q -> k (c q)"), misc[:, :].bitcast(BF16)[:, 0:10 * S])
                    side = prep_ps[0][:, :].bitcast(BF16)
                    nc.vector.tensor_copy(mask_k[:, 10, :], side[:, 0:S])
                    nc.vector.tensor_copy(mask_k[0:LASTK, 11, :], side[0:LASTK, S:2 * S]).then_inc(dve_misc, 1)
                else:
                    nc.vector.tensor_scalar(bo[:, :], bo[:, :], tanh_g, None, ALU.mult).then_inc(once, 1)
                dve.wait_ge(once, ONCE)
                nc.vector.sem_inc(o_out, 1)

                chain = Chain(dve, dve_chain, LINKS)
                tail = Chain(dve, tail_chain, 4)

                def normalize(b):
                    norm_stats(tail, nc, sh.x[:, bass.ds(b, 1), :], ln, LN_EPS, var_ready)
                    dve.wait_ge(rstd_ready, b + 1)
                    tail.link(nc.vector.tensor_scalar(xn[:, :], sh.x[:, b, :], ln.mv[:, 0, 0:1], ln.rstd[:, 0:1],
                                                      ALU.subtract, ALU.mult))
                    nc.vector.sem_inc(dve_ready, 1)

                def q_steps(b, u, pe_turn):
                    dve.wait_ge(pe_misc, pe_turn + 1)
                    nc.vector.tensor_copy(xnT[:, :], misc[:, 0:S]).then_inc(dve_misc, 1)
                    dve.wait_ge(pe_misc, pe_turn + 2)
                    nc.vector.tensor_tensor(q_bd[u][:, :, :], misc[:, 0:S].unsqueeze(1).to_broadcast([P, XH, S]),
                                            sh.head16[:, :].unsqueeze(2).to_broadcast([P, XH, S]), ALU.mult
                                            ).then_inc(dve_misc, 1)

                def batch(b, u, last):
                    chain.begin(b)
                    turn = first + b * MISC
                    for i in range(PIECES):
                        h, j = i // len(COLS), i % len(COLS)
                        dve.wait_ge(piece_mm, b * PIECES + i + 1)
                        nc.vector.tensor_reduce(max_parts[:, h, j:j + 1], ring[0:S, i % 4, 0:COLS[j][1]], AX_X, ALU.max
                                                ).then_inc(max_done, 1)
                    dve.wait_ge(max_done, (b + 1) * PIECES)
                    chain.link(nc.vector.tensor_reduce(neg_max[:, :], max_parts[:, :, :], AX_X, ALU.max))
                    chain.link(nc.vector.tensor_scalar(neg_max[:, :], neg_max[:, :], NEG / 2, -1.0, ALU.max, ALU.mult))
                    chain.link(nc.vector.tensor_copy(parts[:, 0, :], neg_max[:, :]))
                    chain.link(nc.vector.tensor_tensor(rest[:, 0, :], neg_max[:, :], parts[:, 0, :], ALU.subtract))
                    chain.link(nc.vector.tensor_copy(parts[:, 1, :], rest[:, 0, :]))
                    chain.link(nc.vector.tensor_tensor(rest[:, 1, :], rest[:, 0, :], parts[:, 1, :], ALU.subtract))
                    chain.link(nc.vector.tensor_copy(parts[:, 2, :], rest[:, 1, :]))
                    nc.vector.sem_inc(dve_ready, 1)
                    dve.wait_ge(pe_misc, turn + 1)
                    nc.vector.tensor_tensor(max_bd[:, :, :],
                                            misc[0:PARTS, 0:S // 2].bitcast(BF16).unsqueeze(1).to_broadcast([PARTS, XH, S]),
                                            sh.part_head[:, :].unsqueeze(2).to_broadcast([PARTS, XH, S]), ALU.mult
                                            ).then_inc(dve_misc, 1)
                    turn += 1
                    if not last:
                        tail.begin(b + 1)
                        normalize(b + 1)
                        q_steps(b + 1, 1 - u, turn)
                        turn += 2
                    dve.wait_ge(pv_mm, (b + 1) * HALVES + 3)
                    nc.vector.tensor_copy(oT[:, :], o_ps[:, 0:4 * S]).then_inc(o_out, 1)
                    dve.wait_ge(pe_misc, turn + 1)
                    m = misc[0:S, :].rearrange("q (a t j d) -> q a t j d", a=2, t=2, j=4)
                    r = rden[:, :].rearrange("q (a j t) -> q a t j", a=2, t=2)
                    o = o_n[:, :].rearrange("q (a j t d) -> q a t j d", a=2, t=2, d=XD)
                    for t in range(2):
                        den = m[:, :, t, :, t * (XD + 1) + XD]
                        chain.link(nc.vector.tensor_scalar(r[:, :, t, :], den, 1e-9, None, ALU.max))
                    chain.link(nc.vector.reciprocal(rden[:, :], rden[:, :]))
                    for t in range(2):
                        ins = nc.vector.tensor_tensor(o[:, :, t, :, :], m[:, :, t, :, t * (XD + 1):t * (XD + 1) + XD],
                                                      r[:, :, t, :].unsqueeze(3).to_broadcast([S, 2, 4, XD]), ALU.mult)
                    ins.then_inc(dve_misc, 1)
                    dve.wait_ge(pe_misc, turn + 2)
                    nc.vector.tensor_copy(o_nT[:, :], misc[:, 0:S]).then_inc(dve_misc, 1)
                    dve.wait_ge(pe_misc, turn + 3)
                    ins = nc.vector.scalar_tensor_tensor(sh.x[:, b, :], misc[0:S, 0:D], tanh_g, sh.x[:, b, :],
                                                         ALU.mult, ALU.add)
                    if not masked:
                        chain.link(ins)
                        ins = nc.vector.tensor_tensor(sh.x[:, b, :], sh.x[:, b, :], bo[:, :], ALU.add)
                    ins.then_inc(dve_misc, 1)
                    chain.end()

                first = 3 if masked else 2
                tail.begin(0)
                normalize(0)
                q_steps(0, 0, first - 2)
                batches(dve, batch)
    return


GB = 4
GT = GB * S
GROUPS = B // GB
UH = 4


class SmallAttention:

    def __init__(self, nc, c, ctx, name, heads, sh, mask=None):
        self.nc, self.heads, self.size, self.sh, self.mask = nc, heads, D // heads, sh, mask
        self.head_mask = sh.head16 if heads == 16 else sh.head8
        self.scale = float(self.size) ** -0.5
        self.per = heads // UH
        self.units = GB * self.per

        def sb(n, shape, dt=F32):
            return c.enter_context(nc.sbuf_tensor(f"{name}_{n}", shape, dt))

        def ps(n):
            return c.enter_context(nc.psum_tensor(f"{name}_{n}", [P, 512], F32))

        def sem(n):
            return ctx.enter_context(nc.semaphore(f"{name}_{n}"))

        self.qT = sb("qT", [D, GT])
        self.k_bd = sb("k_bd", [D, GB, heads, S])
        self.v = sb("v", [S, GB, heads, self.size + 1])
        self.top = [sb(f"top{r}", [S, UH]) for r in range(2)]
        self.diff = [sb(f"diff{r}", [S, UH, S]) for r in range(2)]
        self.probs = [sb(f"probs{r}", [S, UH, S]) for r in range(2)]
        self.probsT = [sb(f"probsT{r}", [S, UH, S]) for r in range(2)]
        self.rden = [sb(f"rden{r}", [S, heads]) for r in range(2)]
        self.o = sb("o", [S, GB, D])
        self.s_ps = [ps(f"s_ps{r}") for r in range(2)]
        self.t_ps = [ps(f"t_ps{r}") for r in range(2)]
        self.o_ps = [ps(f"o_ps{r}") for r in range(2)]
        self.s_mm = sem("s_mm")
        self.top_done = sem("top_done")
        self.s_out = sem("s_out")
        self.exp_done = sem("exp_done")
        self.t_mm = sem("t_mm")
        self.t_out = sem("t_out")
        self.v_mm = sem("v_mm")
        self.r_done = sem("r_done")
        self.o_out = sem("o_out")

    def prime(self, pe=None, act=None, dve=None):
        for eng, sems in ((pe, (self.t_mm, self.v_mm)), (act, (self.exp_done, self.t_out)), (dve, (self.s_out, self.o_out))):
            for s in sems if eng is not None else ():
                eng.sem_inc(s, 1)

    def tensor(self, pe, turn):
        nc, n = self.nc, self.units
        for i in range(n + 2):
            if i < n:
                b, h0 = i // self.per, UH * (i % self.per)
                pe.wait_ge(self.s_out, 1 + turn * n + max(i - 1, 0))
                bank = self.s_ps[i % 2][0:S, 0:UH * S]
                mm = nc.tensor.matmul(bank, self.qT[:, b * S:b * S + S],
                                      self.k_bd[:, b, h0:h0 + UH, :].rearrange("d h k -> d (h k)"),
                                      start=True, stop=self.mask is None)
                if self.mask is not None:
                    mm = nc.tensor.matmul(bank.rearrange("q (h k) -> q h k", h=UH), self.sh.ident_bf[0:S, 0:S],
                                          self.mask[:, :].unsqueeze(1).to_broadcast([S, UH, S]), start=False, stop=True)
                mm.then_inc(self.s_mm, 1)
            if 1 <= i <= n:
                j = i - 1
                pe.wait_ge(self.exp_done, 1 + turn * n + j + 1)
                pe.wait_ge(self.t_out, 1 + turn * n + max(j - 1, 0))
                for h in range(UH):
                    mm = nc.tensor.transpose(self.t_ps[j % 2][0:S, h * S:h * S + S], self.probs[j % 2][:, h, :],
                                             self.sh.ident[0:S, 0:S])
                mm.then_inc(self.t_mm, 1)
            if i >= 2:
                j = i - 2
                b, h0 = j // self.per, UH * (j % self.per)
                if h0 == 0:
                    pe.wait_ge(self.o_out, 1 + turn * GB + max(b - 1, 0))
                pe.wait_ge(self.t_out, 1 + turn * n + j + 1)
                w = self.size + 1
                for h in range(UH):
                    mm = nc.tensor.matmul(self.o_ps[b % 2][0:S, (h0 + h) * w:(h0 + h) * w + w],
                                          self.probsT[j % 2][:, h, :], self.v[:, b, h0 + h, :], start=True, stop=True)
                mm.then_inc(self.v_mm, 1)

    def scalar(self, act, turn):
        nc, n = self.nc, self.units
        for i in range(n + 1):
            if i < n:
                act.wait_ge(self.s_out, 1 + turn * n + i + 1)
                act.wait_ge(self.t_mm, 1 + turn * n + max(i - 1, 0))
                nc.scalar.activation(self.probs[i % 2][:, :, :], self.diff[i % 2][:, :, :], ACT.Exp, scale=self.scale
                                     ).then_inc(self.exp_done, 1)
            if i >= 1:
                j = i - 1
                act.wait_ge(self.t_mm, 1 + turn * n + j + 1)
                act.wait_ge(self.v_mm, 1 + turn * n + max(j - 1, 0))
                nc.scalar.copy(self.probsT[j % 2][:, :, :].rearrange("k h q -> k (h q)"), self.t_ps[j % 2][0:S, 0:UH * S]
                               ).then_inc(self.t_out, 1)

    def vector(self, dve, turn):
        nc, n = self.nc, self.units

        def divide(b):
            w = self.size + 1
            dve.wait_ge(self.v_mm, 1 + turn * n + (b + 1) * self.per)
            o = self.o_ps[b % 2][0:S, 0:self.heads * w].rearrange("q (h d) -> q h d", d=w)
            nc.vector.reciprocal(self.rden[b % 2][:, :], o[:, :, self.size]).then_inc(self.r_done, 1)
            dve.wait_ge(self.r_done, turn * GB + b + 1)
            nc.vector.tensor_tensor(self.o[:, b, :].rearrange("q (h d) -> q h d", h=self.heads), o[:, :, 0:self.size],
                                    self.rden[b % 2][:, :].unsqueeze(2).to_broadcast([S, self.heads, self.size]), ALU.mult
                                    ).then_inc(self.o_out, 1)

        for i in range(n + 2):
            if i < n:
                dve.wait_ge(self.s_mm, turn * n + i + 1)
                scores = self.s_ps[i % 2][0:S, 0:UH * S].rearrange("q (h k) -> q h k", h=UH)
                nc.vector.tensor_reduce(self.top[i % 2][:, :], scores, AX_X, ALU.max).then_inc(self.top_done, 1)
                dve.wait_ge(self.top_done, turn * n + i + 1)
                dve.wait_ge(self.exp_done, 1 + turn * n + max(i - 1, 0))
                nc.vector.tensor_tensor(self.diff[i % 2][:, :, :], scores,
                                        self.top[i % 2][:, :].unsqueeze(2).to_broadcast([S, UH, S]), ALU.subtract
                                        ).then_inc(self.s_out, 1)
            if i >= self.per + 1 and (i - 1) % self.per == 0:
                divide((i - 1) // self.per - 1)


def ffn0_edges():
    nodes, first = [], 0
    for c in range(6):
        n = min(c + 1, 5)
        source = c - n
        nodes.append(((c - 1, source, source + n // 2), (first + n - 1, first, first + n // 2)))
        first += n
    return nodes


def cell_ffn(nc, ctx, sh, A):
    NODES = ffn0_edges()
    NN = len(NODES)
    tanh_g = sh.tanh_g[0:S, 2:3]
    JN = 4 * NN + 1
    c = ExitStack()
    with c:
        def sb(name, shape, dt=F32):
            return c.enter_context(nc.sbuf_tensor(f"cell_{name}", shape, dt))

        def sem(name):
            return ctx.enter_context(nc.semaphore(f"cell_{name}"))

        we = sb("we", [D, 20, D])
        w = {n: sb(n, [D, NN, D]) for n in ("Wq", "Wk", "Wv", "Wo")}
        ew = sb("ew", [P, NN * 3])
        act_w = sb("act_w", [P, NN])
        be = sb("be", [P, NN * 3])
        gain, shift = sb("gain", [S, D]), sb("shift", [S, D])
        z = sb("z", [S, GB, D])
        nodes = [sb(f"node{n}", [D, GT]) for n in range(NN + 1)]
        qinT, kinT, vinT = sb("qinT", [D, GT]), sb("kinT", [D, GT]), sb("vinT", [D, GT])
        oT = sb("oT", [D, GT])
        ln = LayerNorm(c, nc, "cell_ln", S, sh.minus_half, GB)
        J = [c.enter_context(nc.psum_tensor(f"cell_J{r}", [P, 512], F32)) for r in range(2)]
        att = SmallAttention(nc, c, ctx, "cell_att", 8, sh)

        loaded = sem("loaded")
        j_mm = sem("j_mm")
        j_act, j_dve = sem("j_act"), sem("j_dve")
        var_ready, rstd_ready = sem("var_ready"), sem("rstd_ready")
        z_ready = sem("z_ready")
        chain_sem = sem("chain")
        LOADS = 16 * (5 + 2 + 18 + 2)

        with nc.Block() as block:
            @block.sync
            def _(sp):
                sp.dma_start(we[:, :, :], A["L0_ffn_We"].rearrange("e i o -> i e o")).then_inc(loaded, 16)
                for n in w:
                    sp.dma_start(w[n][:, :, :], A["L0_ffn_" + n].rearrange("c i o -> i c o")).then_inc(loaded, 16)
                sp.dma_start(ew[:, :], A["L0_ffn_ew"].rearrange("c k -> (c k)").partition_broadcast(P)).then_inc(loaded, 16)
                sp.dma_start(act_w[:, :], A["L0_ffn_act_w"].partition_broadcast(P)).then_inc(loaded, 16)
                for n, (_, edges) in enumerate(NODES):
                    for k, e in enumerate(edges):
                        sp.dma_start(be[:, 3 * n + k:3 * n + k + 1], A["L0_ffn_be"][e, :].unsqueeze(1)).then_inc(loaded, 16)
                sp.dma_start(gain[:, :], A["L0_ffn_ln_g"].partition_broadcast(S)).then_inc(loaded, 16)
                sp.dma_start(shift[:, :], A["L0_ffn_ln_b"].partition_broadcast(S)).then_inc(loaded, 16)

            @block.gpsimd
            def _(pool):
                with pool.Fori(0, GROUPS * 2) as i:
                    pool.wait_ge(var_ready, i + 1)
                    ln.inverse_root(nc).then_inc(rstd_ready, 1)

            @block.tensor
            def _(pe):
                pe.wait_ge(loaded, LOADS)
                att.prime(pe=pe)
                with pe.Fori(0, GROUPS) as g:
                    pe.wait_ge(z_ready, g + 1)
                    pe.wait_ge(j_act, 1 + g * JN)
                    for b in range(GB):
                        mm = nc.tensor.transpose(J[0][:, b * S:b * S + S], z[:, b, :], sh.ident[0:S, 0:S])
                    mm.then_inc(j_mm, 1)
                    for n, ((sq, sk, sv), (eq, ek, ev)) in enumerate(NODES):
                        a0, d0 = g * JN + 1 + 4 * n, g * JN + 4 * n
                        bank = [J[r][:, 0:GT] for r in range(2)]

                        def product(r, lhsT, rhs):
                            nc.tensor.matmul(bank[r], lhsT, rhs, start=True, stop=True).then_inc(j_mm, 1)
                        pe.wait_ge(j_dve, 1 + d0)
                        pe.wait_ge(j_act, 1 + a0)
                        product(1, we[:, ek, :], nodes[sk + 1][:, :])
                        product(0, we[:, eq, :], nodes[sq + 1][:, :])
                        pe.wait_ge(j_act, 1 + a0 + 1)
                        product(0, we[:, ev, :], nodes[sv + 1][:, :])
                        pe.wait_ge(j_dve, 1 + d0 + 1)
                        product(1, w["Wk"][:, n, :], kinT[:, :])
                        pe.wait_ge(j_act, 1 + a0 + 2)
                        product(0, w["Wq"][:, n, :], qinT[:, :])
                        pe.wait_ge(j_dve, 1 + d0 + 2)
                        for b in range(GB):
                            mm = nc.tensor.matmul(J[1][0:S, b * D:b * D + D], vinT[:, b * S:b * S + S], w["Wv"][:, n, :],
                                                  start=True, stop=True)
                        mm.then_inc(j_mm, 1)
                        pe.wait_ge(j_act, 1 + a0 + 3)
                        pe.wait_ge(j_dve, 1 + d0 + 3)
                        att.tensor(pe, g * NN + n)
                        pe.wait_ge(att.o_out, 1 + (g * NN + n) * GB + GB)
                        for b in range(GB):
                            mm = nc.tensor.transpose(J[0][:, b * S:b * S + S], att.o[:, b, :], sh.ident[0:S, 0:S])
                        mm.then_inc(j_mm, 1)
                        pe.wait_ge(j_act, 1 + a0 + 4)
                        product(1, w["Wo"][:, n, :], oT[:, :])
                    pe.wait_ge(j_dve, 1 + g * JN + 4 * NN)
                    for b in range(GB):
                        mm = nc.tensor.transpose(J[1][0:S, b * D:b * D + D], nodes[NN][:, b * S:b * S + S], sh.ident[:, :])
                    mm.then_inc(j_mm, 1)

            @block.scalar
            def _(act):
                act.wait_ge(chain_sem, 1)
                att.prime(act=act)
                act.sem_inc(j_act, 1)
                with act.Fori(0, GROUPS) as g:
                    m0 = g * 2 * JN
                    act.wait_ge(j_mm, m0 + 1)
                    nc.scalar.copy(nodes[0][:, :], J[0][:, 0:GT]).then_inc(j_act, 1)
                    for n in range(NN):
                        m = m0 + 1 + 8 * n
                        for k, (at, dst) in enumerate(((2, qinT), (3, vinT))):
                            act.wait_ge(j_mm, m + at)
                            nc.scalar.activation(dst[:, :], J[0][:, 0:GT], ACT.Identity,
                                                 bias=be[:, 3 * n + 2 * k:3 * n + 2 * k + 1],
                                                 scale=ew[:, 3 * n + 2 * k:3 * n + 2 * k + 1]).then_inc(j_act, 1)
                        act.wait_ge(j_mm, m + 5)
                        nc.scalar.copy(att.qT[:, :], J[0][:, 0:GT]).then_inc(j_act, 1)
                        att.scalar(act, g * NN + n)
                        act.wait_ge(j_mm, m + 7)
                        nc.scalar.copy(oT[:, :], J[0][:, 0:GT]).then_inc(j_act, 1)

            @block.vector
            def _(dve):
                dve.wait_ge(loaded, LOADS)
                nc.vector.tensor_tensor(be[:, :], be[:, :], ew[:, :], ALU.mult).then_inc(chain_sem, 1)
                nc.vector.tensor_scalar(gain[:, :], gain[:, :], tanh_g, None, ALU.mult).then_inc(chain_sem, 1)
                nc.vector.tensor_scalar(shift[:, :], shift[:, :], tanh_g, None, ALU.mult).then_inc(chain_sem, 1)
                nc.vector.memset(att.v[:, :, :, :], 1.0).then_inc(chain_sem, 1)
                dve.wait_ge(chain_sem, 4)
                chain = Chain(dve, chain_sem, 5 * GB + 5, 4)
                att.prime(dve=dve)
                dve.sem_inc(j_dve, 1)
                with dve.Fori(0, GROUPS) as g:
                    chain.begin(g)
                    x = sh.x[:, bass.ds(g * GB, GB), :]
                    norm_stats(chain, nc, x, ln, LN_EPS, var_ready)
                    dve.wait_ge(rstd_ready, g * 2 + 1)
                    for b in range(GB):
                        ins = nc.vector.tensor_scalar(z[:, b, :], sh.x[:, g * GB + b, :], ln.mv[:, b, 0:1],
                                                      ln.rstd[:, b:b + 1], ALU.subtract, ALU.mult)
                    ins.then_inc(z_ready, 1)
                    for n in range(NN):
                        m = g * 2 * JN + 1 + 8 * n
                        dve.wait_ge(j_mm, m + 1)
                        nc.vector.tensor_scalar(kinT[:, :], J[1][:, 0:GT], ew[:, 3 * n + 1:3 * n + 2],
                                                be[:, 3 * n + 1:3 * n + 2], ALU.mult, ALU.add).then_inc(j_dve, 1)
                        dve.wait_ge(j_mm, m + 4)
                        for b in range(GB):
                            ins = nc.vector.tensor_tensor(att.k_bd[:, b, :, :],
                                                          J[1][:, b * S:b * S + S].unsqueeze(1).to_broadcast([D, 8, S]),
                                                          sh.head8[:, :].unsqueeze(2).to_broadcast([D, 8, S]), ALU.mult)
                        ins.then_inc(j_dve, 1)
                        dve.wait_ge(j_mm, m + 6)
                        nc.vector.tensor_copy(att.v[:, :, :, 0:att.size].rearrange("k b h d -> k (b h) d"),
                                              J[1][0:S, :].rearrange("k (c d) -> k c d", d=att.size)).then_inc(j_dve, 1)
                        att.vector(dve, g * NN + n)
                        dve.wait_ge(j_mm, m + 8)
                        nc.vector.scalar_tensor_tensor(nodes[n + 1][:, :], J[1][:, 0:GT], act_w[:, n:n + 1], qinT[:, :],
                                                       ALU.mult, ALU.add).then_inc(j_dve, 1)
                    dve.wait_ge(j_mm, (g + 1) * 2 * JN)
                    last = J[1][0:S, :].rearrange("q (b d) -> q b d", b=GB)
                    norm_stats(chain, nc, last, ln, L0_LN_EPS, var_ready)
                    dve.wait_ge(rstd_ready, g * 2 + 2)
                    for b in range(GB):
                        chain.count(nc.vector.tensor_scalar(z[:, b, :], last[:, b, :], ln.mv[:, b, 0:1], ln.rstd[:, b:b + 1],
                                                            ALU.subtract, ALU.mult))
                    chain.wait()
                    nc.vector.sem_inc(j_dve, 1)
                    chain.link(nc.vector.tensor_tensor(z[:, :, :], z[:, :, :], gain[:, :].unsqueeze(1).to_broadcast([S, GB, D]), ALU.mult))
                    chain.link(nc.vector.tensor_tensor(z[:, :, :], z[:, :, :], shift[:, :].unsqueeze(1).to_broadcast([S, GB, D]), ALU.add))
                    chain.link(nc.vector.tensor_tensor(x, x, z[:, :, :], ALU.add))
                    chain.end()


def moe_ffn(nc, ctx, sh, A):
    E, F, TOP = 8, 512, 2
    FT = F // P
    UNITS = E * FT
    tanh_g = sh.tanh_g[0:S, 3:4]
    J_ACT, J_DVE = 5, 5
    CAUSAL = -float(2 ** 100)
    c = ExitStack()
    with c:
        def sb(name, shape, dt=F32):
            return c.enter_context(nc.sbuf_tensor(f"moe_{name}", shape, dt))

        def sem(name):
            return ctx.enter_context(nc.semaphore(f"moe_{name}"))

        wqkv, wo, w_gate = sb("wqkv", [D, 3, D]), sb("wo", [D, D]), sb("w_gate", [D, E])
        w1, w2 = sb("w1", [D, E, F]), sb("w2", [P, E, FT, D])
        b1_rows = sb("b1_rows", [UNITS, P])
        b1, b2 = sb("b1", [P, E, FT]), sb("b2", [E, D])
        norms = {n: sb(n, [S, D]) for n in ("ln1_g", "ln1_b", "ln2_g", "ln2_b")}
        causal = sb("causal", [S, S], BF16)
        before = sb("before", [S, E, E])
        x_in, h = sb("x_in", [S, GB, D]), sb("h", [S, GB, D])
        hT, oT, xfT = sb("hT", [D, GT]), sb("oT", [D, GT]), sb("xfT", [D, GT])
        ln = LayerNorm(c, nc, "moe_ln", S, sh.minus_half, GB)
        p = {n: sb(n, [S, GB, E]) for n in ("shifted", "exps", "prob", "rank", "kept", "gate")}
        one = {n: sb(n, [S, GB]) for n in ("best", "total", "norm", "kept_sum")}
        above, same = sb("above", [S, GB, E, E]), sb("same", [S, GB, E, E])
        gateT = sb("gateT", [E, GT])
        act_h = [sb(f"act_h{r}", [P, GT]) for r in range(2 * FT)]
        J = [c.enter_context(nc.psum_tensor(f"moe_J{r}", [P, 512], F32)) for r in range(2)]
        att = SmallAttention(nc, c, ctx, "moe_att", 16, sh, causal)
        h_ps, y_ps = att.s_ps, att.t_ps

        loaded, made = sem("loaded"), sem("made")
        j_mm = sem("j_mm")
        j_act, j_dve = sem("j_act"), sem("j_dve")
        var_ready, rstd_ready = sem("var_ready"), sem("rstd_ready")
        tokens = sem("tokens")
        shifted_ready, exps_ready = sem("shifted_ready"), sem("exps_ready")
        gate_ready = sem("gate_ready")
        h_mm, h_act = sem("h_mm"), sem("h_act")
        y_mm, y_out = sem("y_mm"), sem("y_out")
        b1_ready = sem("b1_ready")
        chain_sem = sem("chain")
        LOADS = 16 * 11

        with nc.Block() as block:
            @block.sync
            def _(sp):
                for dst, src in (
                    (wqkv[:, :, :], A["L1_ffn_w_qkv"].rearrange("i (k o) -> i k o", k=3)), (wo[:, :], A["L1_ffn_w_o"]),
                    (w_gate[:, :], A["L1_ffn_w_gate"]), (w1[:, :, :], A["L1_ffn_w1"].rearrange("e d f -> d e f")),
                    (w2[:, :, :, :], A["L1_ffn_w2"].rearrange("e (t p) d -> p e t d", p=P)),
                    (b1_rows[:, :], A["L1_ffn_b1"].rearrange("e (t p) -> (e t) p", p=P)), (b2[:, :], A["L1_ffn_b2"]),
                ) + tuple((norms[n][:, :], A["L1_ffn_" + n].partition_broadcast(S)) for n in norms):
                    sp.dma_start(dst, src).then_inc(loaded, 16)

            @block.gpsimd
            def _(pool):
                pool.memset(causal[:, :], 0.0).then_inc(made, 1)
                pool.memset(before[:, :, :], 0.0).then_inc(made, 1)
                pool.wait_ge(made, 2)
                pool.affine_select(out=causal[:, :], in_=causal[:, :], compare_op=ALU.is_ge, fill=CAUSAL, base=0,
                                   pattern=[[-1, S]], channel_multiplier=1).then_inc(made, 1)
                pool.affine_select(out=before[:, :, :], in_=before[:, :, :], compare_op=ALU.is_ge, fill=1.0, base=0,
                                   pattern=[[-1, E], [1, E]], channel_multiplier=0).then_inc(made, 1)
                with pool.Fori(0, GROUPS * 3) as i:
                    pool.wait_ge(var_ready, i + 1)
                    ln.inverse_root(nc).then_inc(rstd_ready, 1)

            @block.tensor
            def _(pe):
                pe.wait_ge(loaded, LOADS)
                pe.wait_ge(made, 4)
                bank = [J[r][:, 0:GT] for r in range(2)]
                nc.tensor.transpose(J[0][:, 0:UNITS], b1_rows[:, :], sh.ident[0:UNITS, 0:UNITS]).then_inc(b1_ready, 1)
                pe.wait_ge(b1_ready, 2)

                def turn_tokens(src, r):
                    for b in range(GB):
                        mm = nc.tensor.transpose(J[r][:, b * S:b * S + S], src[:, b, :], sh.ident[0:S, 0:S])
                    mm.then_inc(j_mm, 1)

                def per_batch(r, lhsT, rhs, n):
                    for b in range(GB):
                        mm = nc.tensor.matmul(J[r][0:S, b * n:b * n + n], lhsT[:, b * S:b * S + S], rhs, start=True, stop=True)
                    mm.then_inc(j_mm, 1)

                att.prime(pe=pe)
                with pe.Fori(0, GROUPS) as g:
                    a0, d0 = g * J_ACT, g * J_DVE
                    pe.wait_ge(tokens, g * 2 + 1)
                    pe.wait_ge(j_act, 1 + a0)
                    turn_tokens(h, 0)
                    pe.wait_ge(j_act, 1 + a0 + 1)
                    pe.wait_ge(j_dve, 1 + d0)
                    nc.tensor.matmul(bank[1], wqkv[:, 1, :], hT[:, :], start=True, stop=True).then_inc(j_mm, 1)
                    nc.tensor.matmul(bank[0], wqkv[:, 0, :], hT[:, :], start=True, stop=True).then_inc(j_mm, 1)
                    pe.wait_ge(j_dve, 1 + d0 + 1)
                    per_batch(1, hT, wqkv[:, 2, :], D)
                    pe.wait_ge(j_act, 1 + a0 + 2)
                    pe.wait_ge(j_dve, 1 + d0 + 2)
                    pe.wait_ge(y_out, 1 + g * E)
                    att.tensor(pe, g)
                    pe.wait_ge(att.o_out, 1 + g * GB + GB)
                    turn_tokens(att.o, 0)
                    pe.wait_ge(j_act, 1 + a0 + 3)
                    per_batch(1, oT, wo[:, :], D)
                    pe.wait_ge(tokens, g * 2 + 2)
                    turn_tokens(h, 0)
                    pe.wait_ge(j_act, 1 + a0 + 4)
                    per_batch(1, xfT, w_gate[:, :], E)

                    def inner(i):
                        e, t = i // FT, i % FT
                        pe.wait_ge(h_act, 1 + g * UNITS + max(i - 1, 0))
                        nc.tensor.matmul(h_ps[i % 2][:, 0:GT], w1[:, e, t * P:t * P + P], xfT[:, :], start=True, stop=True
                                         ).then_inc(h_mm, 1)

                    def outer(e):
                        pe.wait_ge(y_out, 1 + g * E + max(e - 1, 0))
                        pe.wait_ge(h_act, 1 + g * UNITS + (e + 1) * FT)
                        for b in range(GB):
                            for t in range(FT):
                                mm = nc.tensor.matmul(y_ps[e % 2][0:S, b * D:b * D + D],
                                                      act_h[(e % 2) * FT + t][:, b * S:b * S + S], w2[:, e, t, :],
                                                      start=(t == 0), stop=(t == FT - 1))
                        mm.then_inc(y_mm, 1)

                    for i in range(FT):
                        inner(i)
                    for e in range(1, E):
                        for t in range(FT):
                            inner(e * FT + t)
                        if e == 1:
                            pe.wait_ge(gate_ready, g + 1)
                            for b in range(GB):
                                mm = nc.tensor.transpose(J[0][0:E, b * S:b * S + S], p["gate"][:, b, :], sh.ident[0:S, 0:S])
                            mm.then_inc(j_mm, 1)
                            pe.wait_ge(j_act, 1 + a0 + 5)
                            for b in range(GB):
                                mm = nc.tensor.matmul(J[1][0:S, b * D:b * D + D], gateT[:, b * S:b * S + S], b2[:, :],
                                                      start=True, stop=True)
                            mm.then_inc(j_mm, 1)
                        outer(e - 1)
                    outer(E - 1)

            @block.scalar
            def _(act):
                act.wait_ge(b1_ready, 1)
                nc.scalar.copy(b1[:, :, :].rearrange("p e t -> p (e t)"), J[0][:, 0:UNITS]).then_inc(b1_ready, 1)
                act.wait_ge(b1_ready, 2)
                att.prime(act=act)
                act.sem_inc(j_act, 1)
                act.sem_inc(h_act, 1)
                with act.Fori(0, GROUPS) as g:
                    def out_of_bank(at, dst):
                        act.wait_ge(j_mm, g * 10 + at)
                        nc.scalar.copy(dst, J[0][0:dst.shape[0], 0:GT]).then_inc(j_act, 1)
                    out_of_bank(1, hT[:, :])
                    out_of_bank(3, att.qT[:, :])
                    att.scalar(act, g)
                    out_of_bank(5, oT[:, :])
                    out_of_bank(7, xfT[:, :])
                    act.wait_ge(shifted_ready, g + 1)
                    nc.scalar.activation(p["exps"][:, :, :], p["shifted"][:, :, :], ACT.Exp).then_inc(exps_ready, 1)
                    for i in range(UNITS):
                        e, t = i // FT, i % FT
                        if i == 2 * FT:
                            out_of_bank(9, gateT[:, :])
                        act.wait_ge(h_mm, g * UNITS + i + 1)
                        if e >= 2:
                            act.wait_ge(y_mm, g * E + e - 1)
                        nc.scalar.activation(act_h[i % (2 * FT)][:, :], h_ps[i % 2][:, 0:GT], ACT.Gelu_apprx_tanh,
                                             bias=b1[:, e, t:t + 1]).then_inc(h_act, 1)

            @block.vector
            def _(dve):
                nc.vector.memset(att.v[:, :, :, :], 1.0).then_inc(chain_sem, 1)
                dve.wait_ge(chain_sem, 1)
                dve.wait_ge(loaded, LOADS)
                dve.wait_ge(made, 4)
                chain = Chain(dve, chain_sem, 3 * (3 * GB + 1) + 4 + 1 + 2 + 3 + 2 + GB + 6 + 1 + E * GB + 1, 1)

                def normalize(g, k, dst, x, gain=None, shift=None):
                    norm_stats(chain, nc, x, ln, LN_EPS, var_ready)
                    dve.wait_ge(rstd_ready, g * 3 + k + 1)
                    for b in range(GB):
                        chain.count(nc.vector.tensor_scalar(dst[:, b, :], x[:, b, :], ln.mv[:, b, 0:1], ln.rstd[:, b:b + 1],
                                                            ALU.subtract, ALU.mult))
                    chain.wait()
                    if gain is not None:
                        chain.link(nc.vector.tensor_tensor(dst, dst, gain[:, :].unsqueeze(1).to_broadcast([S, GB, D]), ALU.mult))
                        chain.link(nc.vector.tensor_tensor(dst, dst, shift[:, :].unsqueeze(1).to_broadcast([S, GB, D]), ALU.add))

                att.prime(dve=dve)
                dve.sem_inc(j_dve, 1)
                dve.sem_inc(y_out, 1)
                with dve.Fori(0, GROUPS) as g:
                    chain.begin(g)
                    x = sh.x[:, bass.ds(g * GB, GB), :]
                    xi, ht = x_in[:, :, :], h[:, :, :]
                    normalize(g, 0, xi, x)
                    normalize(g, 1, ht, xi, norms["ln1_g"], norms["ln1_b"])
                    nc.vector.sem_inc(tokens, 1)
                    dve.wait_ge(j_mm, g * 10 + 2)
                    for b in range(GB):
                        ins = nc.vector.tensor_tensor(att.k_bd[:, b, :, :],
                                                      J[1][:, b * S:b * S + S].unsqueeze(1).to_broadcast([D, 16, S]),
                                                      sh.head16[:, :].unsqueeze(2).to_broadcast([D, 16, S]), ALU.mult)
                    ins.then_inc(j_dve, 1)
                    dve.wait_ge(j_mm, g * 10 + 4)
                    nc.vector.tensor_copy(att.v[:, :, :, 0:att.size].rearrange("k b h d -> k (b h) d"),
                                          J[1][0:S, :].rearrange("k (c d) -> k c d", d=att.size)).then_inc(j_dve, 1)
                    att.vector(dve, g)
                    dve.wait_ge(j_mm, g * 10 + 6)
                    chain.link(nc.vector.tensor_tensor(xi, xi, J[1][0:S, :].rearrange("q (b d) -> q b d", b=GB), ALU.add))
                    nc.vector.sem_inc(j_dve, 1)
                    normalize(g, 2, ht, xi, norms["ln2_g"], norms["ln2_b"])
                    nc.vector.sem_inc(tokens, 1)

                    def wide(ap):
                        return ap.unsqueeze(2).to_broadcast([S, GB, E])
                    P_ = {n: t[:, :, :] for n, t in p.items()}
                    O_ = {n: t[:, :] for n, t in one.items()}
                    dve.wait_ge(j_mm, g * 10 + 8)
                    logits = J[1][0:S, 0:GB * E].rearrange("q (b e) -> q b e", b=GB)
                    chain.link(nc.vector.tensor_reduce(O_["best"], logits, AX_X, ALU.max))
                    chain.link(nc.vector.tensor_tensor(P_["shifted"], logits, wide(O_["best"]), ALU.subtract))
                    nc.vector.sem_inc(j_dve, 1)
                    nc.vector.sem_inc(shifted_ready, 1)
                    dve.wait_ge(exps_ready, g + 1)
                    chain.link(nc.vector.tensor_reduce(O_["total"], P_["exps"], AX_X, ALU.add))
                    chain.link(nc.vector.reciprocal(O_["norm"], O_["total"]))
                    chain.link(nc.vector.tensor_tensor(P_["prob"], P_["exps"], wide(O_["norm"]), ALU.mult))
                    other = P_["prob"].unsqueeze(2).to_broadcast([S, GB, E, E])
                    own = P_["prob"].unsqueeze(3).to_broadcast([S, GB, E, E])
                    chain.count(nc.vector.tensor_tensor(above[:, :, :, :], other, own, ALU.is_gt))
                    chain.link(nc.vector.tensor_tensor(same[:, :, :, :], other, own, ALU.is_equal))
                    for b in range(GB):
                        chain.count(nc.vector.tensor_tensor(same[:, b, :, :], same[:, b, :, :], before[:, :, :], ALU.mult))
                    chain.wait()
                    chain.link(nc.vector.tensor_tensor(above[:, :, :, :], above[:, :, :, :], same[:, :, :, :], ALU.add))
                    chain.link(nc.vector.tensor_reduce(P_["rank"], above[:, :, :, :], AX_X, ALU.add))
                    chain.link(nc.vector.scalar_tensor_tensor(P_["kept"], P_["rank"], TOP - 0.5, P_["prob"], ALU.is_lt, ALU.mult))
                    chain.link(nc.vector.tensor_reduce(O_["kept_sum"], P_["kept"], AX_X, ALU.add))
                    chain.link(nc.vector.reciprocal(O_["norm"], O_["kept_sum"]))
                    chain.link(nc.vector.tensor_tensor(P_["gate"], P_["kept"], wide(O_["norm"]), ALU.mult))
                    nc.vector.sem_inc(gate_ready, 1)
                    dve.wait_ge(j_mm, g * 10 + 10)
                    chain.link(nc.vector.tensor_tensor(xi, xi, J[1][0:S, :].rearrange("q (b d) -> q b d", b=GB), ALU.add))
                    nc.vector.sem_inc(j_dve, 1)
                    for e in range(E):
                        dve.wait_ge(y_mm, g * E + e + 1)
                        for b in range(GB):
                            chain.count(nc.vector.scalar_tensor_tensor(
                                x_in[:, b, :], y_ps[e % 2][0:S, b * D:b * D + D], p["gate"][:, b, e:e + 1], x_in[:, b, :],
                                ALU.mult, ALU.add))
                        chain.wait()
                        nc.vector.sem_inc(y_out, 1)
                    chain.link(nc.vector.scalar_tensor_tensor(x, xi, tanh_g, x, ALU.mult, ALU.add))
                    chain.end()


def build_program(nc, A, out, phases=(1, 2, 3, 4)):
    with ExitStack() as ctx:
        sh = setup(nc, ctx, A)
        if 1 in phases:
            cross_attention(nc, ctx, sh, A, 0)
        if 2 in phases:
            cell_ffn(nc, ctx, sh, A)
        if 3 in phases:
            cross_attention(nc, ctx, sh, A, 1)
        if 4 in phases:
            moe_ffn(nc, ctx, sh, A)
        stored = ctx.enter_context(nc.semaphore("stored"))
        with nc.Block() as block:
            @block.sync
            def _(sp):
                sp.dma_start(out.rearrange("b s d -> s b d"), sh.x[:, :, :]).then_inc(stored, 16)
                sp.wait_ge(stored, 16)


def kernel(**inputs):
    import numpy as _np
    import concourse.bacc as _bacc
    from concourse import mybir as _mybir
    from concourse.bass_utils import run_bass_kernel_spmd as _run

    nc = _bacc.Bacc("TRN2", target_bir_lowering=False, num_devices=1)
    arrays, A = {}, {}
    for name, value in inputs.items():
        a = _np.ascontiguousarray(value)
        arrays[f"in_{name}"] = a
        A[name] = nc.dram_tensor(f"in_{name}", a.shape, _mybir.dt.from_np(a.dtype), kind="ExternalInput").ap()
    out = nc.dram_tensor("out_x", (B, S, D), F32, kind="ExternalOutput").ap()
    build_program(nc, A, out)
    r = _run(nc, [arrays], core_ids=[0])
    return r.results[0]["out_x"]
```

```python
from contextlib import ExitStack

import concourse.bass as bass
from concourse import mybir

F32 = mybir.dt.float32
BF16 = mybir.dt.bfloat16
U8 = mybir.dt.uint8
ALU = mybir.AluOpType
ACT = mybir.ActivationFunctionType
AX_X = mybir.AxisListType.X

B, S, D = 32, 100, 128
SK = 1444
P = 128
XH, XD = 16, 8
CH = -(-SK // P)
LASTK = SK - (CH - 1) * P
COLS = [(0, 512), (512, 512), (1024, SK - 1024)]
NEG = -float(2 ** 30)
LN_EPS = 1e-5
L0_LN_EPS = 1e-6


def chunk_keys(c):
    return P if c < CH - 1 else LASTK


def col(ap, shape):
    for _ in range(len(shape) - 2):
        ap = ap.unsqueeze(1)
    return ap.to_broadcast(shape)


class Chain:

    def __init__(self, eng, sem, per, ahead=0):
        self.eng, self.sem, self.per, self.ahead, self.turn, self.k = eng, sem, per, ahead, 0, 0

    def begin(self, turn):
        self.turn, self.k = turn, 0

    def count(self, ins):
        self.k += 1
        ins.then_inc(self.sem, 1)

    def wait(self):
        self.eng.wait_ge(self.sem, self.turn * self.per + self.ahead + self.k)

    def link(self, ins):
        self.count(ins)
        self.wait()

    def end(self):
        assert self.k == self.per, (self.k, self.per)


class Shared:
    pass


class LayerNorm:

    def __init__(self, c, nc, name, rows, minus_half, n):
        def sb(what, shape):
            return c.enter_context(nc.sbuf_tensor(f"{name}_{what}", [rows] + shape, F32))

        self.n = n
        self.stats, self.mv, self.var, self.rstd = sb("stats", [n, 6]), sb("mv", [n, 2]), sb("var", [n]), sb("rstd", [n])
        self.held = sb("held", [1])
        self.minus_half = minus_half[0:rows, :].to_broadcast([rows, n])

    def inverse_root(self, nc):
        return nc.gpsimd.tensor_tensor(self.rstd[:, :], self.var[:, :], self.minus_half, ALU.pow)


def norm_stats(chain, nc, x, ln, eps, var_ready):
    for b in range(ln.n):
        chain.count(nc.vector.bn_stats(ln.stats[:, b, :], x[:, b, :]))
    chain.wait()
    chain.count(nc.vector.memset(ln.held[:, :], 0.0))
    for b in range(ln.n):
        chain.count(nc.vector.bn_aggr(ln.mv[:, b, :], ln.stats[:, b, :]))
    chain.wait()
    nc.vector.tensor_scalar(ln.var[:, :], ln.mv[:, :, 1], eps, None, ALU.add).then_inc(var_ready, 1)


def setup(nc, ctx, A):
    sh = Shared()

    def sb(name, shape, dt=F32):
        return ctx.enter_context(nc.sbuf_tensor(name, shape, dt))

    sh.x = sb("x_tokens", [S, B, D])
    sh.ident = sb("ident", [P, P])
    sh.ident_bf = sb("ident_bf", [P, P], BF16)
    sh.head16 = sb("head16", [P, 16])
    sh.head8 = sb("head8", [P, 8])
    sh.side = sb("side", [P, 2])
    sh.row_side = sb("row_side", [P, 2])
    sh.minus_half = sb("minus_half", [P, 1])
    sh.tanh_g = sb("tanh_g", [P, 4])
    sh.cross_w = sb("cross_w", [P, 8, P])
    with ExitStack() as c:
        raw = c.enter_context(nc.sbuf_tensor("raw_w", [P, 8, P], F32))
        alternate = c.enter_context(nc.sbuf_tensor("alternate", [P, 2, P // 2], F32))
        g = c.enter_context(nc.sbuf_tensor("g_raw", [P, 4], F32))
        ps = [c.enter_context(nc.psum_tensor(f"ps_w{i}", [P, 4, P], F32)) for i in range(2)]
        sem = {n: ctx.enter_context(nc.semaphore("setup_" + n)) for n in ("loaded", "x_loaded", "ident", "tp", "cp", "g")}
        names = ["L0_xattn_wq", "L0_xattn_wk", "L0_xattn_wv", "L0_xattn_wo", "L1_xattn_Wq", "L1_xattn_Wk", "L1_xattn_Wv", "L1_xattn_Wo"]
        with nc.Block() as block:
            @block.sync
            def _(sp):
                for n, name in enumerate(names):
                    sp.dma_start(raw[:, n, :], A[name]).then_inc(sem["loaded"], 16)
                sp.dma_start(sh.x[:, :, :], A["x"].rearrange("b s d -> s b d")).then_inc(sem["x_loaded"], 16)

            @block.gpsimd
            def _(pool):
                k = 0

                def link(ins):
                    nonlocal k
                    k += 1
                    ins.then_inc(sem["ident"], 1)
                    pool.wait_ge(sem["ident"], k)
                link(pool.memset(sh.ident[:, :], 0.0))
                link(pool.memset(sh.ident_bf[:, :], 0.0))
                link(pool.memset(sh.minus_half[:, :], -0.5))
                link(pool.memset(sh.head16[:, :], 1.0))
                link(pool.memset(sh.head8[:, :], 1.0))
                link(pool.memset(alternate[:, :, :], 0.0))
                for m in (sh.ident, sh.ident_bf):
                    link(pool.affine_select(out=m[:, :], in_=m[:, :], compare_op=ALU.not_equal, fill=1.0, base=0,
                                            pattern=[[-1, P]], channel_multiplier=1))
                link(pool.affine_select(out=alternate[:, :, :], in_=alternate[:, :, :], compare_op=ALU.not_equal,
                                        fill=1.0, base=0, pattern=[[-1, 2], [-2, P // 2]], channel_multiplier=1))
                for m, heads in ((sh.head16, 16), (sh.head8, 8)):
                    size = P // heads
                    link(pool.affine_select(out=m[:, :], in_=m[:, :], compare_op=ALU.is_ge, fill=0.0, base=0,
                                            pattern=[[-size, heads]], channel_multiplier=1))
                    link(pool.affine_select(out=m[:, :], in_=m[:, :], compare_op=ALU.is_ge, fill=0.0, base=size - 1,
                                            pattern=[[size, heads]], channel_multiplier=-1))

            @block.scalar
            def _(act):
                for n, name in enumerate(("g_xattn", "g_ffn")):
                    act.dma_start(g[:, 2 * n:2 * n + 2], A[name].partition_broadcast(P)).then_inc(sem["g"], 16)
                act.wait_ge(sem["g"], 32)
                nc.scalar.activation(sh.tanh_g[:, :], g[:, :], ACT.Tanh).then_inc(sem["g"], 1)
                for i in range(2):
                    act.wait_ge(sem["tp"], i + 1)
                    nc.scalar.copy(sh.cross_w[:, 4 * i:4 * i + 4, :], ps[i][:, :, :]).then_inc(sem["cp"], 1)

            @block.tensor
            def _(pe):
                pe.wait_ge(sem["loaded"], 128)
                pe.wait_ge(sem["ident"], 13)
                for i in range(2):
                    for j in range(4):
                        mm = nc.tensor.transpose(ps[i][:, j, :], raw[:, 4 * i + j, :], sh.ident[:, :])
                    mm.then_inc(sem["tp"], 1)

            @block.vector
            def _(dve):
                dve.wait_ge(sem["x_loaded"], 16)
                dve.wait_ge(sem["cp"], 2)
                dve.wait_ge(sem["g"], 33)
                dve.wait_ge(sem["ident"], 13)
                nc.vector.tensor_reduce(sh.side[:, :], sh.head16[:, :].rearrange("p (a t) -> p t a", t=2), AX_X, ALU.add
                                        ).then_inc(sem["g"], 1)
                nc.vector.tensor_reduce(sh.row_side[:, :], alternate[:, :, :], AX_X, ALU.add).then_inc(sem["g"], 1)
                dve.wait_ge(sem["g"], 35)
    return sh


PRODUCTS = ((0, 0), (0, 1), (1, 0), (0, 2), (2, 0), (1, 1))
PAIR = 2 * XD
PAIRS = XH // 2
SPLIT = len(PRODUCTS) * PAIR
FOLD = SPLIT + 6


def after(eng, sem, value):
    if not isinstance(value, int) or value > 0:
        eng.wait_ge(sem, value)


class Turn:

    def __init__(self, n, third, r):
        self.n, self.third, self.r = n, third, r

    def plus(self, d):
        return Turn(self.n + d, self.third + (self.r + d) // 3, (self.r + d) % 3)


def cross_attention(nc, ctx, sh, A, layer):
    SCALE = float(XD) ** -0.5
    masked = layer == 1
    wqT, wkT, wvT, woT = (sh.cross_w[:, 4 * layer + n, :] for n in range(4))
    tanh_g = sh.tanh_g[0:S, layer:layer + 1]
    MAXES = XH * len(COLS)
    SLOTS = 4 * CH
    MAX_SLOTS = 38 if not masked else 40
    PREP = 9
    MISC = 6
    BODY = (CH - 1) * P

    c = ExitStack()
    with c:
        def sb(name, shape, dt=F32):
            return c.enter_context(nc.sbuf_tensor(f"x{layer}_{name}", shape, dt))

        def dram(name, shape):
            return [nc.dram_tensor(f"x{layer}_{name}{r}", shape, BF16).ap() for r in range(3)]

        def sem(name):
            return ctx.enter_context(nc.semaphore(f"x{layer}_{name}"))

        ctx_raw = sb("ctx_raw", [P, CH, D])
        ctxT = sb("ctxT", [D, SK])
        k_parts = sb("k_parts", [D, 3, SK], BF16)
        k_rest = sb("k_rest", [D, SK])
        k_st = [sb(f"k_st{r}", [P, PAIRS, SK], BF16) for r in range(3)]
        v = [sb(f"v{r}", [P, CH, XH, XD + 1]) for r in range(3)]
        xn, xnT = sb("xn", [S, D]), sb("xnT", [D, S])
        q_parts, q_rest = sb("q_parts", [D, 3, S], BF16), sb("q_rest", [D, S])
        q_par = sb("q_par", [D, 3, 2, S], BF16)
        q_st = [sb(f"q_st{r}", [P, PAIRS, 2 * S], BF16) for r in range(3)]
        max_parts = sb("max_parts", [S, XH, len(COLS)])
        neg_max, rest = sb("neg_max", [S, XH]), sb("rest", [S, 2, XH])
        parts = sb("parts", [S, PAIRS, 3, 2], BF16)
        probs = [sb(f"probs{r}", [P, 4 * S]) for r in range(4)]
        oT = sb("oT", [P, 4 * S])
        rden, o_n, o_nT = sb("rden", [S, XH]), sb("o_n", [S, D]), sb("o_nT", [D, S])
        ln = LayerNorm(c, nc, f"x{layer}_ln", S, sh.minus_half, 1)
        bo = None if masked else sb("bo", [S, D])
        if masked:
            mask_raw = sb("mask_raw", [S, SK], U8)
            mask_q = sb("mask_q", [S, SK], BF16)
            mask_k = sb("mask_k", [P, CH, S], BF16)
        k_dram, q_dram = dram("k_dram", [D, 3, SK]), dram("q_dram", [D, 3, 2 * S])

        def bank(name):
            return c.enter_context(nc.psum_tensor(f"x{layer}_{name}", [P, 512], F32))

        max_ps = [bank(f"max_ps{r}") for r in range(2)]
        exp_ps = [bank(f"exp_ps{r}") for r in range(3)]
        o_ps, prep_ps, misc = bank("o_ps"), bank("prep_ps"), bank("misc")

        ctx_in = sem("ctx_in")
        prep_mm = sem("prep_mm")
        prep_out = sem("prep_out")
        rest_out = sem("rest_out")
        mid_out = sem("mid_out")
        low_out = sem("low_out")
        q_out = sem("q_out")
        max_placed = sem("max_placed")
        k_written = [sem(f"k_written{r}") for r in range(3)]
        q_written = [sem(f"q_written{r}") for r in range(3)]
        k_in = [sem(f"k_in{r}") for r in range(3)]
        q_in = [sem(f"q_in{r}") for r in range(3)]
        max_mm = sem("max_mm")
        max_out = sem("max_out")
        exp_mm = sem("exp_mm")
        exp_out = sem("exp_out")
        pv_mm = sem("pv_mm")
        o_out = sem("o_out")
        xn_out = sem("xn_out")
        parts_out = sem("parts_out")
        pe_misc = sem("pe_misc")
        dve_misc = sem("dve_misc")
        chain_sems = [sem(n) for n in ("norm_chain", "query_chain", "max_chain", "out_chain")]
        var_ready = sem("var_ready")
        rstd_ready = sem("rstd_ready")
        once, first_in = sem("once"), sem("first_in")
        ones_in = sem("ones_in")
        ONCE = 14 if masked else 13
        HEAD = 1 if masked else 0

        class Steps:

            def __init__(self, b):
                n = b.n
                known = isinstance(n, int)
                self.k = HEAD + 5 + n * MISC - (0 if known and n == 0 else 3)
                if known and n > B - 2:
                    self.k -= 2 * (n - (B - 2))
                if known and n > B - 1:
                    self.k -= (n - (B - 1))

            def next(self):
                self.k = self.k + 1
                return self.k - 1

        def turns(eng, body):
            body(Turn(0, 0, 0))
            with eng.Fori(0, (B - 5) // 3) as i:
                for t in range(3):
                    body(Turn(i * 3 + 1 + t, i + (1 + t) // 3, (1 + t) % 3))
            for n in range(B - 4, B):
                body(Turn(n, n // 3, n % 3))

        def there(b, n):
            return not isinstance(b.n, int) or b.n + n < B

        max_at = [[k for k in range(MAXES) if k * MAX_SLOTS // MAXES == s] for s in range(SLOTS)]

        with nc.Block() as block:
            @block.sync
            def _(sp):
                if masked:
                    sp.dma_start(mask_raw[:, :], A["mask_SxS2_bk0"]).then_inc(first_in, 16)
                else:
                    sp.dma_start(bo[:, :], A["L0_xattn_bo"].partition_broadcast(S)).then_inc(first_in, 16)

                def load_ctx(n):
                    sp.dma_start(ctx_raw[:, 0:CH - 1, :], A["ctx_1024"][n, 0:BODY, :].rearrange("(p c) d -> p c d", p=P)
                                 ).then_inc(ctx_in, 16)
                    sp.dma_start(ctx_raw[0:LASTK, CH - 1, :], A["ctx_1024"][n, BODY:SK, :]).then_inc(ctx_in, 16)

                def stack(b, source, through, written, dst, landed, part_of):
                    r = b.r
                    sp.dma_start(through[r], source).then_inc(written[r], 16)
                    sp.wait_ge(written[r], (b.third + 1) * 16)
                    for j, pr in enumerate(PRODUCTS):
                        sp.dma_start(dst[r][PAIR * j:PAIR * j + PAIR, :, :],
                                     through[r][:, pr[part_of], :].rearrange("(p r) n -> r p n", r=PAIR)
                                     ).then_inc(landed[r], 16)

                def stack_q(b):
                    sp.wait_ge(q_out, b.n + 1)
                    after(sp, exp_mm, (b.n - 2) * SLOTS)
                    stack(b, q_par[:, :, :, :].rearrange("d a t q -> d a (t q)"), q_dram, q_written, q_st, q_in, 0)

                def stack_k(b):
                    sp.wait_ge(low_out, (b.n + 1) * 3)
                    stack(b, k_parts[:, :, :], k_dram, k_written, k_st, k_in, 1)

                def turn(b):
                    if there(b, 3):
                        sp.wait_ge(prep_out, (b.n + 2) * PREP + 3)
                        load_ctx(b.n + 3)
                    if there(b, 2):
                        stack_q(b.plus(2))
                        stack_k(b.plus(2))

                load_ctx(0)
                sp.wait_ge(once, ONCE - 1)
                for r in range(1, 3):
                    sp.dma_start(k_st[r][SPLIT:FOLD, :, :], k_st[0][SPLIT:FOLD, :, :]).then_inc(ones_in, 16)
                for n in range(2):
                    sp.wait_ge(prep_out, n * PREP + 3)
                    load_ctx(n + 1)
                    stack_q(Turn(n, 0, n))
                    stack_k(Turn(n, 0, n))
                turns(sp, turn)

            @block.gpsimd
            def _(pool):
                def low(b):
                    for j, (c0, n) in enumerate(COLS):
                        pool.wait_ge(mid_out, b.n * 3 + j + 1)
                        nc.gpsimd.tensor_tensor(k_parts[:, 2, c0:c0 + n], k_rest[:, c0:c0 + n], k_parts[:, 1, c0:c0 + n],
                                                ALU.subtract).then_inc(low_out, 1)

                def root(b):
                    pool.wait_ge(var_ready, b.n + 1)
                    ln.inverse_root(nc).then_inc(rstd_ready, 1)

                def turn(b):
                    if there(b, 2):
                        low(b.plus(2))
                        root(b.plus(2))
                for n in range(2):
                    root(Turn(n, 0, n))
                    low(Turn(n, 0, n))
                turns(pool, turn)

            @block.tensor
            def _(pe):
                pe.sem_inc(pv_mm, 4)

                def prep(b, m):
                    j = m % 3
                    c0, n = COLS[j]
                    if m <= 3 or m >= 7:
                        after(pe, prep_out, b.n * PREP + m)
                    if 4 <= m <= 6:
                        pe.wait_ge(rest_out, b.n * 3 + m - 3)
                    if m == 0:
                        pe.wait_ge(ctx_in, (b.n + 1) * 32)
                    if m < 3:
                        for ch in range(4 * j, 4 * j + 4):
                            k = chunk_keys(ch)
                            mm = nc.tensor.transpose(prep_ps[:, (ch % 4) * P:(ch % 4) * P + k], ctx_raw[0:k, ch, :],
                                                     sh.ident[0:k, 0:k])
                    elif m < 6:
                        mm = nc.tensor.matmul(prep_ps[:, 0:n], wkT, ctxT[:, c0:c0 + n], start=True, stop=True)
                    else:
                        for ch in range(4 * j, 4 * j + 4):
                            k = chunk_keys(ch)
                            mm = nc.tensor.matmul(prep_ps[0:k, (ch % 4) * P:(ch % 4) * P + P],
                                                  ctxT[:, ch * P:ch * P + k], wvT, start=True, stop=True)
                    mm.then_inc(prep_mm, 1)

                def xn_transpose(b, step):
                    after(pe, dve_misc, step)
                    pe.wait_ge(xn_out, b.n + 1)
                    nc.tensor.transpose(misc[:, 0:S], xn[:, :], sh.ident[0:S, 0:S]).then_inc(pe_misc, 1)

                def q_product(b, step):
                    pe.wait_ge(dve_misc, step)
                    nc.tensor.matmul(misc[:, 0:S], wqT, xnT[:, :], start=True, stop=True).then_inc(pe_misc, 1)

                def max_piece(b, i):
                    h, j = i // len(COLS), i % len(COLS)
                    c0, n = COLS[j]
                    if i == 0:
                        pe.wait_ge(k_in[b.r], (b.third + 1) * 96)
                        pe.wait_ge(q_in[b.r], (b.third + 1) * 96)
                    after(pe, max_out, b.n * MAXES + i - 1)
                    out = max_ps[i % 2][0:S, 0:n]
                    if masked:
                        nc.tensor.matmul(out, sh.ident_bf[0:S, 0:S], mask_q[:, c0:c0 + n], start=True, stop=False)
                    nc.tensor.matmul(out, q_st[b.r][0:SPLIT, h // 2, (h % 2) * S:(h % 2) * S + S],
                                     k_st[b.r][0:SPLIT, h // 2, c0:c0 + n], start=not masked, stop=True).then_inc(max_mm, 1)

                def turn_parts(b, step):
                    pe.wait_ge(parts_out, b.n + 1)
                    pe.wait_ge(dve_misc, step)
                    pe.wait_ge(prep_out, (b.n + 2) * PREP if there(b, 1) else B * PREP)
                    for pair in range(PAIRS):
                        bank, place = (misc, prep_ps)[pair // 4], pair % 4 * S
                        mm = nc.tensor.matmul(bank[SPLIT:FOLD, place:place + S], parts[:, pair, :, :].rearrange("q a t -> q (a t)"),
                                              sh.ident_bf[0:S, 0:S], start=True, stop=True)
                    mm.then_inc(pe_misc, 1)

                def exp_piece(b, i):
                    ch, k = i // 4, chunk_keys(i // 4)
                    if i == 0:
                        pe.wait_ge(max_placed, (b.n + 1) * 2)
                    after(pe, exp_out, b.n * SLOTS + i - 2)
                    out = exp_ps[i % 3][0:k, 0:4 * S]
                    if masked:
                        nc.tensor.matmul(out.rearrange("k (h q) -> k h q", h=4), sh.ident_bf[:, 0:k],
                                         mask_k[:, ch, :].unsqueeze(1).to_broadcast([P, 4, S]),
                                         start=True, stop=False, skip_group_check=True)
                    for t in range(2):
                        pair = 2 * (i % 4) + t
                        mm = nc.tensor.matmul(out[:, t * 2 * S:(t + 1) * 2 * S], k_st[b.r][0:FOLD, pair, ch * P:ch * P + k],
                                              q_st[b.r][0:FOLD, pair, :], start=not masked and t == 0, stop=True,
                                              skip_group_check=True)
                    mm.then_inc(exp_mm, 1)

                def values(b, i):
                    ch = i // 4
                    pe.wait_ge(exp_out, b.n * SLOTS + i + 1)
                    if i == 0:
                        after(pe, o_out, b.n)
                    for t in range(2):
                        pair = 2 * (i % 4) + t
                        tile, half = pair % 4, pair // 4
                        mm = nc.tensor.matmul(o_ps[32 * tile:32 * tile + 2 * (XD + 1), half * 2 * S:(half + 1) * 2 * S],
                                              v[b.r][:, ch, 2 * pair:2 * pair + 2, :].rearrange("k h d -> k (h d)"),
                                              probs[i % 4][:, t * 2 * S:(t + 1) * 2 * S], start=(ch == 0 and half == 0),
                                              stop=(ch == CH - 1), skip_group_check=True)
                    mm.then_inc(pv_mm, 1)

                def out_transpose(b, step):
                    pe.wait_ge(dve_misc, step)
                    pe.wait_ge(o_out, b.n + 1)
                    for t in range(4):
                        mm = nc.tensor.transpose(misc[0:S, t * P:t * P + P], oT[:, t * S:t * S + S], sh.ident[:, :])
                    mm.then_inc(pe_misc, 1)

                def out_back(step):
                    pe.wait_ge(dve_misc, step)
                    nc.tensor.transpose(misc[:, 0:S], o_n[:, :], sh.ident[0:S, 0:S]).then_inc(pe_misc, 1)

                def out_product(step):
                    pe.wait_ge(dve_misc, step)
                    nc.tensor.matmul(misc[0:S, 0:D], o_nT[:, :], woT, start=True, stop=True).then_inc(pe_misc, 1)

                def turn(b):
                    steps = Steps(b)
                    for s in range(SLOTS):
                        exp_piece(b, s)
                        if s >= 2:
                            values(b, s - 2)
                        if there(b, 1):
                            for k in max_at[s]:
                                max_piece(b.plus(1), k)
                        if not isinstance(b.n, int) or b.n > 0:
                            if s == 3:
                                out_transpose(b.plus(-1), steps.next())
                            if s == 6:
                                out_back(steps.next())
                            if s == 9:
                                out_product(steps.next())
                        if there(b, 2):
                            if s % 2 == 0 and s < 2 * PREP:
                                prep(b.plus(2), s // 2)
                            if s == 19:
                                xn_transpose(b.plus(2), steps.next())
                            if s == 22:
                                q_product(b.plus(2), steps.next())
                        if there(b, 1) and s == MAX_SLOTS + 3:
                            turn_parts(b.plus(1), steps.next())
                    values(b, SLOTS - 2)
                    values(b, SLOTS - 1)

                if masked:
                    pe.wait_ge(once, ONCE)
                    whole, side = misc[:, :].bitcast(BF16), prep_ps[:, :].bitcast(BF16)
                    for ch in range(CH):
                        k = chunk_keys(ch)
                        dst = whole[0:k, ch * S:ch * S + S] if ch < 10 else side[0:k, (ch - 10) * S:(ch - 10) * S + S]
                        mm = nc.tensor.transpose(dst, mask_q[:, ch * P:ch * P + k], sh.ident_bf[0:S, 0:S])
                    mm.then_inc(pe_misc, 1)
                    pe.wait_ge(dve_misc, 1)
                for n in range(2):
                    b = Turn(n, 0, n)
                    xn_transpose(b, HEAD + 2 * n)
                    q_product(b, HEAD + 2 * n + 1)
                    for m in range(PREP):
                        prep(b, m)
                b = Turn(0, 0, 0)
                for k in range(MAXES):
                    max_piece(b, k)
                turn_parts(b, HEAD + 4)
                pe.wait_ge(once, ONCE)
                pe.wait_ge(ones_in, 32)
                turns(pe, turn)
                steps = Steps(Turn(B, 0, 0))
                out_transpose(Turn(B - 1, 0, 0), steps.next())
                out_back(steps.next())
                out_product(steps.next())

            @block.scalar
            def _(act):
                def prep(b, m):
                    j = m % 3
                    c0, n = COLS[j]
                    act.wait_ge(prep_mm, b.n * PREP + m + 1)
                    if m < 3:
                        ins = nc.scalar.copy(ctxT[:, c0:c0 + n], prep_ps[:, 0:n])
                    elif m < 6:
                        if m == 3 and (not isinstance(b.n, int) or b.n > 0):
                            before = b.plus(-1)
                            act.wait_ge(k_written[before.r], (before.third + 1) * 16)
                        ins = nc.scalar.copy(k_parts[:, 0, c0:c0 + n], prep_ps[:, 0:n])
                    else:
                        if m == 6:
                            after(act, pv_mm, (b.n - 2) * SLOTS + 4 if not isinstance(b.n, int) or b.n > 2 else 0)
                        chunks = 4 if j < 2 else 3
                        ins = nc.scalar.copy(v[b.r][:, 4 * j:4 * j + chunks, :, 0:XD].rearrange("k c h d -> k (c h) d"),
                                             prep_ps[:, 0:chunks * P].rearrange("k (c d) -> k c d", d=XD))
                        if chunks < 4:
                            ins = nc.scalar.copy(v[b.r][0:LASTK, CH - 1, :, 0:XD],
                                                 prep_ps[0:LASTK, chunks * P:4 * P].rearrange("k (h d) -> k h d", d=XD))
                    ins.then_inc(prep_out, 1)

                def middle(b, j):
                    c0, n = COLS[j]
                    act.wait_ge(rest_out, b.n * 3 + j + 1)
                    nc.scalar.copy(k_parts[:, 1, c0:c0 + n], k_rest[:, c0:c0 + n]).then_inc(mid_out, 1)

                def place_max(b, step):
                    act.wait_ge(pe_misc, step + 1)
                    for t in range(2):
                        ins = nc.scalar.mul(q_st[b.r][SPLIT:FOLD, 4:8, t * S:t * S + S],
                                            prep_ps[SPLIT:FOLD, 0:4 * S].rearrange("a (p q) -> a p q", p=4),
                                            sh.row_side[SPLIT:FOLD, t:t + 1])
                    ins.then_inc(max_placed, 1)

                def exponentials(b, i):
                    k = chunk_keys(i // 4)
                    act.wait_ge(pv_mm, b.n * SLOTS + i + 1)
                    act.wait_ge(exp_mm, b.n * SLOTS + i + 1)
                    nc.scalar.activation(probs[i % 4][0:k, :], exp_ps[i % 3][0:k, 0:4 * S], ACT.Exp, scale=SCALE
                                         ).then_inc(exp_out, 1)

                def turn(b):
                    place_step = Steps(b).k + (3 if not isinstance(b.n, int) or b.n > 0 else 0) + (2 if there(b, 2) else 0)
                    for s in range(SLOTS):
                        exponentials(b, s)
                        if there(b, 1) and s == MAX_SLOTS + 3:
                            place_max(b.plus(1), place_step)
                        if there(b, 2):
                            if s % 2 == 0 and s < 2 * PREP:
                                prep(b.plus(2), s // 2)
                            if s in (8, 10, 12):
                                middle(b.plus(2), (s - 8) // 2)

                act.wait_ge(once, ONCE)
                for n in range(2):
                    b = Turn(n, 0, n)
                    for m in range(PREP):
                        prep(b, m)
                        if 4 <= m <= 6:
                            middle(b, m - 4)
                place_max(Turn(0, 0, 0), HEAD + 4)
                turns(act, turn)

            @block.vector
            def _(dve):
                nc.vector.memset(o_ps[:, :], 0.0).then_inc(once, 1)
                nc.vector.memset(misc[:, :], 0.0).then_inc(once, 1)
                for r in range(3):
                    nc.vector.memset(v[r][:, 0:CH - 1, :, XD:XD + 1], 1.0).then_inc(once, 1)
                    nc.vector.memset(v[r][:, CH - 1, :, :], 0.0).then_inc(once, 1)
                if masked:
                    nc.vector.memset(mask_k[:, CH - 1, :], 0.0).then_inc(once, 1)
                    dve.wait_ge(once, 9)
                else:
                    dve.wait_ge(once, 8)
                for r in range(3):
                    nc.vector.memset(v[r][0:LASTK, CH - 1, :, XD:XD + 1], 1.0).then_inc(once, 1)
                nc.vector.memset(k_st[0][SPLIT:FOLD, :, :], 1.0).then_inc(once, 1)
                dve.wait_ge(first_in, 16)
                if masked:
                    nc.vector.tensor_scalar(mask_q[:, 0:BODY].rearrange("q (c p) -> q c p", p=P),
                                            mask_raw[:, 0:BODY].rearrange("q (p c) -> q c p", p=P),
                                            0.0, NEG, ALU.is_equal, ALU.mult)
                    nc.vector.tensor_scalar(mask_q[:, BODY:SK], mask_raw[:, BODY:SK], 0.0, NEG, ALU.is_equal, ALU.mult
                                            ).then_inc(once, 1)
                    dve.wait_ge(pe_misc, 1)
                    nc.vector.tensor_copy(mask_k[:, 0:10, :].rearrange("k c q -> k (c q)"), misc[:, :].bitcast(BF16)[:, 0:10 * S])
                    side = prep_ps[:, :].bitcast(BF16)
                    nc.vector.tensor_copy(mask_k[:, 10, :], side[:, 0:S])
                    nc.vector.tensor_copy(mask_k[0:LASTK, 11, :], side[0:LASTK, S:2 * S]).then_inc(dve_misc, 1)
                else:
                    nc.vector.tensor_scalar(bo[:, :], bo[:, :], tanh_g, None, ALU.mult).then_inc(once, 1)
                dve.wait_ge(once, ONCE)

                chains = {n: Chain(dve, c_sem, per) for n, (c_sem, per) in
                          dict(norm=(chain_sems[0], 4), query=(chain_sems[1], 4), top=(chain_sems[2], 7),
                               out=(chain_sems[3], 3 if masked else 4)).items()}

                def maximum(b, i):
                    h, j = i // len(COLS), i % len(COLS)
                    dve.wait_ge(max_mm, b.n * MAXES + i + 1)
                    nc.vector.tensor_reduce(max_parts[:, h, j:j + 1], max_ps[i % 2][0:S, 0:COLS[j][1]], AX_X, ALU.max
                                            ).then_inc(max_out, 1)

                def split_max(b):
                    chain = chains["top"]
                    chain.begin(b.n)
                    dve.wait_ge(max_out, (b.n + 1) * MAXES)
                    chain.link(nc.vector.tensor_reduce(neg_max[:, :], max_parts[:, :, :], AX_X, ALU.max))
                    chain.link(nc.vector.tensor_scalar(neg_max[:, :], neg_max[:, :], NEG / 2, -1.0, ALU.max, ALU.mult))

                    def by_pairs(ap):
                        return ap.rearrange("q (p t) -> q p t", t=2)
                    chain.link(nc.vector.tensor_copy(parts[:, :, 0, :], by_pairs(neg_max[:, :])))
                    chain.link(nc.vector.tensor_tensor(by_pairs(rest[:, 0, :]), by_pairs(neg_max[:, :]), parts[:, :, 0, :], ALU.subtract))
                    chain.link(nc.vector.tensor_copy(parts[:, :, 1, :], by_pairs(rest[:, 0, :])))
                    chain.link(nc.vector.tensor_tensor(by_pairs(rest[:, 1, :]), by_pairs(rest[:, 0, :]), parts[:, :, 1, :], ALU.subtract))
                    chain.link(nc.vector.tensor_copy(parts[:, :, 2, :], by_pairs(rest[:, 1, :])))
                    nc.vector.sem_inc(parts_out, 1)
                    chain.end()

                def place_max(b, step):
                    dve.wait_ge(pe_misc, step + 1)
                    shape = [FOLD - SPLIT, 4, 2, S]
                    nc.vector.tensor_tensor(q_st[b.r][SPLIT:FOLD, 0:4, :].rearrange("a p (t q) -> a p t q", t=2),
                                            misc[SPLIT:FOLD, 0:4 * S].rearrange("a (p q) -> a p q", p=4).unsqueeze(2).to_broadcast(shape),
                                            sh.row_side[SPLIT:FOLD, :].unsqueeze(1).unsqueeze(3).to_broadcast(shape), ALU.mult
                                            ).then_inc(dve_misc, 1)
                    dve.wait_ge(dve_misc, step + 1)
                    nc.vector.sem_inc(max_placed, 1)

                def norm_begin(b):
                    chains["norm"].begin(b.n)
                    norm_stats(chains["norm"], nc, sh.x[:, bass.ds(b.n, 1), :], ln, LN_EPS, var_ready)

                def norm_end(b):
                    dve.wait_ge(rstd_ready, b.n + 1)
                    chains["norm"].link(nc.vector.tensor_scalar(xn[:, :], sh.x[:, b.n, :], ln.mv[:, 0, 0:1], ln.rstd[:, 0:1],
                                                                ALU.subtract, ALU.mult))
                    nc.vector.sem_inc(xn_out, 1)
                    chains["norm"].end()

                def copy_xnT(step):
                    dve.wait_ge(pe_misc, step + 1)
                    nc.vector.tensor_copy(xnT[:, :], misc[:, 0:S]).then_inc(dve_misc, 1)

                def split_q(b, step):
                    chain = chains["query"]
                    chain.begin(b.n)
                    dve.wait_ge(pe_misc, step + 1)
                    chain.link(nc.vector.tensor_copy(q_parts[:, 0, :], misc[:, 0:S]))
                    nc.vector.tensor_tensor(q_rest[:, :], misc[:, 0:S], q_parts[:, 0, :], ALU.subtract).then_inc(dve_misc, 1)
                    dve.wait_ge(dve_misc, step + 1)
                    chain.link(nc.vector.tensor_copy(q_parts[:, 1, :], q_rest[:, :]))
                    chain.link(nc.vector.tensor_tensor(q_parts[:, 2, :], q_rest[:, :], q_parts[:, 1, :], ALU.subtract))
                    if not isinstance(b.n, int) or b.n > 0:
                        before = b.plus(-1)
                        dve.wait_ge(q_written[before.r], (before.third + 1) * 16)
                    chain.link(nc.vector.tensor_tensor(q_par[:, :, :, :], q_parts[:, :, :].unsqueeze(2).to_broadcast([D, 3, 2, S]),
                                                       sh.side[:, :].unsqueeze(1).unsqueeze(3).to_broadcast([D, 3, 2, S]), ALU.mult))
                    nc.vector.sem_inc(q_out, 1)
                    chain.end()

                def k_less_high(b, j):
                    c0, n = COLS[j]
                    dve.wait_ge(prep_out, b.n * PREP + 3 + j + 1)
                    after(dve, low_out, b.n * 3)
                    nc.vector.tensor_tensor(k_rest[:, c0:c0 + n], prep_ps[:, 0:n], k_parts[:, 0, c0:c0 + n], ALU.subtract
                                            ).then_inc(rest_out, 1)

                def out_sums(b):
                    dve.wait_ge(pv_mm, (b.n + 1) * SLOTS + 4)
                    nc.vector.tensor_copy(oT[:, :], o_ps[:, 0:4 * S]).then_inc(o_out, 1)

                def out_divide(b, step):
                    chain = chains["out"]
                    chain.begin(b.n)
                    dve.wait_ge(pe_misc, step + 1)
                    m = misc[0:S, :].rearrange("q (a t j d) -> q a t j d", a=2, t=2, j=4)
                    r = rden[:, :].rearrange("q (a j t) -> q a t j", a=2, t=2)
                    o = o_n[:, :].rearrange("q (a j t d) -> q a t j d", a=2, t=2, d=XD)
                    for t in range(2):
                        chain.count(nc.vector.tensor_scalar(r[:, :, t, :], m[:, :, t, :, t * (XD + 1) + XD], 1e-9, None, ALU.max))
                    chain.wait()
                    chain.link(nc.vector.reciprocal(rden[:, :], rden[:, :]))
                    for t in range(2):
                        ins = nc.vector.tensor_tensor(o[:, :, t, :, :], m[:, :, t, :, t * (XD + 1):t * (XD + 1) + XD],
                                                      r[:, :, t, :].unsqueeze(3).to_broadcast([S, 2, 4, XD]), ALU.mult)
                    ins.then_inc(dve_misc, 1)

                def out_copy(step):
                    dve.wait_ge(pe_misc, step + 1)
                    nc.vector.tensor_copy(o_nT[:, :], misc[:, 0:S]).then_inc(dve_misc, 1)

                def out_add(b, step):
                    dve.wait_ge(pe_misc, step + 1)
                    ins = nc.vector.scalar_tensor_tensor(sh.x[:, b.n, :], misc[0:S, 0:D], tanh_g, sh.x[:, b.n, :],
                                                         ALU.mult, ALU.add)
                    if not masked:
                        chains["out"].link(ins)
                        ins = nc.vector.tensor_tensor(sh.x[:, b.n, :], sh.x[:, b.n, :], bo[:, :], ALU.add)
                    ins.then_inc(dve_misc, 1)
                    chains["out"].end()

                def turn(b):
                    steps = Steps(b)
                    first, second, third = steps.k, steps.k + 1, steps.k + 2
                    ended = not isinstance(b.n, int) or b.n > 0
                    if ended:
                        out_sums(b.plus(-1))
                        steps.k = steps.k + 3
                    for s in range(SLOTS):
                        if there(b, 1):
                            for k in max_at[s]:
                                maximum(b.plus(1), k)
                        if ended:
                            if s == 4:
                                out_divide(b.plus(-1), first)
                            if s == 7:
                                out_copy(second)
                            if s == 10:
                                out_add(b.plus(-1), third)
                        if there(b, 2):
                            if s in (6, 8, 10):
                                k_less_high(b.plus(2), (s - 6) // 2)
                            if s == 14:
                                norm_begin(b.plus(2))
                            if s == 17:
                                norm_end(b.plus(2))
                            if s == 20:
                                copy_xnT(steps.next())
                            if s == 23:
                                split_q(b.plus(2), steps.next())
                        if there(b, 1) and s == MAX_SLOTS:
                            split_max(b.plus(1))
                        if there(b, 1) and s == MAX_SLOTS + 3:
                            place_max(b.plus(1), steps.next())

                for n in range(2):
                    b = Turn(n, 0, n)
                    norm_begin(b)
                    norm_end(b)
                    copy_xnT(HEAD + 2 * n)
                    split_q(b, HEAD + 2 * n + 1)
                    for j in range(3):
                        k_less_high(b, j)
                b = Turn(0, 0, 0)
                for k in range(MAXES):
                    maximum(b, k)
                split_max(b)
                place_max(b, HEAD + 4)
                turns(dve, turn)
                last = Turn(B - 1, 0, 0)
                steps = Steps(Turn(B, 0, 0))
                out_sums(last)
                out_divide(last, steps.next())
                out_copy(steps.next())
                out_add(last, steps.next())


GB = 4
GT = GB * S
GROUPS = B // GB
UH = 4


class SmallAttention:

    def __init__(self, nc, c, ctx, name, heads, sh, mask=None):
        self.nc, self.heads, self.size, self.sh, self.mask = nc, heads, D // heads, sh, mask
        self.head_mask = sh.head16 if heads == 16 else sh.head8
        self.scale = float(self.size) ** -0.5
        self.per = heads // UH
        self.units = GB * self.per

        def sb(n, shape, dt=F32):
            return c.enter_context(nc.sbuf_tensor(f"{name}_{n}", shape, dt))

        def ps(n):
            return c.enter_context(nc.psum_tensor(f"{name}_{n}", [P, 512], F32))

        def sem(n):
            return ctx.enter_context(nc.semaphore(f"{name}_{n}"))

        self.qT = sb("qT", [D, GT])
        self.k_bd = sb("k_bd", [D, GB, heads, S])
        self.v = sb("v", [S, GB, heads, self.size + 1])
        self.top = [sb(f"top{r}", [S, UH]) for r in range(2)]
        self.diff = [sb(f"diff{r}", [S, UH, S]) for r in range(2)]
        self.probs = [sb(f"probs{r}", [S, UH, S]) for r in range(2)]
        self.probsT = [sb(f"probsT{r}", [S, UH, S]) for r in range(2)]
        self.rden = [sb(f"rden{r}", [S, heads]) for r in range(2)]
        self.o = sb("o", [S, GB, D])
        self.s_ps = [ps(f"s_ps{r}") for r in range(2)]
        self.t_ps = [ps(f"t_ps{r}") for r in range(2)]
        self.o_ps = [ps(f"o_ps{r}") for r in range(2)]
        self.s_mm = sem("s_mm")
        self.top_done = sem("top_done")
        self.s_out = sem("s_out")
        self.exp_done = sem("exp_done")
        self.t_mm = sem("t_mm")
        self.t_out = sem("t_out")
        self.v_mm = sem("v_mm")
        self.r_done = sem("r_done")
        self.o_out = sem("o_out")

    def prime(self, pe=None, act=None, dve=None):
        for eng, sems in ((pe, (self.t_mm, self.v_mm)), (act, (self.exp_done, self.t_out)), (dve, (self.s_out, self.o_out))):
            for s in sems if eng is not None else ():
                eng.sem_inc(s, 1)

    def tensor(self, pe, turn):
        nc, n = self.nc, self.units
        for i in range(n + 2):
            if i < n:
                b, h0 = i // self.per, UH * (i % self.per)
                pe.wait_ge(self.s_out, 1 + turn * n + max(i - 1, 0))
                bank = self.s_ps[i % 2][0:S, 0:UH * S]
                mm = nc.tensor.matmul(bank, self.qT[:, b * S:b * S + S],
                                      self.k_bd[:, b, h0:h0 + UH, :].rearrange("d h k -> d (h k)"),
                                      start=True, stop=self.mask is None)
                if self.mask is not None:
                    mm = nc.tensor.matmul(bank.rearrange("q (h k) -> q h k", h=UH), self.sh.ident_bf[0:S, 0:S],
                                          self.mask[:, :].unsqueeze(1).to_broadcast([S, UH, S]), start=False, stop=True)
                mm.then_inc(self.s_mm, 1)
            if 1 <= i <= n:
                j = i - 1
                pe.wait_ge(self.exp_done, 1 + turn * n + j + 1)
                pe.wait_ge(self.t_out, 1 + turn * n + max(j - 1, 0))
                for h in range(UH):
                    mm = nc.tensor.transpose(self.t_ps[j % 2][0:S, h * S:h * S + S], self.probs[j % 2][:, h, :],
                                             self.sh.ident[0:S, 0:S])
                mm.then_inc(self.t_mm, 1)
            if i >= 2:
                j = i - 2
                b, h0 = j // self.per, UH * (j % self.per)
                if h0 == 0:
                    pe.wait_ge(self.o_out, 1 + turn * GB + max(b - 1, 0))
                pe.wait_ge(self.t_out, 1 + turn * n + j + 1)
                w = self.size + 1
                for h in range(UH):
                    mm = nc.tensor.matmul(self.o_ps[b % 2][0:S, (h0 + h) * w:(h0 + h) * w + w],
                                          self.probsT[j % 2][:, h, :], self.v[:, b, h0 + h, :], start=True, stop=True)
                mm.then_inc(self.v_mm, 1)

    def scalar(self, act, turn):
        nc, n = self.nc, self.units
        for i in range(n + 1):
            if i < n:
                act.wait_ge(self.s_out, 1 + turn * n + i + 1)
                act.wait_ge(self.t_mm, 1 + turn * n + max(i - 1, 0))
                nc.scalar.activation(self.probs[i % 2][:, :, :], self.diff[i % 2][:, :, :], ACT.Exp, scale=self.scale
                                     ).then_inc(self.exp_done, 1)
            if i >= 1:
                j = i - 1
                act.wait_ge(self.t_mm, 1 + turn * n + j + 1)
                act.wait_ge(self.v_mm, 1 + turn * n + max(j - 1, 0))
                nc.scalar.copy(self.probsT[j % 2][:, :, :].rearrange("k h q -> k (h q)"), self.t_ps[j % 2][0:S, 0:UH * S]
                               ).then_inc(self.t_out, 1)

    def vector(self, dve, turn):
        nc, n = self.nc, self.units

        def divide(b):
            w = self.size + 1
            dve.wait_ge(self.v_mm, 1 + turn * n + (b + 1) * self.per)
            o = self.o_ps[b % 2][0:S, 0:self.heads * w].rearrange("q (h d) -> q h d", d=w)
            nc.vector.reciprocal(self.rden[b % 2][:, :], o[:, :, self.size]).then_inc(self.r_done, 1)
            dve.wait_ge(self.r_done, turn * GB + b + 1)
            nc.vector.tensor_tensor(self.o[:, b, :].rearrange("q (h d) -> q h d", h=self.heads), o[:, :, 0:self.size],
                                    self.rden[b % 2][:, :].unsqueeze(2).to_broadcast([S, self.heads, self.size]), ALU.mult
                                    ).then_inc(self.o_out, 1)

        for i in range(n + 2):
            if i < n:
                dve.wait_ge(self.s_mm, turn * n + i + 1)
                scores = self.s_ps[i % 2][0:S, 0:UH * S].rearrange("q (h k) -> q h k", h=UH)
                nc.vector.tensor_reduce(self.top[i % 2][:, :], scores, AX_X, ALU.max).then_inc(self.top_done, 1)
                dve.wait_ge(self.top_done, turn * n + i + 1)
                dve.wait_ge(self.exp_done, 1 + turn * n + max(i - 1, 0))
                nc.vector.tensor_tensor(self.diff[i % 2][:, :, :], scores,
                                        self.top[i % 2][:, :].unsqueeze(2).to_broadcast([S, UH, S]), ALU.subtract
                                        ).then_inc(self.s_out, 1)
            if i >= self.per + 1 and (i - 1) % self.per == 0:
                divide((i - 1) // self.per - 1)


def ffn0_edges():
    nodes, first = [], 0
    for c in range(6):
        n = min(c + 1, 5)
        source = c - n
        nodes.append(((c - 1, source, source + n // 2), (first + n - 1, first, first + n // 2)))
        first += n
    return nodes


def cell_ffn(nc, ctx, sh, A):
    NODES = ffn0_edges()
    NN = len(NODES)
    tanh_g = sh.tanh_g[0:S, 2:3]
    JN = 4 * NN + 1
    c = ExitStack()
    with c:
        def sb(name, shape, dt=F32):
            return c.enter_context(nc.sbuf_tensor(f"cell_{name}", shape, dt))

        def sem(name):
            return ctx.enter_context(nc.semaphore(f"cell_{name}"))

        we = sb("we", [D, 20, D])
        w = {n: sb(n, [D, NN, D]) for n in ("Wq", "Wk", "Wv", "Wo")}
        ew = sb("ew", [P, NN * 3])
        act_w = sb("act_w", [P, NN])
        be = sb("be", [P, NN * 3])
        gain, shift = sb("gain", [S, D]), sb("shift", [S, D])
        z = sb("z", [S, GB, D])
        nodes = [sb(f"node{n}", [D, GT]) for n in range(NN + 1)]
        qinT, kinT, vinT = sb("qinT", [D, GT]), sb("kinT", [D, GT]), sb("vinT", [D, GT])
        oT = sb("oT", [D, GT])
        ln = LayerNorm(c, nc, "cell_ln", S, sh.minus_half, GB)
        J = [c.enter_context(nc.psum_tensor(f"cell_J{r}", [P, 512], F32)) for r in range(2)]
        att = SmallAttention(nc, c, ctx, "cell_att", 8, sh)

        loaded = sem("loaded")
        j_mm = sem("j_mm")
        j_act, j_dve = sem("j_act"), sem("j_dve")
        var_ready, rstd_ready = sem("var_ready"), sem("rstd_ready")
        z_ready = sem("z_ready")
        chain_sem = sem("chain")
        LOADS = 16 * (5 + 2 + 18 + 2)

        with nc.Block() as block:
            @block.sync
            def _(sp):
                sp.dma_start(we[:, :, :], A["L0_ffn_We"].rearrange("e i o -> i e o")).then_inc(loaded, 16)
                for n in w:
                    sp.dma_start(w[n][:, :, :], A["L0_ffn_" + n].rearrange("c i o -> i c o")).then_inc(loaded, 16)
                sp.dma_start(ew[:, :], A["L0_ffn_ew"].rearrange("c k -> (c k)").partition_broadcast(P)).then_inc(loaded, 16)
                sp.dma_start(act_w[:, :], A["L0_ffn_act_w"].partition_broadcast(P)).then_inc(loaded, 16)
                for n, (_, edges) in enumerate(NODES):
                    for k, e in enumerate(edges):
                        sp.dma_start(be[:, 3 * n + k:3 * n + k + 1], A["L0_ffn_be"][e, :].unsqueeze(1)).then_inc(loaded, 16)
                sp.dma_start(gain[:, :], A["L0_ffn_ln_g"].partition_broadcast(S)).then_inc(loaded, 16)
                sp.dma_start(shift[:, :], A["L0_ffn_ln_b"].partition_broadcast(S)).then_inc(loaded, 16)

            @block.gpsimd
            def _(pool):
                with pool.Fori(0, GROUPS * 2) as i:
                    pool.wait_ge(var_ready, i + 1)
                    ln.inverse_root(nc).then_inc(rstd_ready, 1)

            @block.tensor
            def _(pe):
                pe.wait_ge(loaded, LOADS)
                att.prime(pe=pe)
                with pe.Fori(0, GROUPS) as g:
                    pe.wait_ge(z_ready, g + 1)
                    pe.wait_ge(j_act, 1 + g * JN)
                    for b in range(GB):
                        mm = nc.tensor.transpose(J[0][:, b * S:b * S + S], z[:, b, :], sh.ident[0:S, 0:S])
                    mm.then_inc(j_mm, 1)
                    for n, ((sq, sk, sv), (eq, ek, ev)) in enumerate(NODES):
                        a0, d0 = g * JN + 1 + 4 * n, g * JN + 4 * n
                        bank = [J[r][:, 0:GT] for r in range(2)]

                        def product(r, lhsT, rhs):
                            nc.tensor.matmul(bank[r], lhsT, rhs, start=True, stop=True).then_inc(j_mm, 1)
                        pe.wait_ge(j_dve, 1 + d0)
                        pe.wait_ge(j_act, 1 + a0)
                        product(1, we[:, ek, :], nodes[sk + 1][:, :])
                        product(0, we[:, eq, :], nodes[sq + 1][:, :])
                        pe.wait_ge(j_act, 1 + a0 + 1)
                        product(0, we[:, ev, :], nodes[sv + 1][:, :])
                        pe.wait_ge(j_dve, 1 + d0 + 1)
                        product(1, w["Wk"][:, n, :], kinT[:, :])
                        pe.wait_ge(j_act, 1 + a0 + 2)
                        product(0, w["Wq"][:, n, :], qinT[:, :])
                        pe.wait_ge(j_dve, 1 + d0 + 2)
                        for b in range(GB):
                            mm = nc.tensor.matmul(J[1][0:S, b * D:b * D + D], vinT[:, b * S:b * S + S], w["Wv"][:, n, :],
                                                  start=True, stop=True)
                        mm.then_inc(j_mm, 1)
                        pe.wait_ge(j_act, 1 + a0 + 3)
                        pe.wait_ge(j_dve, 1 + d0 + 3)
                        att.tensor(pe, g * NN + n)
                        pe.wait_ge(att.o_out, 1 + (g * NN + n) * GB + GB)
                        for b in range(GB):
                            mm = nc.tensor.transpose(J[0][:, b * S:b * S + S], att.o[:, b, :], sh.ident[0:S, 0:S])
                        mm.then_inc(j_mm, 1)
                        pe.wait_ge(j_act, 1 + a0 + 4)
                        product(1, w["Wo"][:, n, :], oT[:, :])
                    pe.wait_ge(j_dve, 1 + g * JN + 4 * NN)
                    for b in range(GB):
                        mm = nc.tensor.transpose(J[1][0:S, b * D:b * D + D], nodes[NN][:, b * S:b * S + S], sh.ident[:, :])
                    mm.then_inc(j_mm, 1)

            @block.scalar
            def _(act):
                act.wait_ge(chain_sem, 1)
                att.prime(act=act)
                act.sem_inc(j_act, 1)
                with act.Fori(0, GROUPS) as g:
                    m0 = g * 2 * JN
                    act.wait_ge(j_mm, m0 + 1)
                    nc.scalar.copy(nodes[0][:, :], J[0][:, 0:GT]).then_inc(j_act, 1)
                    for n in range(NN):
                        m = m0 + 1 + 8 * n
                        for k, (at, dst) in enumerate(((2, qinT), (3, vinT))):
                            act.wait_ge(j_mm, m + at)
                            nc.scalar.activation(dst[:, :], J[0][:, 0:GT], ACT.Identity,
                                                 bias=be[:, 3 * n + 2 * k:3 * n + 2 * k + 1],
                                                 scale=ew[:, 3 * n + 2 * k:3 * n + 2 * k + 1]).then_inc(j_act, 1)
                        act.wait_ge(j_mm, m + 5)
                        nc.scalar.copy(att.qT[:, :], J[0][:, 0:GT]).then_inc(j_act, 1)
                        att.scalar(act, g * NN + n)
                        act.wait_ge(j_mm, m + 7)
                        nc.scalar.copy(oT[:, :], J[0][:, 0:GT]).then_inc(j_act, 1)

            @block.vector
            def _(dve):
                dve.wait_ge(loaded, LOADS)
                nc.vector.tensor_tensor(be[:, :], be[:, :], ew[:, :], ALU.mult).then_inc(chain_sem, 1)
                nc.vector.tensor_scalar(gain[:, :], gain[:, :], tanh_g, None, ALU.mult).then_inc(chain_sem, 1)
                nc.vector.tensor_scalar(shift[:, :], shift[:, :], tanh_g, None, ALU.mult).then_inc(chain_sem, 1)
                nc.vector.memset(att.v[:, :, :, :], 1.0).then_inc(chain_sem, 1)
                dve.wait_ge(chain_sem, 4)
                chain = Chain(dve, chain_sem, 5 * GB + 5, 4)
                att.prime(dve=dve)
                dve.sem_inc(j_dve, 1)
                with dve.Fori(0, GROUPS) as g:
                    chain.begin(g)
                    x = sh.x[:, bass.ds(g * GB, GB), :]
                    norm_stats(chain, nc, x, ln, LN_EPS, var_ready)
                    dve.wait_ge(rstd_ready, g * 2 + 1)
                    for b in range(GB):
                        ins = nc.vector.tensor_scalar(z[:, b, :], sh.x[:, g * GB + b, :], ln.mv[:, b, 0:1],
                                                      ln.rstd[:, b:b + 1], ALU.subtract, ALU.mult)
                    ins.then_inc(z_ready, 1)
                    for n in range(NN):
                        m = g * 2 * JN + 1 + 8 * n
                        dve.wait_ge(j_mm, m + 1)
                        nc.vector.tensor_scalar(kinT[:, :], J[1][:, 0:GT], ew[:, 3 * n + 1:3 * n + 2],
                                                be[:, 3 * n + 1:3 * n + 2], ALU.mult, ALU.add).then_inc(j_dve, 1)
                        dve.wait_ge(j_mm, m + 4)
                        for b in range(GB):
                            ins = nc.vector.tensor_tensor(att.k_bd[:, b, :, :],
                                                          J[1][:, b * S:b * S + S].unsqueeze(1).to_broadcast([D, 8, S]),
                                                          sh.head8[:, :].unsqueeze(2).to_broadcast([D, 8, S]), ALU.mult)
                        ins.then_inc(j_dve, 1)
                        dve.wait_ge(j_mm, m + 6)
                        nc.vector.tensor_copy(att.v[:, :, :, 0:att.size].rearrange("k b h d -> k (b h) d"),
                                              J[1][0:S, :].rearrange("k (c d) -> k c d", d=att.size)).then_inc(j_dve, 1)
                        att.vector(dve, g * NN + n)
                        dve.wait_ge(j_mm, m + 8)
                        nc.vector.scalar_tensor_tensor(nodes[n + 1][:, :], J[1][:, 0:GT], act_w[:, n:n + 1], qinT[:, :],
                                                       ALU.mult, ALU.add).then_inc(j_dve, 1)
                    dve.wait_ge(j_mm, (g + 1) * 2 * JN)
                    last = J[1][0:S, :].rearrange("q (b d) -> q b d", b=GB)
                    norm_stats(chain, nc, last, ln, L0_LN_EPS, var_ready)
                    dve.wait_ge(rstd_ready, g * 2 + 2)
                    for b in range(GB):
                        chain.count(nc.vector.tensor_scalar(z[:, b, :], last[:, b, :], ln.mv[:, b, 0:1], ln.rstd[:, b:b + 1],
                                                            ALU.subtract, ALU.mult))
                    chain.wait()
                    nc.vector.sem_inc(j_dve, 1)
                    chain.link(nc.vector.tensor_tensor(z[:, :, :], z[:, :, :], gain[:, :].unsqueeze(1).to_broadcast([S, GB, D]), ALU.mult))
                    chain.link(nc.vector.tensor_tensor(z[:, :, :], z[:, :, :], shift[:, :].unsqueeze(1).to_broadcast([S, GB, D]), ALU.add))
                    chain.link(nc.vector.tensor_tensor(x, x, z[:, :, :], ALU.add))
                    chain.end()


def moe_ffn(nc, ctx, sh, A):
    E, F, TOP = 8, 512, 2
    FT = F // P
    UNITS = E * FT
    tanh_g = sh.tanh_g[0:S, 3:4]
    J_ACT, J_DVE = 5, 5
    CAUSAL = -float(2 ** 100)
    c = ExitStack()
    with c:
        def sb(name, shape, dt=F32):
            return c.enter_context(nc.sbuf_tensor(f"moe_{name}", shape, dt))

        def sem(name):
            return ctx.enter_context(nc.semaphore(f"moe_{name}"))

        wqkv, wo, w_gate = sb("wqkv", [D, 3, D]), sb("wo", [D, D]), sb("w_gate", [D, E])
        w1, w2 = sb("w1", [D, E, F]), sb("w2", [P, E, FT, D])
        b1_rows = sb("b1_rows", [UNITS, P])
        b1, b2 = sb("b1", [P, E, FT]), sb("b2", [E, D])
        norms = {n: sb(n, [S, D]) for n in ("ln1_g", "ln1_b", "ln2_g", "ln2_b")}
        causal = sb("causal", [S, S], BF16)
        before = sb("before", [S, E, E])
        x_in, h = sb("x_in", [S, GB, D]), sb("h", [S, GB, D])
        hT, oT, xfT = sb("hT", [D, GT]), sb("oT", [D, GT]), sb("xfT", [D, GT])
        ln = LayerNorm(c, nc, "moe_ln", S, sh.minus_half, GB)
        p = {n: sb(n, [S, GB, E]) for n in ("shifted", "exps", "prob", "rank", "kept", "gate")}
        one = {n: sb(n, [S, GB]) for n in ("best", "total", "norm", "kept_sum")}
        above, same = sb("above", [S, GB, E, E]), sb("same", [S, GB, E, E])
        gateT = sb("gateT", [E, GT])
        act_h = [sb(f"act_h{r}", [P, GT]) for r in range(2 * FT)]
        J = [c.enter_context(nc.psum_tensor(f"moe_J{r}", [P, 512], F32)) for r in range(2)]
        att = SmallAttention(nc, c, ctx, "moe_att", 16, sh, causal)
        h_ps, y_ps = att.s_ps, att.t_ps

        loaded, made = sem("loaded"), sem("made")
        j_mm = sem("j_mm")
        j_act, j_dve = sem("j_act"), sem("j_dve")
        var_ready, rstd_ready = sem("var_ready"), sem("rstd_ready")
        tokens = sem("tokens")
        shifted_ready, exps_ready = sem("shifted_ready"), sem("exps_ready")
        gate_ready = sem("gate_ready")
        h_mm, h_act = sem("h_mm"), sem("h_act")
        y_mm, y_out = sem("y_mm"), sem("y_out")
        b1_ready = sem("b1_ready")
        chain_sem = sem("chain")
        LOADS = 16 * 11

        with nc.Block() as block:
            @block.sync
            def _(sp):
                for dst, src in (
                    (wqkv[:, :, :], A["L1_ffn_w_qkv"].rearrange("i (k o) -> i k o", k=3)), (wo[:, :], A["L1_ffn_w_o"]),
                    (w_gate[:, :], A["L1_ffn_w_gate"]), (w1[:, :, :], A["L1_ffn_w1"].rearrange("e d f -> d e f")),
                    (w2[:, :, :, :], A["L1_ffn_w2"].rearrange("e (t p) d -> p e t d", p=P)),
                    (b1_rows[:, :], A["L1_ffn_b1"].rearrange("e (t p) -> (e t) p", p=P)), (b2[:, :], A["L1_ffn_b2"]),
                ) + tuple((norms[n][:, :], A["L1_ffn_" + n].partition_broadcast(S)) for n in norms):
                    sp.dma_start(dst, src).then_inc(loaded, 16)

            @block.gpsimd
            def _(pool):
                pool.memset(causal[:, :], 0.0).then_inc(made, 1)
                pool.memset(before[:, :, :], 0.0).then_inc(made, 1)
                pool.wait_ge(made, 2)
                pool.affine_select(out=causal[:, :], in_=causal[:, :], compare_op=ALU.is_ge, fill=CAUSAL, base=0,
                                   pattern=[[-1, S]], channel_multiplier=1).then_inc(made, 1)
                pool.affine_select(out=before[:, :, :], in_=before[:, :, :], compare_op=ALU.is_ge, fill=1.0, base=0,
                                   pattern=[[-1, E], [1, E]], channel_multiplier=0).then_inc(made, 1)
                with pool.Fori(0, GROUPS * 3) as i:
                    pool.wait_ge(var_ready, i + 1)
                    ln.inverse_root(nc).then_inc(rstd_ready, 1)

            @block.tensor
            def _(pe):
                pe.wait_ge(loaded, LOADS)
                pe.wait_ge(made, 4)
                bank = [J[r][:, 0:GT] for r in range(2)]
                nc.tensor.transpose(J[0][:, 0:UNITS], b1_rows[:, :], sh.ident[0:UNITS, 0:UNITS]).then_inc(b1_ready, 1)
                pe.wait_ge(b1_ready, 2)

                def turn_tokens(src, r):
                    for b in range(GB):
                        mm = nc.tensor.transpose(J[r][:, b * S:b * S + S], src[:, b, :], sh.ident[0:S, 0:S])
                    mm.then_inc(j_mm, 1)

                def per_batch(r, lhsT, rhs, n):
                    for b in range(GB):
                        mm = nc.tensor.matmul(J[r][0:S, b * n:b * n + n], lhsT[:, b * S:b * S + S], rhs, start=True, stop=True)
                    mm.then_inc(j_mm, 1)

                att.prime(pe=pe)
                with pe.Fori(0, GROUPS) as g:
                    a0, d0 = g * J_ACT, g * J_DVE
                    pe.wait_ge(tokens, g * 2 + 1)
                    pe.wait_ge(j_act, 1 + a0)
                    turn_tokens(h, 0)
                    pe.wait_ge(j_act, 1 + a0 + 1)
                    pe.wait_ge(j_dve, 1 + d0)
                    nc.tensor.matmul(bank[1], wqkv[:, 1, :], hT[:, :], start=True, stop=True).then_inc(j_mm, 1)
                    nc.tensor.matmul(bank[0], wqkv[:, 0, :], hT[:, :], start=True, stop=True).then_inc(j_mm, 1)
                    pe.wait_ge(j_dve, 1 + d0 + 1)
                    per_batch(1, hT, wqkv[:, 2, :], D)
                    pe.wait_ge(j_act, 1 + a0 + 2)
                    pe.wait_ge(j_dve, 1 + d0 + 2)
                    pe.wait_ge(y_out, 1 + g * E)
                    att.tensor(pe, g)
                    pe.wait_ge(att.o_out, 1 + g * GB + GB)
                    turn_tokens(att.o, 0)
                    pe.wait_ge(j_act, 1 + a0 + 3)
                    per_batch(1, oT, wo[:, :], D)
                    pe.wait_ge(tokens, g * 2 + 2)
                    turn_tokens(h, 0)
                    pe.wait_ge(j_act, 1 + a0 + 4)
                    per_batch(1, xfT, w_gate[:, :], E)

                    def inner(i):
                        e, t = i // FT, i % FT
                        pe.wait_ge(h_act, 1 + g * UNITS + max(i - 1, 0))
                        nc.tensor.matmul(h_ps[i % 2][:, 0:GT], w1[:, e, t * P:t * P + P], xfT[:, :], start=True, stop=True
                                         ).then_inc(h_mm, 1)

                    def outer(e):
                        pe.wait_ge(y_out, 1 + g * E + max(e - 1, 0))
                        pe.wait_ge(h_act, 1 + g * UNITS + (e + 1) * FT)
                        for b in range(GB):
                            for t in range(FT):
                                mm = nc.tensor.matmul(y_ps[e % 2][0:S, b * D:b * D + D],
                                                      act_h[(e % 2) * FT + t][:, b * S:b * S + S], w2[:, e, t, :],
                                                      start=(t == 0), stop=(t == FT - 1))
                        mm.then_inc(y_mm, 1)

                    for i in range(FT):
                        inner(i)
                    for e in range(1, E):
                        for t in range(FT):
                            inner(e * FT + t)
                        if e == 1:
                            pe.wait_ge(gate_ready, g + 1)
                            for b in range(GB):
                                mm = nc.tensor.transpose(J[0][0:E, b * S:b * S + S], p["gate"][:, b, :], sh.ident[0:S, 0:S])
                            mm.then_inc(j_mm, 1)
                            pe.wait_ge(j_act, 1 + a0 + 5)
                            for b in range(GB):
                                mm = nc.tensor.matmul(J[1][0:S, b * D:b * D + D], gateT[:, b * S:b * S + S], b2[:, :],
                                                      start=True, stop=True)
                            mm.then_inc(j_mm, 1)
                        outer(e - 1)
                    outer(E - 1)

            @block.scalar
            def _(act):
                act.wait_ge(b1_ready, 1)
                nc.scalar.copy(b1[:, :, :].rearrange("p e t -> p (e t)"), J[0][:, 0:UNITS]).then_inc(b1_ready, 1)
                act.wait_ge(b1_ready, 2)
                att.prime(act=act)
                act.sem_inc(j_act, 1)
                act.sem_inc(h_act, 1)
                with act.Fori(0, GROUPS) as g:
                    def out_of_bank(at, dst):
                        act.wait_ge(j_mm, g * 10 + at)
                        nc.scalar.copy(dst, J[0][0:dst.shape[0], 0:GT]).then_inc(j_act, 1)
                    out_of_bank(1, hT[:, :])
                    out_of_bank(3, att.qT[:, :])
                    att.scalar(act, g)
                    out_of_bank(5, oT[:, :])
                    out_of_bank(7, xfT[:, :])
                    act.wait_ge(shifted_ready, g + 1)
                    nc.scalar.activation(p["exps"][:, :, :], p["shifted"][:, :, :], ACT.Exp).then_inc(exps_ready, 1)
                    for i in range(UNITS):
                        e, t = i // FT, i % FT
                        if i == 2 * FT:
                            out_of_bank(9, gateT[:, :])
                        act.wait_ge(h_mm, g * UNITS + i + 1)
                        if e >= 2:
                            act.wait_ge(y_mm, g * E + e - 1)
                        nc.scalar.activation(act_h[i % (2 * FT)][:, :], h_ps[i % 2][:, 0:GT], ACT.Gelu_apprx_tanh,
                                             bias=b1[:, e, t:t + 1]).then_inc(h_act, 1)

            @block.vector
            def _(dve):
                nc.vector.memset(att.v[:, :, :, :], 1.0).then_inc(chain_sem, 1)
                dve.wait_ge(chain_sem, 1)
                dve.wait_ge(loaded, LOADS)
                dve.wait_ge(made, 4)
                chain = Chain(dve, chain_sem, 3 * (3 * GB + 1) + 4 + 1 + 2 + 3 + 2 + GB + 6 + 1 + E * GB + 1, 1)

                def normalize(g, k, dst, x, gain=None, shift=None):
                    norm_stats(chain, nc, x, ln, LN_EPS, var_ready)
                    dve.wait_ge(rstd_ready, g * 3 + k + 1)
                    for b in range(GB):
                        chain.count(nc.vector.tensor_scalar(dst[:, b, :], x[:, b, :], ln.mv[:, b, 0:1], ln.rstd[:, b:b + 1],
                                                            ALU.subtract, ALU.mult))
                    chain.wait()
                    if gain is not None:
                        chain.link(nc.vector.tensor_tensor(dst, dst, gain[:, :].unsqueeze(1).to_broadcast([S, GB, D]), ALU.mult))
                        chain.link(nc.vector.tensor_tensor(dst, dst, shift[:, :].unsqueeze(1).to_broadcast([S, GB, D]), ALU.add))

                att.prime(dve=dve)
                dve.sem_inc(j_dve, 1)
                dve.sem_inc(y_out, 1)
                with dve.Fori(0, GROUPS) as g:
                    chain.begin(g)
                    x = sh.x[:, bass.ds(g * GB, GB), :]
                    xi, ht = x_in[:, :, :], h[:, :, :]
                    normalize(g, 0, xi, x)
                    normalize(g, 1, ht, xi, norms["ln1_g"], norms["ln1_b"])
                    nc.vector.sem_inc(tokens, 1)
                    dve.wait_ge(j_mm, g * 10 + 2)
                    for b in range(GB):
                        ins = nc.vector.tensor_tensor(att.k_bd[:, b, :, :],
                                                      J[1][:, b * S:b * S + S].unsqueeze(1).to_broadcast([D, 16, S]),
                                                      sh.head16[:, :].unsqueeze(2).to_broadcast([D, 16, S]), ALU.mult)
                    ins.then_inc(j_dve, 1)
                    dve.wait_ge(j_mm, g * 10 + 4)
                    nc.vector.tensor_copy(att.v[:, :, :, 0:att.size].rearrange("k b h d -> k (b h) d"),
                                          J[1][0:S, :].rearrange("k (c d) -> k c d", d=att.size)).then_inc(j_dve, 1)
                    att.vector(dve, g)
                    dve.wait_ge(j_mm, g * 10 + 6)
                    chain.link(nc.vector.tensor_tensor(xi, xi, J[1][0:S, :].rearrange("q (b d) -> q b d", b=GB), ALU.add))
                    nc.vector.sem_inc(j_dve, 1)
                    normalize(g, 2, ht, xi, norms["ln2_g"], norms["ln2_b"])
                    nc.vector.sem_inc(tokens, 1)

                    def wide(ap):
                        return ap.unsqueeze(2).to_broadcast([S, GB, E])
                    P_ = {n: t[:, :, :] for n, t in p.items()}
                    O_ = {n: t[:, :] for n, t in one.items()}
                    dve.wait_ge(j_mm, g * 10 + 8)
                    logits = J[1][0:S, 0:GB * E].rearrange("q (b e) -> q b e", b=GB)
                    chain.link(nc.vector.tensor_reduce(O_["best"], logits, AX_X, ALU.max))
                    chain.link(nc.vector.tensor_tensor(P_["shifted"], logits, wide(O_["best"]), ALU.subtract))
                    nc.vector.sem_inc(j_dve, 1)
                    nc.vector.sem_inc(shifted_ready, 1)
                    dve.wait_ge(exps_ready, g + 1)
                    chain.link(nc.vector.tensor_reduce(O_["total"], P_["exps"], AX_X, ALU.add))
                    chain.link(nc.vector.reciprocal(O_["norm"], O_["total"]))
                    chain.link(nc.vector.tensor_tensor(P_["prob"], P_["exps"], wide(O_["norm"]), ALU.mult))
                    other = P_["prob"].unsqueeze(2).to_broadcast([S, GB, E, E])
                    own = P_["prob"].unsqueeze(3).to_broadcast([S, GB, E, E])
                    chain.count(nc.vector.tensor_tensor(above[:, :, :, :], other, own, ALU.is_gt))
                    chain.link(nc.vector.tensor_tensor(same[:, :, :, :], other, own, ALU.is_equal))
                    for b in range(GB):
                        chain.count(nc.vector.tensor_tensor(same[:, b, :, :], same[:, b, :, :], before[:, :, :], ALU.mult))
                    chain.wait()
                    chain.link(nc.vector.tensor_tensor(above[:, :, :, :], above[:, :, :, :], same[:, :, :, :], ALU.add))
                    chain.link(nc.vector.tensor_reduce(P_["rank"], above[:, :, :, :], AX_X, ALU.add))
                    chain.link(nc.vector.scalar_tensor_tensor(P_["kept"], P_["rank"], TOP - 0.5, P_["prob"], ALU.is_lt, ALU.mult))
                    chain.link(nc.vector.tensor_reduce(O_["kept_sum"], P_["kept"], AX_X, ALU.add))
                    chain.link(nc.vector.reciprocal(O_["norm"], O_["kept_sum"]))
                    chain.link(nc.vector.tensor_tensor(P_["gate"], P_["kept"], wide(O_["norm"]), ALU.mult))
                    nc.vector.sem_inc(gate_ready, 1)
                    dve.wait_ge(j_mm, g * 10 + 10)
                    chain.link(nc.vector.tensor_tensor(xi, xi, J[1][0:S, :].rearrange("q (b d) -> q b d", b=GB), ALU.add))
                    nc.vector.sem_inc(j_dve, 1)
                    for e in range(E):
                        dve.wait_ge(y_mm, g * E + e + 1)
                        for b in range(GB):
                            chain.count(nc.vector.scalar_tensor_tensor(
                                x_in[:, b, :], y_ps[e % 2][0:S, b * D:b * D + D], p["gate"][:, b, e:e + 1], x_in[:, b, :],
                                ALU.mult, ALU.add))
                        chain.wait()
                        nc.vector.sem_inc(y_out, 1)
                    chain.link(nc.vector.scalar_tensor_tensor(x, xi, tanh_g, x, ALU.mult, ALU.add))
                    chain.end()


def build_program(nc, A, out, phases=(1, 2, 3, 4)):
    nc.disable_value_cache = True
    with ExitStack() as ctx:
        sh = setup(nc, ctx, A)
        if 1 in phases:
            cross_attention(nc, ctx, sh, A, 0)
        if 2 in phases:
            cell_ffn(nc, ctx, sh, A)
        if 3 in phases:
            cross_attention(nc, ctx, sh, A, 1)
        if 4 in phases:
            moe_ffn(nc, ctx, sh, A)
        stored = ctx.enter_context(nc.semaphore("stored"))
        with nc.Block() as block:
            @block.sync
            def _(sp):
                sp.dma_start(out.rearrange("b s d -> s b d"), sh.x[:, :, :]).then_inc(stored, 16)
                sp.wait_ge(stored, 16)


def kernel(**inputs):
    import numpy as _np
    import concourse.bacc as _bacc
    from concourse import mybir as _mybir
    from concourse.bass_utils import run_bass_kernel_spmd as _run

    nc = _bacc.Bacc("TRN2", target_bir_lowering=False, num_devices=1)
    arrays, A = {}, {}
    for name, value in inputs.items():
        a = _np.ascontiguousarray(value)
        arrays[f"in_{name}"] = a
        A[name] = nc.dram_tensor(f"in_{name}", a.shape, _mybir.dt.from_np(a.dtype), kind="ExternalInput").ap()
    out = nc.dram_tensor("out_x", (B, S, D), F32, kind="ExternalOutput").ap()
    build_program(nc, A, out)
    r = _run(nc, [arrays], core_ids=[0])
    return r.results[0]["out_x"]
```

```python
from contextlib import ExitStack

import concourse.bass as bass
from concourse import mybir

F32 = mybir.dt.float32
BF16 = mybir.dt.bfloat16
U8 = mybir.dt.uint8
ALU = mybir.AluOpType
ACT = mybir.ActivationFunctionType
AX_X = mybir.AxisListType.X

B, S, D = 32, 100, 128
SK = 1444
P = 128
XH, XD = 16, 8
CH = -(-SK // P)
LASTK = SK - (CH - 1) * P
COLS = [(0, 512), (512, 512), (1024, SK - 1024)]
NEG = -float(2 ** 30)
LN_EPS = 1e-5
L0_LN_EPS = 1e-6


def chunk_keys(c):
    return P if c < CH - 1 else LASTK


def col(ap, shape):
    for _ in range(len(shape) - 2):
        ap = ap.unsqueeze(1)
    return ap.to_broadcast(shape)


class Chain:

    def __init__(self, eng, sem, per, ahead=0):
        self.eng, self.sem, self.per, self.ahead, self.turn, self.k = eng, sem, per, ahead, 0, 0

    def begin(self, turn):
        self.turn, self.k = turn, 0

    def count(self, ins):
        self.k += 1
        ins.then_inc(self.sem, 1)

    def wait(self):
        self.eng.wait_ge(self.sem, self.turn * self.per + self.ahead + self.k)

    def link(self, ins):
        self.count(ins)
        self.wait()

    def end(self):
        assert self.k == self.per, (self.k, self.per)


class Shared:
    pass


class LayerNorm:

    def __init__(self, c, nc, name, rows, minus_half, n):
        def sb(what, shape):
            return c.enter_context(nc.sbuf_tensor(f"{name}_{what}", [rows] + shape, F32))

        self.n = n
        self.stats, self.mv, self.var, self.rstd = sb("stats", [n, 6]), sb("mv", [n, 2]), sb("var", [n]), sb("rstd", [n])
        self.held = sb("held", [1])
        self.minus_half = minus_half[0:rows, :].to_broadcast([rows, n])

    def inverse_root(self, nc):
        return nc.gpsimd.tensor_tensor(self.rstd[:, :], self.var[:, :], self.minus_half, ALU.pow)


def norm_stats(chain, nc, x, ln, eps, var_ready):
    norm_sums(chain, nc, x, ln)
    norm_variance(chain, nc, ln, eps, var_ready)


def norm_sums(chain, nc, x, ln):
    for b in range(ln.n):
        chain.count(nc.vector.bn_stats(ln.stats[:, b, :], x[:, b, :]))


def norm_variance(chain, nc, ln, eps, var_ready):
    chain.wait()
    chain.count(nc.vector.memset(ln.held[:, :], 0.0))
    for b in range(ln.n):
        chain.count(nc.vector.bn_aggr(ln.mv[:, b, :], ln.stats[:, b, :]))
    chain.wait()
    nc.vector.tensor_scalar(ln.var[:, :], ln.mv[:, :, 1], eps, None, ALU.add).then_inc(var_ready, 1)


def setup(nc, ctx, A):
    sh = Shared()

    def sb(name, shape, dt=F32):
        return ctx.enter_context(nc.sbuf_tensor(name, shape, dt))

    sh.x = sb("x_tokens", [S, B, D])
    sh.ident = sb("ident", [P, P])
    sh.ident_bf = sb("ident_bf", [P, P], BF16)
    sh.head16 = sb("head16", [P, 16])
    sh.head8 = sb("head8", [P, 8])
    sh.side = sb("side", [P, 2])
    sh.row_side = sb("row_side", [P, 2])
    sh.minus_half = sb("minus_half", [P, 1])
    sh.tanh_g = sb("tanh_g", [P, 4])
    sh.cross_w = sb("cross_w", [P, 8, P])
    with ExitStack() as c:
        raw = c.enter_context(nc.sbuf_tensor("raw_w", [P, 8, P], F32))
        alternate = c.enter_context(nc.sbuf_tensor("alternate", [P, 2, P // 2], F32))
        g = c.enter_context(nc.sbuf_tensor("g_raw", [P, 4], F32))
        ps = [c.enter_context(nc.psum_tensor(f"ps_w{i}", [P, 4, P], F32)) for i in range(2)]
        sem = {n: ctx.enter_context(nc.semaphore("setup_" + n)) for n in ("loaded", "x_loaded", "ident", "tp", "cp", "g")}
        names = ["L0_xattn_wq", "L0_xattn_wk", "L0_xattn_wv", "L0_xattn_wo", "L1_xattn_Wq", "L1_xattn_Wk", "L1_xattn_Wv", "L1_xattn_Wo"]
        with nc.Block() as block:
            @block.sync
            def _(sp):
                for n, name in enumerate(names):
                    sp.dma_start(raw[:, n, :], A[name]).then_inc(sem["loaded"], 16)
                sp.dma_start(sh.x[:, :, :], A["x"].rearrange("b s d -> s b d")).then_inc(sem["x_loaded"], 16)

            @block.gpsimd
            def _(pool):
                k = 0

                def link(ins):
                    nonlocal k
                    k += 1
                    ins.then_inc(sem["ident"], 1)
                    pool.wait_ge(sem["ident"], k)
                link(pool.memset(sh.ident[:, :], 0.0))
                link(pool.memset(sh.ident_bf[:, :], 0.0))
                link(pool.memset(sh.minus_half[:, :], -0.5))
                link(pool.memset(sh.head16[:, :], 1.0))
                link(pool.memset(sh.head8[:, :], 1.0))
                link(pool.memset(alternate[:, :, :], 0.0))
                for m in (sh.ident, sh.ident_bf):
                    link(pool.affine_select(out=m[:, :], in_=m[:, :], compare_op=ALU.not_equal, fill=1.0, base=0,
                                            pattern=[[-1, P]], channel_multiplier=1))
                link(pool.affine_select(out=alternate[:, :, :], in_=alternate[:, :, :], compare_op=ALU.not_equal,
                                        fill=1.0, base=0, pattern=[[-1, 2], [-2, P // 2]], channel_multiplier=1))
                for m, heads in ((sh.head16, 16), (sh.head8, 8)):
                    size = P // heads
                    link(pool.affine_select(out=m[:, :], in_=m[:, :], compare_op=ALU.is_ge, fill=0.0, base=0,
                                            pattern=[[-size, heads]], channel_multiplier=1))
                    link(pool.affine_select(out=m[:, :], in_=m[:, :], compare_op=ALU.is_ge, fill=0.0, base=size - 1,
                                            pattern=[[size, heads]], channel_multiplier=-1))

            @block.scalar
            def _(act):
                for n, name in enumerate(("g_xattn", "g_ffn")):
                    act.dma_start(g[:, 2 * n:2 * n + 2], A[name].partition_broadcast(P)).then_inc(sem["g"], 16)
                act.wait_ge(sem["g"], 32)
                nc.scalar.activation(sh.tanh_g[:, :], g[:, :], ACT.Tanh).then_inc(sem["g"], 1)
                for i in range(2):
                    act.wait_ge(sem["tp"], i + 1)
                    nc.scalar.copy(sh.cross_w[:, 4 * i:4 * i + 4, :], ps[i][:, :, :]).then_inc(sem["cp"], 1)

            @block.tensor
            def _(pe):
                pe.wait_ge(sem["loaded"], 128)
                pe.wait_ge(sem["ident"], 13)
                for i in range(2):
                    for j in range(4):
                        mm = nc.tensor.transpose(ps[i][:, j, :], raw[:, 4 * i + j, :], sh.ident[:, :])
                    mm.then_inc(sem["tp"], 1)

            @block.vector
            def _(dve):
                dve.wait_ge(sem["x_loaded"], 16)
                dve.wait_ge(sem["cp"], 2)
                dve.wait_ge(sem["g"], 33)
                dve.wait_ge(sem["ident"], 13)
                nc.vector.tensor_reduce(sh.side[:, :], sh.head16[:, :].rearrange("p (a t) -> p t a", t=2), AX_X, ALU.add
                                        ).then_inc(sem["g"], 1)
                nc.vector.tensor_reduce(sh.row_side[:, :], alternate[:, :, :], AX_X, ALU.add).then_inc(sem["g"], 1)
                dve.wait_ge(sem["g"], 35)
    return sh


PRODUCTS = ((0, 0), (0, 1), (1, 0), (0, 2), (2, 0), (1, 1))
PAIR = 2 * XD
PAIRS = XH // 2
SPLIT = len(PRODUCTS) * PAIR
FOLD = SPLIT + 6


def after(eng, sem, value):
    if not isinstance(value, int) or value > 0:
        eng.wait_ge(sem, value)


class Turn:

    def __init__(self, n, third, r):
        self.n, self.third, self.r = n, third, r

    def plus(self, d):
        return Turn(self.n + d, self.third + (self.r + d) // 3, (self.r + d) % 3)


def cross_attention(nc, ctx, sh, A, layer):
    SCALE = float(XD) ** -0.5
    masked = layer == 1
    wqT, wkT, wvT, woT = (sh.cross_w[:, 4 * layer + n, :] for n in range(4))
    tanh_g = sh.tanh_g[0:S, layer:layer + 1]
    MAXES = XH * len(COLS)
    SLOTS = 4 * CH
    MAX_SLOTS = 44
    PREP_SLOTS, EARLY = 30, 42
    PREP = 9
    DVE_MASKS = 2
    MISC = 6
    BODY = (CH - 1) * P

    c = ExitStack()
    with c:
        def sb(name, shape, dt=F32):
            return c.enter_context(nc.sbuf_tensor(f"x{layer}_{name}", shape, dt))

        def dram(name, shape):
            return [nc.dram_tensor(f"x{layer}_{name}{r}", shape, BF16).ap() for r in range(3)]

        def sem(name):
            return ctx.enter_context(nc.semaphore(f"x{layer}_{name}"))

        ctx_raw = sb("ctx_raw", [P, CH, D])
        ctxT = sb("ctxT", [D, SK])
        k_parts = sb("k_parts", [D, 3, SK], BF16)
        k_rest = sb("k_rest", [D, SK])
        k_st = [sb(f"k_st{r}", [P, PAIRS, SK], BF16) for r in range(3)]
        v = [sb(f"v{r}", [P, CH, XH, XD + 1]) for r in range(3)]
        xn, xnT = sb("xn", [S, D]), sb("xnT", [D, S])
        q_parts, q_rest = sb("q_parts", [D, 3, S], BF16), sb("q_rest", [D, S])
        q_par = sb("q_par", [D, 3, 2, S], BF16)
        q_st = [sb(f"q_st{r}", [P, PAIRS, 2 * S], BF16) for r in range(3)]
        max_parts = sb("max_parts", [S, XH, len(COLS)])
        neg_max, rest = sb("neg_max", [S, XH]), sb("rest", [S, 2, XH])
        parts = sb("parts", [S, PAIRS, 3, 2], BF16)
        probs = [sb(f"probs{r}", [P, 4 * S]) for r in range(4)]
        oT = sb("oT", [P, 4 * S])
        rden, o_n, o_nT = sb("rden", [S, XH]), sb("o_n", [S, D]), sb("o_nT", [D, S])
        ln = LayerNorm(c, nc, f"x{layer}_ln", S, sh.minus_half, 1)
        bo = None if masked else sb("bo", [S, D])
        if masked:
            mask_raw = sb("mask_raw", [S, SK], U8)
            mask_q = sb("mask_q", [S, SK], BF16)
            mask_k = sb("mask_k", [P, CH, S], BF16)
            piece_masked = sb("piece_masked", [S, COLS[DVE_MASKS][1]])
        k_dram, q_dram = dram("k_dram", [D, 3, SK]), dram("q_dram", [D, 3, 2 * S])

        def bank(name):
            return c.enter_context(nc.psum_tensor(f"x{layer}_{name}", [P, 512], F32))

        max_ps = [bank(f"max_ps{r}") for r in range(3)]
        exp_ps = [bank(f"exp_ps{r}") for r in range(2)]
        o_ps, prep_ps, misc = bank("o_ps"), bank("prep_ps"), bank("misc")

        ctx_in = sem("ctx_in")
        prep_mm = sem("prep_mm")
        prep_out = sem("prep_out")
        rest_out = sem("rest_out")
        mid_out = sem("mid_out")
        low_out = sem("low_out")
        q_out = sem("q_out")
        max_placed = sem("max_placed")
        k_written = [sem(f"k_written{r}") for r in range(3)]
        q_written = [sem(f"q_written{r}") for r in range(3)]
        k_in = [sem(f"k_in{r}") for r in range(3)]
        q_in = [sem(f"q_in{r}") for r in range(3)]
        max_mm = sem("max_mm")
        mask_added = sem("mask_added")
        max_out = sem("max_out")
        exp_mm = sem("exp_mm")
        exp_out = sem("exp_out")
        pv_mm = sem("pv_mm")
        o_out = sem("o_out")
        xn_out = sem("xn_out")
        bo_added = sem("bo_added")
        parts_out = sem("parts_out")
        pe_misc = sem("pe_misc")
        dve_misc = sem("dve_misc")
        chain_sems = [sem(n) for n in ("norm_chain", "query_chain", "max_chain", "out_chain")]
        var_ready = sem("var_ready")
        rstd_ready = sem("rstd_ready")
        once, first_in = sem("once"), sem("first_in")
        ones_in = sem("ones_in")
        ONCE = 14 if masked else 13
        HEAD = 1 if masked else 0

        class Steps:

            def __init__(self, b):
                n = b.n
                known = isinstance(n, int)
                if known and n < 0:
                    self.k = HEAD + 2
                    return
                self.k = HEAD + 5 + n * MISC - (0 if known and n == 0 else 3)
                if known and n > B - 2:
                    self.k -= 2 * (n - (B - 2))
                if known and n > B - 1:
                    self.k -= (n - (B - 1))

            def next(self):
                self.k = self.k + 1
                return self.k - 1

        def turns(eng, body):
            body(Turn(0, 0, 0))
            with eng.Fori(0, (B - 5) // 3) as i:
                for t in range(3):
                    body(Turn(i * 3 + 1 + t, i + (1 + t) // 3, (1 + t) % 3))
            for n in range(B - 4, B):
                body(Turn(n, n // 3, n % 3))

        FIRST = Turn(-1, -1, 2)

        def runs(b):
            return not isinstance(b.n, int) or b.n >= 0

        def there(b, n):
            return not isinstance(b.n, int) or b.n + n < B

        max_at = [[k for k in range(MAXES)
                   if (k * PREP_SLOTS // EARLY if k < EARLY
                       else PREP_SLOTS + (k - EARLY) * (MAX_SLOTS - PREP_SLOTS) // (MAXES - EARLY)) == s] for s in range(SLOTS)]

        with nc.Block() as block:
            @block.sync
            def _(sp):
                if masked:
                    sp.dma_start(mask_raw[:, :], A["mask_SxS2_bk0"]).then_inc(first_in, 16)
                else:
                    sp.dma_start(bo[:, :], A["L0_xattn_bo"].partition_broadcast(S)).then_inc(first_in, 16)

                def load_ctx(n):
                    sp.dma_start(ctx_raw[:, 0:CH - 1, :], A["ctx_1024"][n, 0:BODY, :].rearrange("(p c) d -> p c d", p=P)
                                 ).then_inc(ctx_in, 16)
                    sp.dma_start(ctx_raw[0:LASTK, CH - 1, :], A["ctx_1024"][n, BODY:SK, :]).then_inc(ctx_in, 16)

                def stack(b, source, through, written, dst, landed, part_of):
                    r = b.r
                    sp.dma_start(through[r], source).then_inc(written[r], 16)
                    sp.wait_ge(written[r], (b.third + 1) * 16)
                    for j, pr in enumerate(PRODUCTS):
                        sp.dma_start(dst[r][PAIR * j:PAIR * j + PAIR, :, :],
                                     through[r][:, pr[part_of], :].rearrange("(p r) n -> r p n", r=PAIR)
                                     ).then_inc(landed[r], 16)

                def stack_q(b):
                    sp.wait_ge(q_out, b.n + 1)
                    after(sp, exp_mm, (b.n - 2) * SLOTS)
                    stack(b, q_par[:, :, :, :].rearrange("d a t q -> d a (t q)"), q_dram, q_written, q_st, q_in, 0)

                def stack_k(b):
                    sp.wait_ge(low_out, (b.n + 1) * 3)
                    stack(b, k_parts[:, :, :], k_dram, k_written, k_st, k_in, 1)

                def turn(b):
                    if there(b, 3):
                        sp.wait_ge(prep_out, (b.n + 2) * PREP + 3)
                        load_ctx(b.n + 3)
                    if there(b, 2):
                        stack_k(b.plus(2))
                        stack_q(b.plus(2))

                load_ctx(0)
                sp.wait_ge(once, ONCE - 1)
                for r in range(3):
                    first = 1 if r == 0 else 0
                    sp.dma_start(k_st[r][SPLIT:FOLD, first:PAIRS, :],
                                 k_st[0][SPLIT:FOLD, 0:1, :].to_broadcast([FOLD - SPLIT, PAIRS - first, SK])
                                 ).then_inc(ones_in, 16)
                sp.wait_ge(prep_out, 3)
                load_ctx(1)
                stack_q(Turn(0, 0, 0))
                stack_k(Turn(0, 0, 0))
                turn(FIRST)
                turns(sp, turn)

            @block.gpsimd
            def _(pool):
                def low(b):
                    for j, (c0, n) in enumerate(COLS):
                        pool.wait_ge(mid_out, b.n * 3 + j + 1)
                        nc.gpsimd.tensor_tensor(k_parts[:, 2, c0:c0 + n], k_rest[:, c0:c0 + n], k_parts[:, 1, c0:c0 + n],
                                                ALU.subtract).then_inc(low_out, 1)

                def root(b):
                    pool.wait_ge(var_ready, b.n + 1)
                    ln.inverse_root(nc).then_inc(rstd_ready, 1)
                    if not masked:
                        pool.wait_ge(xn_out, b.n + 1)
                        nc.gpsimd.tensor_tensor(sh.x[:, b.n, :], sh.x[:, b.n, :], bo[:, :], ALU.add).then_inc(bo_added, 1)

                def turn(b):
                    if there(b, 2):
                        low(b.plus(2))
                        root(b.plus(2))
                root(Turn(0, 0, 0))
                low(Turn(0, 0, 0))
                turn(FIRST)
                turns(pool, turn)

            @block.tensor
            def _(pe):
                pe.sem_inc(pv_mm, 4)

                def prep(b, m):
                    j = m % 3
                    c0, n = COLS[j]
                    if m <= 3 or m >= 7:
                        after(pe, prep_out, b.n * PREP + m)
                    if 4 <= m <= 6:
                        pe.wait_ge(rest_out, b.n * 3 + m - 3)
                    if m == 0:
                        pe.wait_ge(ctx_in, (b.n + 1) * 32)
                    if m < 3:
                        for ch in range(4 * j, 4 * j + 4):
                            k = chunk_keys(ch)
                            mm = nc.tensor.transpose(prep_ps[:, (ch % 4) * P:(ch % 4) * P + k], ctx_raw[0:k, ch, :],
                                                     sh.ident[0:k, 0:k])
                    elif m < 6:
                        mm = nc.tensor.matmul(prep_ps[:, 0:n], wkT, ctxT[:, c0:c0 + n], start=True, stop=True)
                    else:
                        for ch in range(4 * j, 4 * j + 4):
                            k = chunk_keys(ch)
                            mm = nc.tensor.matmul(prep_ps[0:k, (ch % 4) * P:(ch % 4) * P + P],
                                                  ctxT[:, ch * P:ch * P + k], wvT, start=True, stop=True)
                    mm.then_inc(prep_mm, 1)

                def xn_transpose(b, step):
                    after(pe, dve_misc, step)
                    pe.wait_ge(xn_out, b.n + 1)
                    nc.tensor.transpose(misc[:, 0:S], xn[:, :], sh.ident[0:S, 0:S]).then_inc(pe_misc, 1)

                def q_product(b, step):
                    pe.wait_ge(dve_misc, step)
                    nc.tensor.matmul(misc[:, 0:S], wqT, xnT[:, :], start=True, stop=True).then_inc(pe_misc, 1)

                def max_piece(b, i):
                    h, j = i // len(COLS), i % len(COLS)
                    c0, n = COLS[j]
                    if i == 0:
                        pe.wait_ge(k_in[b.r], (b.third + 1) * 96)
                        pe.wait_ge(q_in[b.r], (b.third + 1) * 96)
                    after(pe, max_out, b.n * MAXES + i - 2)
                    out = max_ps[i % 3][0:S, 0:n]
                    adds_mask = masked and j != DVE_MASKS
                    if adds_mask:
                        nc.tensor.matmul(out, sh.ident_bf[0:S, 0:S], mask_q[:, c0:c0 + n], start=True, stop=False)
                    nc.tensor.matmul(out, q_st[b.r][0:SPLIT, h // 2, (h % 2) * S:(h % 2) * S + S],
                                     k_st[b.r][0:SPLIT, h // 2, c0:c0 + n], start=not adds_mask, stop=True).then_inc(max_mm, 1)

                def turn_parts(b, step):
                    pe.wait_ge(parts_out, b.n + 1)
                    pe.wait_ge(dve_misc, step)
                    pe.wait_ge(prep_out, (b.n + 2) * PREP if there(b, 1) else B * PREP)
                    for pair in range(PAIRS):
                        bank, place = (misc, prep_ps)[pair // 4], pair % 4 * S
                        mm = nc.tensor.matmul(bank[SPLIT:FOLD, place:place + S], parts[:, pair, :, :].rearrange("q a t -> q (a t)"),
                                              sh.ident_bf[0:S, 0:S], start=True, stop=True)
                    mm.then_inc(pe_misc, 1)

                def exp_piece(b, i):
                    ch, k = i // 4, chunk_keys(i // 4)
                    if i == 0:
                        pe.wait_ge(max_placed, (b.n + 1) * 2)
                    after(pe, exp_out, b.n * SLOTS + i - 1)
                    out = exp_ps[i % 2][0:k, 0:4 * S]
                    if masked:
                        nc.tensor.matmul(out.rearrange("k (h q) -> k h q", h=4), sh.ident_bf[:, 0:k],
                                         mask_k[:, ch, :].unsqueeze(1).to_broadcast([P, 4, S]),
                                         start=True, stop=False, skip_group_check=True)
                    for t in range(2):
                        pair = 2 * (i % 4) + t
                        mm = nc.tensor.matmul(out[:, t * 2 * S:(t + 1) * 2 * S], k_st[b.r][0:FOLD, pair, ch * P:ch * P + k],
                                              q_st[b.r][0:FOLD, pair, :], start=not masked and t == 0, stop=True,
                                              skip_group_check=True)
                    mm.then_inc(exp_mm, 1)

                def values(b, i):
                    ch = i // 4
                    pe.wait_ge(exp_out, b.n * SLOTS + i + 1)
                    if i == 0:
                        after(pe, o_out, b.n)
                    for t in range(2):
                        pair = 2 * (i % 4) + t
                        tile, half = pair % 4, pair // 4
                        mm = nc.tensor.matmul(o_ps[32 * tile:32 * tile + 2 * (XD + 1), half * 2 * S:(half + 1) * 2 * S],
                                              v[b.r][:, ch, 2 * pair:2 * pair + 2, :].rearrange("k h d -> k (h d)"),
                                              probs[i % 4][:, t * 2 * S:(t + 1) * 2 * S], start=(ch == 0 and half == 0),
                                              stop=(ch == CH - 1), skip_group_check=True)
                    mm.then_inc(pv_mm, 1)

                def out_transpose(b, step):
                    pe.wait_ge(dve_misc, step)
                    pe.wait_ge(o_out, b.n + 1)
                    for t in range(4):
                        mm = nc.tensor.transpose(misc[0:S, t * P:t * P + P], oT[:, t * S:t * S + S], sh.ident[:, :])
                    mm.then_inc(pe_misc, 1)

                def out_back(step):
                    pe.wait_ge(dve_misc, step)
                    nc.tensor.transpose(misc[:, 0:S], o_n[:, :], sh.ident[0:S, 0:S]).then_inc(pe_misc, 1)

                def out_product(step):
                    pe.wait_ge(dve_misc, step)
                    nc.tensor.matmul(misc[0:S, 0:D], o_nT[:, :], woT, start=True, stop=True).then_inc(pe_misc, 1)

                def turn(b):
                    steps = Steps(b)
                    for s in range(SLOTS):
                        if runs(b):
                            exp_piece(b, s)
                            if s >= 2:
                                values(b, s - 2)
                        if there(b, 1):
                            for k in max_at[s]:
                                max_piece(b.plus(1), k)
                        if not isinstance(b.n, int) or b.n > 0:
                            if s == 3:
                                out_transpose(b.plus(-1), steps.next())
                            if s == 6:
                                out_back(steps.next())
                            if s == 9:
                                out_product(steps.next())
                        if there(b, 2):
                            if s % 3 == 0 and s < 3 * PREP:
                                prep(b.plus(2), s // 3)
                            if s == 22:
                                xn_transpose(b.plus(2), steps.next())
                            if s == 25:
                                q_product(b.plus(2), steps.next())
                        if there(b, 1) and s == MAX_SLOTS + 3:
                            turn_parts(b.plus(1), steps.next())
                    if runs(b):
                        values(b, SLOTS - 2)
                        values(b, SLOTS - 1)

                if masked:
                    pe.wait_ge(once, ONCE)
                    whole, side = misc[:, :].bitcast(BF16), prep_ps[:, :].bitcast(BF16)
                    for ch in range(CH):
                        k = chunk_keys(ch)
                        dst = whole[0:k, ch * S:ch * S + S] if ch < 10 else side[0:k, (ch - 10) * S:(ch - 10) * S + S]
                        mm = nc.tensor.transpose(dst, mask_q[:, ch * P:ch * P + k], sh.ident_bf[0:S, 0:S])
                    mm.then_inc(pe_misc, 1)
                    pe.wait_ge(dve_misc, 1)
                b = Turn(0, 0, 0)
                xn_transpose(b, HEAD)
                q_product(b, HEAD + 1)
                for m in range(PREP):
                    prep(b, m)
                turn(FIRST)
                pe.wait_ge(once, ONCE)
                pe.wait_ge(ones_in, 48)
                turns(pe, turn)
                steps = Steps(Turn(B, 0, 0))
                out_transpose(Turn(B - 1, 0, 0), steps.next())
                out_back(steps.next())
                out_product(steps.next())

            @block.scalar
            def _(act):
                def prep(b, m):
                    j = m % 3
                    c0, n = COLS[j]
                    act.wait_ge(prep_mm, b.n * PREP + m + 1)
                    if m < 3:
                        ins = nc.scalar.copy(ctxT[:, c0:c0 + n], prep_ps[:, 0:n])
                    elif m < 6:
                        if m == 3 and (not isinstance(b.n, int) or b.n > 0):
                            before = b.plus(-1)
                            act.wait_ge(k_written[before.r], (before.third + 1) * 16)
                        ins = nc.scalar.copy(k_parts[:, 0, c0:c0 + n], prep_ps[:, 0:n])
                    else:
                        if m == 6:
                            after(act, pv_mm, (b.n - 2) * SLOTS + 4 if not isinstance(b.n, int) or b.n > 2 else 0)
                        chunks = 4 if j < 2 else 3
                        ins = nc.scalar.copy(v[b.r][:, 4 * j:4 * j + chunks, :, 0:XD].rearrange("k c h d -> k (c h) d"),
                                             prep_ps[:, 0:chunks * P].rearrange("k (c d) -> k c d", d=XD))
                        if chunks < 4:
                            ins = nc.scalar.copy(v[b.r][0:LASTK, CH - 1, :, 0:XD],
                                                 prep_ps[0:LASTK, chunks * P:4 * P].rearrange("k (h d) -> k h d", d=XD))
                    ins.then_inc(prep_out, 1)

                def middle(b, j):
                    c0, n = COLS[j]
                    act.wait_ge(rest_out, b.n * 3 + j + 1)
                    nc.scalar.copy(k_parts[:, 1, c0:c0 + n], k_rest[:, c0:c0 + n]).then_inc(mid_out, 1)

                def place_max(b, step):
                    act.wait_ge(pe_misc, step + 1)
                    for t in range(2):
                        ins = nc.scalar.mul(q_st[b.r][SPLIT:FOLD, 4:8, t * S:t * S + S],
                                            prep_ps[SPLIT:FOLD, 0:4 * S].rearrange("a (p q) -> a p q", p=4),
                                            sh.row_side[SPLIT:FOLD, t:t + 1])
                    ins.then_inc(max_placed, 1)

                def exponentials(b, i):
                    k = chunk_keys(i // 4)
                    act.wait_ge(pv_mm, b.n * SLOTS + i + 1)
                    act.wait_ge(exp_mm, b.n * SLOTS + i + 1)
                    nc.scalar.activation(probs[i % 4][0:k, :], exp_ps[i % 2][0:k, 0:4 * S], ACT.Exp, scale=SCALE
                                         ).then_inc(exp_out, 1)

                def turn(b):
                    place_step = Steps(b).k + (3 if not isinstance(b.n, int) or b.n > 0 else 0) + (2 if there(b, 2) else 0)
                    for s in range(SLOTS):
                        if runs(b):
                            exponentials(b, s)
                        if there(b, 1) and s == MAX_SLOTS + 3:
                            place_max(b.plus(1), place_step)
                        if there(b, 2):
                            if s % 3 == 0 and s < 3 * PREP:
                                prep(b.plus(2), s // 3)
                            if s in (11, 14, 17):
                                middle(b.plus(2), (s - 11) // 3)

                act.wait_ge(once, ONCE)
                for m in range(PREP):
                    prep(Turn(0, 0, 0), m)
                    if 4 <= m <= 6:
                        middle(Turn(0, 0, 0), m - 4)
                turn(FIRST)
                turns(act, turn)

            @block.vector
            def _(dve):
                nc.vector.memset(o_ps[:, :], 0.0).then_inc(once, 1)
                nc.vector.memset(misc[:, :], 0.0).then_inc(once, 1)
                for r in range(3):
                    nc.vector.memset(v[r][:, 0:CH - 1, :, XD:XD + 1], 1.0).then_inc(once, 1)
                    nc.vector.memset(v[r][:, CH - 1, :, :], 0.0).then_inc(once, 1)
                if masked:
                    nc.vector.memset(mask_k[:, CH - 1, :], 0.0).then_inc(once, 1)
                    dve.wait_ge(once, 9)
                else:
                    dve.wait_ge(once, 8)
                for r in range(3):
                    nc.vector.memset(v[r][0:LASTK, CH - 1, :, XD:XD + 1], 1.0).then_inc(once, 1)
                nc.vector.memset(k_st[0][SPLIT:FOLD, 0:1, :], 1.0).then_inc(once, 1)
                dve.wait_ge(first_in, 16)
                if masked:
                    nc.vector.tensor_scalar(mask_q[:, 0:BODY].rearrange("q (c p) -> q c p", p=P),
                                            mask_raw[:, 0:BODY].rearrange("q (p c) -> q c p", p=P),
                                            0.0, NEG, ALU.is_equal, ALU.mult)
                    nc.vector.tensor_scalar(mask_q[:, BODY:SK], mask_raw[:, BODY:SK], 0.0, NEG, ALU.is_equal, ALU.mult
                                            ).then_inc(once, 1)
                    dve.wait_ge(pe_misc, 1)
                    nc.vector.tensor_copy(mask_k[:, 0:10, :].rearrange("k c q -> k (c q)"), misc[:, :].bitcast(BF16)[:, 0:10 * S])
                    side = prep_ps[:, :].bitcast(BF16)
                    nc.vector.tensor_copy(mask_k[:, 10, :], side[:, 0:S])
                    nc.vector.tensor_copy(mask_k[0:LASTK, 11, :], side[0:LASTK, S:2 * S]).then_inc(dve_misc, 1)
                else:
                    nc.vector.tensor_scalar(bo[:, :], bo[:, :], tanh_g, None, ALU.mult).then_inc(once, 1)
                dve.wait_ge(once, ONCE)

                chains = {n: Chain(dve, c_sem, per) for n, (c_sem, per) in
                          dict(norm=(chain_sems[0], 4), query=(chain_sems[1], 4), top=(chain_sems[2], 7),
                               out=(chain_sems[3], 3)).items()}

                def maximum(b, i):
                    h, j = i // len(COLS), i % len(COLS)
                    dve.wait_ge(max_mm, b.n * MAXES + i + 1)
                    c0, n = COLS[j]
                    piece = max_ps[i % 3][0:S, 0:n]
                    if masked and j == DVE_MASKS:
                        nc.vector.tensor_tensor(piece_masked[:, 0:n], piece, mask_q[:, c0:c0 + n], ALU.add).then_inc(mask_added, 1)
                        dve.wait_ge(mask_added, b.n * XH + h + 1)
                        piece = piece_masked[:, 0:n]
                    nc.vector.tensor_reduce(max_parts[:, h, j:j + 1], piece, AX_X, ALU.max).then_inc(max_out, 1)

                def split_max(b):
                    chain = chains["top"]
                    chain.begin(b.n)
                    dve.wait_ge(max_out, (b.n + 1) * MAXES)
                    chain.link(nc.vector.tensor_reduce(neg_max[:, :], max_parts[:, :, :], AX_X, ALU.max))
                    chain.link(nc.vector.tensor_scalar(neg_max[:, :], neg_max[:, :], NEG / 2, -1.0, ALU.max, ALU.mult))

                    def by_pairs(ap):
                        return ap.rearrange("q (p t) -> q p t", t=2)
                    chain.link(nc.vector.tensor_copy(parts[:, :, 0, :], by_pairs(neg_max[:, :])))
                    chain.link(nc.vector.tensor_tensor(by_pairs(rest[:, 0, :]), by_pairs(neg_max[:, :]), parts[:, :, 0, :], ALU.subtract))
                    chain.link(nc.vector.tensor_copy(parts[:, :, 1, :], by_pairs(rest[:, 0, :])))
                    chain.link(nc.vector.tensor_tensor(by_pairs(rest[:, 1, :]), by_pairs(rest[:, 0, :]), parts[:, :, 1, :], ALU.subtract))
                    chain.link(nc.vector.tensor_copy(parts[:, :, 2, :], by_pairs(rest[:, 1, :])))
                    nc.vector.sem_inc(parts_out, 1)
                    chain.end()

                def place_max(b, step):
                    dve.wait_ge(pe_misc, step + 1)
                    shape = [FOLD - SPLIT, 4, 2, S]
                    nc.vector.tensor_tensor(q_st[b.r][SPLIT:FOLD, 0:4, :].rearrange("a p (t q) -> a p t q", t=2),
                                            misc[SPLIT:FOLD, 0:4 * S].rearrange("a (p q) -> a p q", p=4).unsqueeze(2).to_broadcast(shape),
                                            sh.row_side[SPLIT:FOLD, :].unsqueeze(1).unsqueeze(3).to_broadcast(shape), ALU.mult
                                            ).then_inc(dve_misc, 1)
                    dve.wait_ge(dve_misc, step + 1)
                    nc.vector.sem_inc(max_placed, 1)

                def norm_begin(b):
                    chains["norm"].begin(b.n)
                    norm_stats(chains["norm"], nc, sh.x[:, bass.ds(b.n, 1), :], ln, LN_EPS, var_ready)

                def norm_end(b):
                    dve.wait_ge(rstd_ready, b.n + 1)
                    chains["norm"].link(nc.vector.tensor_scalar(xn[:, :], sh.x[:, b.n, :], ln.mv[:, 0, 0:1], ln.rstd[:, 0:1],
                                                                ALU.subtract, ALU.mult))
                    nc.vector.sem_inc(xn_out, 1)
                    chains["norm"].end()

                def copy_xnT(step):
                    dve.wait_ge(pe_misc, step + 1)
                    nc.vector.tensor_copy(xnT[:, :], misc[:, 0:S]).then_inc(dve_misc, 1)

                def split_q(b, step):
                    chain = chains["query"]
                    chain.begin(b.n)
                    dve.wait_ge(pe_misc, step + 1)
                    chain.link(nc.vector.tensor_copy(q_parts[:, 0, :], misc[:, 0:S]))
                    nc.vector.tensor_tensor(q_rest[:, :], misc[:, 0:S], q_parts[:, 0, :], ALU.subtract).then_inc(dve_misc, 1)

                def split_q_rest(b, step):
                    chain = chains["query"]
                    dve.wait_ge(dve_misc, step + 1)
                    chain.link(nc.vector.tensor_copy(q_parts[:, 1, :], q_rest[:, :]))
                    chain.count(nc.vector.tensor_tensor(q_parts[:, 2, :], q_rest[:, :], q_parts[:, 1, :], ALU.subtract))

                def split_q_place(b):
                    chain = chains["query"]
                    chain.wait()
                    if not isinstance(b.n, int) or b.n > 0:
                        before = b.plus(-1)
                        dve.wait_ge(q_written[before.r], (before.third + 1) * 16)
                    chain.link(nc.vector.tensor_tensor(q_par[:, :, :, :], q_parts[:, :, :].unsqueeze(2).to_broadcast([D, 3, 2, S]),
                                                       sh.side[:, :].unsqueeze(1).unsqueeze(3).to_broadcast([D, 3, 2, S]), ALU.mult))
                    nc.vector.sem_inc(q_out, 1)
                    chain.end()

                def k_less_high(b, j):
                    c0, n = COLS[j]
                    dve.wait_ge(prep_out, b.n * PREP + 3 + j + 1)
                    after(dve, low_out, b.n * 3)
                    nc.vector.tensor_tensor(k_rest[:, c0:c0 + n], prep_ps[:, 0:n], k_parts[:, 0, c0:c0 + n], ALU.subtract
                                            ).then_inc(rest_out, 1)

                def out_sums(b):
                    dve.wait_ge(pv_mm, (b.n + 1) * SLOTS + 4)
                    nc.vector.tensor_copy(oT[:, :], o_ps[:, 0:4 * S]).then_inc(o_out, 1)

                def out_divide(b, step):
                    chain = chains["out"]
                    chain.begin(b.n)
                    dve.wait_ge(pe_misc, step + 1)
                    m = misc[0:S, :].rearrange("q (a t j d) -> q a t j d", a=2, t=2, j=4)
                    r = rden[:, :].rearrange("q (a j t) -> q a t j", a=2, t=2)
                    o = o_n[:, :].rearrange("q (a j t d) -> q a t j d", a=2, t=2, d=XD)
                    for t in range(2):
                        chain.count(nc.vector.tensor_scalar(r[:, :, t, :], m[:, :, t, :, t * (XD + 1) + XD], 1e-9, None, ALU.max))
                    chain.wait()
                    chain.link(nc.vector.reciprocal(rden[:, :], rden[:, :]))
                    for t in range(2):
                        ins = nc.vector.tensor_tensor(o[:, :, t, :, :], m[:, :, t, :, t * (XD + 1):t * (XD + 1) + XD],
                                                      r[:, :, t, :].unsqueeze(3).to_broadcast([S, 2, 4, XD]), ALU.mult)
                    ins.then_inc(dve_misc, 1)

                def out_copy(step):
                    dve.wait_ge(pe_misc, step + 1)
                    nc.vector.tensor_copy(o_nT[:, :], misc[:, 0:S]).then_inc(dve_misc, 1)

                def out_add(b, step):
                    dve.wait_ge(pe_misc, step + 1)
                    if not masked:
                        dve.wait_ge(bo_added, b.n + 1)
                    ins = nc.vector.scalar_tensor_tensor(sh.x[:, b.n, :], misc[0:S, 0:D], tanh_g, sh.x[:, b.n, :],
                                                         ALU.mult, ALU.add)
                    ins.then_inc(dve_misc, 1)
                    chains["out"].end()

                def turn(b):
                    steps = Steps(b)
                    first, second, third = steps.k, steps.k + 1, steps.k + 2
                    ended = not isinstance(b.n, int) or b.n > 0
                    if ended:
                        out_sums(b.plus(-1))
                        steps.k = steps.k + 3
                    for s in range(SLOTS):
                        if there(b, 1):
                            for k in max_at[s]:
                                maximum(b.plus(1), k)
                        if ended:
                            if s == 4:
                                out_divide(b.plus(-1), first)
                            if s == 7:
                                out_copy(second)
                            if s == 10:
                                out_add(b.plus(-1), third)
                        if there(b, 2):
                            if s in (10, 13, 16):
                                k_less_high(b.plus(2), (s - 10) // 3)
                            if s == 18:
                                norm_begin(b.plus(2))
                            if s == 20:
                                norm_end(b.plus(2))
                            if s == 23:
                                copy_xnT(steps.next())
                            if s == 26:
                                q_step = steps.next()
                                split_q(b.plus(2), q_step)
                            if s == 27:
                                split_q_rest(b.plus(2), q_step)
                            if s == 28:
                                split_q_place(b.plus(2))
                        if there(b, 1) and s == MAX_SLOTS:
                            split_max(b.plus(1))
                        if there(b, 1) and s == MAX_SLOTS + 3:
                            place_max(b.plus(1), steps.next())

                b = Turn(0, 0, 0)
                norm_begin(b)
                norm_end(b)
                copy_xnT(HEAD)
                split_q(b, HEAD + 1)
                split_q_rest(b, HEAD + 1)
                split_q_place(b)
                for j in range(3):
                    k_less_high(b, j)
                turn(FIRST)
                turns(dve, turn)
                last = Turn(B - 1, 0, 0)
                steps = Steps(Turn(B, 0, 0))
                out_sums(last)
                out_divide(last, steps.next())
                out_copy(steps.next())
                out_add(last, steps.next())


GB = 4
GT = GB * S
GROUPS = B // GB
UH = 4


def ffn0_edges():
    nodes, first = [], 0
    for c in range(6):
        n = min(c + 1, 5)
        source = c - n
        nodes.append(((c - 1, source, source + n // 2), (first + n - 1, first, first + n // 2)))
        first += n
    return nodes


class At:

    def __init__(self, n, pair, k):
        self.n, self.pair, self.k = n, pair, k
        self.node, self.slot = k // 2, k % 2
        self.group = pair * 2 + self.slot

    def plus(self, d):
        return At(self.n + d, self.pair + (self.k + d) // 12, (self.k + d) % 12)


def cell_ffn(nc, ctx, sh, A):
    NODES = ffn0_edges()
    NN = len(NODES)
    HEADS, SIZE = 8, D // 8
    SCALE = float(SIZE) ** -0.5
    UNITS = 2 * GB
    TOTAL = GROUPS * NN
    tanh_g = sh.tanh_g[0:S, 2:3]
    FIRST0, NEXT0 = ("tokens", "Wo", "query", "Wq"), ("Wo", "query", "Wq")
    FIRST1, NEXT1 = ("key", "Wk", "last", "value", "Wv"), ("key", "Wk", "value", "Wv")

    def count(a, what, first, later):
        if isinstance(a.n, int) and a.n >= TOTAL:
            return (GROUPS // 2) * (2 * len(first) + 10 * len(later)) + a.n - TOTAL
        names = first if a.k < 2 else later
        ahead = a.k * len(first) if a.k < 2 else 2 * len(first) + (a.k - 2) * len(later)
        return a.pair * (2 * len(first) + 10 * len(later)) + ahead + names.index(what)

    def count0(a, what):
        return count(a, what, FIRST0, NEXT0)

    def count1(a, what):
        return count(a, what, FIRST1, NEXT1)

    def known(a):
        return isinstance(a.n, int)

    def prepares(a):
        return not known(a) or a.n < TOTAL

    def finishes(a):
        return not known(a) or a.n >= 2

    c = ExitStack()
    with c:
        def sb(name, shape, dt=F32):
            return c.enter_context(nc.sbuf_tensor(f"cell_{name}", shape, dt))

        def sem(name):
            return ctx.enter_context(nc.semaphore(f"cell_{name}"))

        def ps(name):
            return c.enter_context(nc.psum_tensor(f"cell_{name}", [P, 512], F32))

        def two(name, shape):
            return [sb(f"{name}{r}", shape) for r in range(2)]

        we = sb("we", [D, 20, D])
        w = {n: sb(n, [D, NN, D]) for n in ("Wq", "Wk", "Wv")}
        wo = sb("Wo", [P, NN, 2, D])
        ew = sb("ew", [P, NN * 3])
        act_w = sb("act_w", [P, NN])
        be = sb("be", [P, NN * 3])
        gain, shift = sb("gain", [S, D]), sb("shift", [S, D])
        z, last, y = sb("z", [S, GB, D]), sb("last", [S, GB, D]), sb("y", [S, GB, D])
        nodes = [two(f"node{n}_", [D, GT]) for n in range(NN + 1)]
        qinT, kinT, vinT, qT = two("qinT", [D, GT]), two("kinT", [D, GT]), two("vinT", [D, GT]), two("qT", [D, GT])
        k_bd = two("k_bd", [D, GB, HEADS, S])
        kT = sb("kT", [D, GT])
        v = two("v", [S, GB, D])
        top, neg_top = two("top", [S, UH]), two("neg_top", [S, UH])
        probs = [sb(f"probs{r}", [S, UH, S]) for r in range(4)]
        sums = [sb(f"sums{r}", [S, UH]) for r in range(4)]
        probsT = two("probsT", [S, UH, S])
        oT = two("oT", [P, GT])
        ln_in, ln_out = (LayerNorm(c, nc, f"cell_ln_{n}", S, sh.minus_half, GB) for n in ("in", "out"))
        J, s_ps, t_ps, o_ps = ([ps(f"{n}{r}") for r in range(2)] for n in ("J", "s_ps", "t_ps", "o_ps"))

        loaded, ready = sem("loaded"), sem("ready")
        mm = [sem("J0_mm"), sem("J1_mm")]
        out = [sem("J0_out"), sem("J1_out")]
        k_ready = sem("k_ready")
        z_ready = sem("z_ready")
        in_var, in_rstd = sem("in_var"), sem("in_rstd")
        out_var, out_rstd = sem("out_var"), sem("out_rstd")
        in_chain, out_chain = sem("in_chain"), sem("out_chain")
        s_mm = sem("s_mm")
        raw_top = sem("raw_top")
        top_done = sem("top_done")
        exp_done = sem("exp_done")
        sum_done = sem("sum_done")
        r_done = sem("r_done")
        norm_done = sem("norm_done")
        t_mm = sem("t_mm")
        t_out = sem("t_out")
        v_mm = sem("v_mm")
        o_out = [sem("o_out0"), sem("o_out1")]
        LOADS = 16 * (4 + 8 + 2 + 18 + 2)
        READY = 6
        OUT_STEPS = 3 * GB + 4

        def attentions(eng, step):
            for n in range(2):
                for i in range(UNITS):
                    step(At(n, 0, n), i)
            with eng.Fori(0, GROUPS // 2 - 1) as pair:
                for t in range(2, 14):
                    for i in range(UNITS):
                        step(At(pair * 12 + t, pair + t // 12, t % 12), i)
            for n in range(TOTAL - 10, TOTAL + 1):
                for i in range(UNITS):
                    step(At(n, n // 12, n % 12), i)

        def unit(a, i, back):
            d, j = (i - back) // UNITS, (i - back) % UNITS
            u = a.plus(d)
            if known(u) and not 0 <= u.n < TOTAL:
                return None
            return u, j, u.n * UNITS + j

        with nc.Block() as block:
            @block.sync
            def _(sp):
                sp.dma_start(we[:, :, :], A["L0_ffn_We"].rearrange("e i o -> i e o")).then_inc(loaded, 16)
                for n in w:
                    sp.dma_start(w[n][:, :, :], A["L0_ffn_" + n].rearrange("c i o -> i c o")).then_inc(loaded, 16)
                sp.dma_start(ew[:, :], A["L0_ffn_ew"].rearrange("c k -> (c k)").partition_broadcast(P)).then_inc(loaded, 16)
                sp.dma_start(act_w[:, :], A["L0_ffn_act_w"].partition_broadcast(P)).then_inc(loaded, 16)
                for n, (_, edges) in enumerate(NODES):
                    for k, e in enumerate(edges):
                        sp.dma_start(be[:, 3 * n + k:3 * n + k + 1], A["L0_ffn_be"][e, :].unsqueeze(1)).then_inc(loaded, 16)
                sp.dma_start(gain[:, :], A["L0_ffn_ln_g"].partition_broadcast(S)).then_inc(loaded, 16)
                sp.dma_start(shift[:, :], A["L0_ffn_ln_b"].partition_broadcast(S)).then_inc(loaded, 16)
                sp.wait_ge(ready, 1)
                for h in range(HEADS):
                    sp.dma_start(wo[32 * (h % 4):32 * (h % 4) + SIZE, :, h // 4, :],
                                 A["L0_ffn_Wo"][:, h * SIZE:(h + 1) * SIZE, :].rearrange("c i o -> i c o")).then_inc(loaded, 16)

            @block.gpsimd
            def _(pool):
                def root_in(g):
                    pool.wait_ge(in_var, g + 1)
                    ln_in.inverse_root(nc).then_inc(in_rstd, 1)

                def weigh(a, i, u):
                    pool.wait_ge(r_done, u + 1)
                    nc.gpsimd.tensor_tensor(probs[i % 4][:, :, :], probs[i % 4][:, :, :],
                                            sums[i % 4][:, :].unsqueeze(2).to_broadcast([S, UH, S]), ALU.mult).then_inc(norm_done, 1)

                def stage(a, s):
                    following, before = a.plus(1), a.plus(-1)
                    if prepares(a) and 2 <= s < 2 + GB:
                        b = s - 2
                        if b == 0:
                            pool.wait_ge(out[1], count1(a, "Wk") + 1)
                        ins = nc.gpsimd.tensor_tensor(k_bd[a.slot][:, b, :, :],
                                                      kT[:, b * S:b * S + S].unsqueeze(1).to_broadcast([D, HEADS, S]),
                                                      sh.head8[:, :].unsqueeze(2).to_broadcast([D, HEADS, S]), ALU.mult)
                        if b == GB - 1:
                            ins.then_inc(k_ready, 1)
                    if s == 6 and following.k < 2 and prepares(following):
                        root_in(following.group)
                    if s == 1 and before.k < 2 and finishes(before):
                        root_out(before.group - 2)

                def step(a, i):
                    weighed = unit(a, i, 1)
                    if weighed:
                        weigh(*weighed)
                    stage(a.plus(1), i)

                def root_out(g):
                    pool.wait_ge(out_var, g + 1)
                    ln_out.inverse_root(nc).then_inc(out_rstd, 1)

                root_in(0)
                for s in range(UNITS):
                    stage(At(0, 0, 0), s)
                attentions(pool, step)
                root_out(GROUPS - 1)

            @block.tensor
            def _(pe):
                def product(a, bank, what, rhs_of):
                    at = (count0, count1)[bank](a, what)
                    after(pe, out[bank], at)
                    rhs_of(J[bank]).then_inc(mm[bank], 1)

                def wide(lhsT, rhs):
                    return lambda bank: nc.tensor.matmul(bank[:, 0:GT], lhsT, rhs, start=True, stop=True)

                def stage(a, s):
                    g, n = a.slot, a.node
                    (sq, sk, sv), (eq, ek, ev) = NODES[n]
                    if prepares(a):
                        if s == 0 and a.k < 2:
                            pe.wait_ge(z_ready, a.group + 1)

                            def turn_tokens(bank):
                                for b in range(GB):
                                    ins = nc.tensor.transpose(bank[:, b * S:b * S + S], z[:, b, :], sh.ident[0:S, 0:S])
                                return ins
                            product(a, 0, "tokens", turn_tokens)
                        if s == 1:
                            if a.k < 2:
                                pe.wait_ge(out[0], count0(a, "tokens") + 1)
                            product(a, 1, "key", wide(we[:, ek, :], nodes[sk + 1][g][:, :]))
                        if s == 2:
                            product(a, 1, "Wk", wide(w["Wk"][:, n, :], kinT[g][:, :]))
                    if s == 4:
                        if finishes(a):
                            before = a.plus(-2)
                            for half in range(2):
                                pe.wait_ge(o_out[half], before.n + 1)
                            after(pe, out[0], count0(a, "Wo"))
                            for half in range(2):
                                ins = nc.tensor.matmul(J[0][:, 0:GT], wo[:, before.node, half, :], oT[half][:, :],
                                                       start=(half == 0), stop=(half == 1))
                            ins.then_inc(mm[0], 1)
                        else:
                            pe.wait_ge(out[0], count0(a, "Wo"))
                            pe.sem_inc(mm[0], 1)
                    if prepares(a):
                        if s == 5:
                            product(a, 0, "query", wide(we[:, eq, :], nodes[sq + 1][g][:, :]))
                        if s == 6:
                            product(a, 0, "Wq", wide(w["Wq"][:, n, :], qinT[g][:, :]))
                    if s == 6 and a.k < 2:
                        if finishes(a):
                            if not prepares(a):
                                pe.wait_ge(out[0], count0(a, "Wo") + 1)

                            def turn_last(bank):
                                for b in range(GB):
                                    ins = nc.tensor.transpose(bank[0:S, b * D:b * D + D], nodes[NN][g][:, b * S:b * S + S],
                                                              sh.ident[:, :])
                                return ins
                            product(a, 1, "last", turn_last)
                        else:
                            pe.wait_ge(out[1], count1(a, "last"))
                            pe.sem_inc(mm[1], 1)
                    if s == 6 and prepares(a):
                        product(a, 1, "value", wide(we[:, ev, :], nodes[sv + 1][g][:, :]))
                    if s == 7 and prepares(a):
                        def values(bank):
                            for b in range(GB):
                                ins = nc.tensor.matmul(bank[0:S, b * D:b * D + D], vinT[g][:, b * S:b * S + S],
                                                       w["Wv"][:, n, :], start=True, stop=True)
                            return ins
                        product(a, 1, "Wv", values)

                def scores(a, i, u):
                    half, b, g = i // GB, i % GB, a.slot
                    if i == 0:
                        pe.wait_ge(out[0], count0(a, "Wq") + 1)
                        pe.wait_ge(k_ready, a.n + 1)
                    after(pe, exp_done, u - 1)
                    nc.tensor.matmul(s_ps[i % 2][0:S, 0:UH * S], qT[g][:, b * S:b * S + S],
                                     k_bd[g][:, b, UH * half:UH * half + UH, :].rearrange("d h k -> d (h k)"),
                                     start=True, stop=True).then_inc(s_mm, 1)

                def transposes(a, i, u):
                    pe.wait_ge(norm_done, u + 1)
                    after(pe, t_out, u - 1)
                    for h in range(UH):
                        ins = nc.tensor.transpose(t_ps[i % 2][0:S, h * S:h * S + S], probs[i % 4][:, h, :], sh.ident[0:S, 0:S])
                    ins.then_inc(t_mm, 1)

                def outputs(a, i, u):
                    half, b, g = i // GB, i % GB, a.slot
                    if i == 0:
                        pe.wait_ge(out[1], count1(a, "Wv") + 1)
                    if b == 0:
                        after(pe, o_out[half], a.n)
                    pe.wait_ge(t_out, u + 1)
                    for h in range(UH):
                        d0 = (UH * half + h) * SIZE
                        ins = nc.tensor.matmul(o_ps[half][32 * h:32 * h + SIZE, b * S:b * S + S], v[g][:, b, d0:d0 + SIZE],
                                               probsT[i % 2][:, h, :], start=True, stop=True, skip_group_check=True)
                    ins.then_inc(v_mm, 1)

                def step(a, i):
                    now, turned, used = unit(a, i, 0), unit(a, i, 3), unit(a, i, 4)
                    if now:
                        scores(*now)
                    if turned:
                        transposes(*turned)
                    if used:
                        outputs(*used)
                    stage(a.plus(1), i)

                pe.wait_ge(loaded, LOADS)
                pe.wait_ge(ready, READY)
                for s in range(UNITS):
                    stage(At(0, 0, 0), s)
                attentions(pe, step)

            @block.scalar
            def _(act):
                def edge(a, bank, what, k, dst):
                    act.wait_ge(mm[bank], (count0, count1)[bank](a, what) + 1)
                    col = 3 * a.node + k
                    nc.scalar.activation(dst[:, :], J[bank][:, 0:GT], ACT.Identity, bias=be[:, col:col + 1],
                                         scale=ew[:, col:col + 1]).then_inc(out[bank], 1)

                def stage(a, s):
                    g = a.slot
                    if prepares(a):
                        if s == 0 and a.k < 2:
                            act.wait_ge(mm[0], count0(a, "tokens") + 1)
                            nc.scalar.copy(nodes[0][g][:, :], J[0][:, 0:GT]).then_inc(out[0], 1)
                        if s == 1:
                            edge(a, 1, "key", 1, kinT[g])
                        if s == 2:
                            act.wait_ge(mm[1], count1(a, "Wk") + 1)
                            after(act, k_ready, a.n)
                            nc.scalar.copy(kT[:, :], J[1][:, 0:GT]).then_inc(out[1], 1)
                        if s == 5:
                            edge(a, 0, "query", 0, qinT[g])
                        if s == 6:
                            act.wait_ge(mm[0], count0(a, "Wq") + 1)
                            nc.scalar.copy(qT[g][:, :], J[0][:, 0:GT]).then_inc(out[0], 1)
                    if s == 6 and a.k < 2:
                        act.wait_ge(mm[1], count1(a, "last") + 1)
                        if finishes(a):
                            act.wait_ge(out_chain, 1 + (a.group - 2) * OUT_STEPS)
                            nc.scalar.copy(last[:, :, :].rearrange("q b d -> q (b d)"), J[1][0:S, :]).then_inc(out[1], 1)
                        else:
                            act.sem_inc(out[1], 1)
                    if s == 6 and prepares(a):
                        edge(a, 1, "value", 2, vinT[g])
                    if s == 7 and prepares(a):
                        act.wait_ge(mm[1], count1(a, "Wv") + 1)
                        nc.scalar.copy(v[g][:, :, :].rearrange("k b d -> k (b d)"), J[1][0:S, :]).then_inc(out[1], 1)

                def exponentials(a, i, u):
                    act.wait_ge(top_done, u + 1)
                    after(act, t_mm, u - 3)
                    for h in range(UH):
                        ins = nc.scalar.activation(probs[i % 4][:, h, :], s_ps[i % 2][0:S, h * S:h * S + S], ACT.Exp,
                                                   bias=neg_top[i % 2][:, h:h + 1], scale=SCALE)
                    ins.then_inc(exp_done, 1)

                def transposed(a, i, u):
                    act.wait_ge(t_mm, u + 1)
                    after(act, v_mm, u - 1)
                    nc.scalar.copy(probsT[i % 2][:, :, :].rearrange("k h q -> k (h q)"), t_ps[i % 2][0:S, 0:UH * S]
                                   ).then_inc(t_out, 1)

                def half_out(a, half):
                    act.wait_ge(v_mm, a.n * UNITS + GB * (half + 1))
                    nc.scalar.copy(oT[half][:, :], o_ps[half][:, 0:GT]).then_inc(o_out[half], 1)

                def step(a, i):
                    now, turned = unit(a, i, 0), unit(a, i, 3)
                    if i in (0, 4) and unit(a, i, 5):
                        half_out(a.plus(-1), i // 4)
                    if turned:
                        transposed(*turned)
                    if now:
                        exponentials(*now)
                    stage(a.plus(1), i)

                act.wait_ge(ready, READY)
                act.wait_ge(loaded, LOADS)
                for s in range(UNITS):
                    stage(At(0, 0, 0), s)
                attentions(act, step)

            @block.vector
            def _(dve):
                chain_in, chain_out = Chain(dve, in_chain, 2 * GB + 1), Chain(dve, out_chain, OUT_STEPS, 1)
                dve.sem_inc(out_chain, 1)

                def norm_in(a, part):
                    if part == 0:
                        chain_in.begin(a.group)
                        norm_sums(chain_in, nc, sh.x[:, bass.ds(a.group * GB, GB), :], ln_in)
                    else:
                        norm_variance(chain_in, nc, ln_in, LN_EPS, in_var)
                        chain_in.end()

                def place_z(a):
                    dve.wait_ge(in_rstd, a.group + 1)
                    for b in range(GB):
                        ins = nc.vector.tensor_scalar(z[:, b, :], sh.x[:, a.group * GB + b, :], ln_in.mv[:, b, 0:1],
                                                      ln_in.rstd[:, b:b + 1], ALU.subtract, ALU.mult)
                    ins.then_inc(z_ready, 1)

                def norm_out(a, part):
                    g = a.group - 2
                    x = sh.x[:, bass.ds(g * GB, GB), :]
                    if part == 0:
                        chain_out.begin(g)
                        dve.wait_ge(out[1], count1(a, "last") + 1)
                        norm_sums(chain_out, nc, last, ln_out)
                    if part == 1:
                        norm_variance(chain_out, nc, ln_out, L0_LN_EPS, out_var)
                    if part == 2:
                        dve.wait_ge(out_rstd, g + 1)
                        for b in range(GB):
                            chain_out.count(nc.vector.tensor_scalar(y[:, b, :], last[:, b, :], ln_out.mv[:, b, 0:1],
                                                                    ln_out.rstd[:, b:b + 1], ALU.subtract, ALU.mult))
                        chain_out.wait()
                    if part == 3:
                        chain_out.link(nc.vector.tensor_tensor(y[:, :, :], y[:, :, :], gain[:, :].unsqueeze(1).to_broadcast([S, GB, D]), ALU.mult))
                        chain_out.link(nc.vector.tensor_tensor(y[:, :, :], y[:, :, :], shift[:, :].unsqueeze(1).to_broadcast([S, GB, D]), ALU.add))
                        chain_out.link(nc.vector.tensor_tensor(x, x, y[:, :, :], ALU.add))
                        chain_out.end()

                def stage(a, s):
                    g, n = a.slot, a.node
                    following = a.plus(1)
                    if s == 4:
                        dve.wait_ge(mm[0], count0(a, "Wo") + 1)
                        if finishes(a):
                            node = a.plus(-2).node
                            nc.vector.scalar_tensor_tensor(nodes[node + 1][g][:, :], J[0][:, 0:GT], act_w[:, node:node + 1],
                                                           qinT[g][:, :], ALU.mult, ALU.add).then_inc(out[0], 1)
                        else:
                            dve.sem_inc(out[0], 1)
                    if prepares(following) and following.k < 2:
                        if s in (5, 6):
                            norm_in(following, s - 5)
                        if s == 7:
                            place_z(following)
                    before = a.plus(-1)
                    if s < 4 and before.k < 2 and finishes(before):
                        norm_out(before, s)

                def maxima(a, i, u):
                    dve.wait_ge(s_mm, u + 1)
                    nc.vector.tensor_reduce(top[i % 2][:, :], s_ps[i % 2][0:S, 0:UH * S].rearrange("q (h k) -> q h k", h=UH),
                                            AX_X, ALU.max).then_inc(raw_top, 1)
                    dve.wait_ge(raw_top, u + 1)
                    nc.vector.tensor_scalar(neg_top[i % 2][:, :], top[i % 2][:, :], -SCALE, None, ALU.mult).then_inc(top_done, 1)

                def invert(a, i, u):
                    dve.wait_ge(exp_done, u + 1)
                    nc.vector.tensor_reduce(sums[i % 4][:, :], probs[i % 4][:, :, :], AX_X, ALU.add).then_inc(sum_done, 1)
                    dve.wait_ge(sum_done, u + 1)
                    nc.vector.reciprocal(sums[i % 4][:, :], sums[i % 4][:, :]).then_inc(r_done, 1)

                def step(a, i):
                    now, summed = unit(a, i, 0), unit(a, i, 1)
                    if now:
                        maxima(*now)
                    if summed:
                        invert(*summed)
                    stage(a.plus(1), i)

                nc.vector.memset(wo[:, :, :, :], 0.0).then_inc(ready, 1)
                for half in range(2):
                    nc.vector.memset(o_ps[half][:, :], 0.0).then_inc(ready, 1)
                norm_in(At(0, 0, 0), 0)
                norm_in(At(0, 0, 0), 1)
                place_z(At(0, 0, 0))
                dve.wait_ge(loaded, LOADS)
                nc.vector.tensor_tensor(be[:, :], be[:, :], ew[:, :], ALU.mult).then_inc(ready, 1)
                nc.vector.tensor_scalar(gain[:, :], gain[:, :], tanh_g, None, ALU.mult).then_inc(ready, 1)
                nc.vector.tensor_scalar(shift[:, :], shift[:, :], tanh_g, None, ALU.mult).then_inc(ready, 1)
                dve.wait_ge(ready, READY)
                for s in range(UNITS):
                    stage(At(0, 0, 0), s)
                attentions(dve, step)
                for part in range(4):
                    norm_out(At(TOTAL + 1, GROUPS // 2, 1), part)


class Group:

    def __init__(self, n, pair, slot):
        self.n, self.pair, self.slot = n, pair, slot

    def plus(self, d):
        return Group(self.n + d, self.pair + (self.slot + d) // 2, (self.slot + d) % 2)


def moe_ffn(nc, ctx, sh, A):
    E, F, TOP = 8, 512, 2
    FT = F // P
    HIDDEN = E * FT
    HEADS, SIZE = 16, D // 16
    QUARTERS = HEADS // UH
    UNITS = GB * QUARTERS
    SCALE = float(SIZE) ** -0.5
    tanh_g = sh.tanh_g[0:S, 3:4]
    CAUSAL = -float(2 ** 100)
    ORDER0 = ("tokens", "query", "back0", "back1", "back2", "back3", "out")
    ORDER1 = ("key", "Wo", "value")
    PREPARE = ("tokens", "query", "key", "value")

    def count(a, what, order):
        prepare = tuple(n for n in order if n in PREPARE)
        finish = tuple(n for n in order if n not in PREPARE)
        if isinstance(a.n, int) and a.n < 2:
            return a.n * len(prepare) + prepare.index(what)
        if isinstance(a.n, int) and a.n >= GROUPS:
            return 2 * len(prepare) + (GROUPS - 2) * len(order) + (a.n - GROUPS) * len(finish) + finish.index(what)
        return (a.n - 2) * len(order) + 2 * len(prepare) + order.index(what)

    def count0(a, what):
        return count(a, what, ORDER0)

    def count1(a, what):
        return count(a, what, ORDER1)

    STAGED0 = count0(Group(GROUPS + 1, 0, 0), "out") + 1
    STAGED1 = count1(Group(GROUPS + 1, 0, 0), "Wo") + 1

    def known(a):
        return isinstance(a.n, int)

    def prepares(a):
        return not known(a) or a.n < GROUPS

    def finishes(a):
        return not known(a) or a.n >= 2

    c = ExitStack()
    with c:
        def sb(name, shape, dt=F32):
            return c.enter_context(nc.sbuf_tensor(f"moe_{name}", shape, dt))

        def sem(name):
            return ctx.enter_context(nc.semaphore(f"moe_{name}"))

        def ps(name):
            return c.enter_context(nc.psum_tensor(f"moe_{name}", [P, 512], F32))

        def two(name, shape):
            return [sb(f"{name}{r}", shape) for r in range(2)]

        wqkv, wo, w_gate = sb("wqkv", [D, 3, D]), sb("wo", [D, D]), sb("w_gate", [D, E])
        w1, w2 = sb("w1", [D, E, F]), sb("w2", [P, E, FT, D])
        b1_rows = sb("b1_rows", [HIDDEN, P])
        b1, b2 = sb("b1", [P, E, FT]), sb("b2", [E, D])
        norms = {n: sb(n, [S, D]) for n in ("ln1_g", "ln1_b", "ln2_g", "ln2_b")}
        causal = sb("causal", [S, S], BF16)
        before = sb("before", [S, E, E])
        xi = sb("xi", [S, B, D])
        h = sb("h", [S, GB, D])
        hT = sb("hT", [D, GT])
        qT, k_bd = two("qT", [D, GT]), two("k_bd", [D, GB, HEADS, S])
        kT = sb("kT", [D, GT])
        v = two("v", [S, GB, HEADS, SIZE + 1])
        xfT = two("xfT", [D, GT])
        p = {n: two(n, [S, GB, E]) for n in ("shifted", "exps", "prob", "rank", "kept", "gate")}
        one = {n: two(n, [S, GB]) for n in ("best", "total", "norm", "kept_sum")}
        gateT = two("gateT", [E, GT])
        top, neg_top = two("top", [S, UH]), two("neg_top", [S, UH])
        probs = [sb(f"probs{r}", [S, UH, S]) for r in range(4)]
        probsT = two("probsT", [S, UH, S])
        oT = [sb(f"oT{r}", [P, GT]) for r in range(QUARTERS)]
        rden, o_n, o_nT = sb("rden", [S, HEADS]), sb("o_n", [S, GB, D]), sb("o_nT", [D, GT])
        above, same = sb("above", [S, GB, E, E]), sb("same", [S, GB, E, E])
        act_h = [sb(f"act_h{r}", [P, GT]) for r in range(2 * FT)]
        ln = LayerNorm(c, nc, "moe_ln", S, sh.minus_half, GB)
        J, s_ps, t_ps, o_ps = ([ps(f"{n}{r}") for r in range(2)] for n in ("J", "s_ps", "t_ps", "o_ps"))
        h_ps, y_ps = s_ps + o_ps, t_ps

        loaded, experts_loaded, made, ready = sem("loaded"), sem("experts_loaded"), sem("made"), sem("ready")
        b1_ready = sem("b1_ready")
        var_ready, rstd_ready = sem("var_ready"), sem("rstd_ready")
        tokens = sem("tokens")
        k_ready = sem("k_ready")
        mm = [sem("J0_mm"), sem("J1_mm")]
        out = [sem("J0_out"), sem("J1_out")]
        s_mm = sem("s_mm")
        raw_top = sem("raw_top")
        top_done = sem("top_done")
        exp_done = sem("exp_done")
        t_mm = sem("t_mm")
        t_out = sem("t_out")
        v_mm = sem("v_mm")
        o_out = sem("o_out")
        r_done = sem("r_done")
        norm_chain, gate_chain, add_chain = sem("norm_chain"), sem("gate_chain"), sem("add_chain")
        inputs = sem("inputs")
        shifted_ready, exps_ready = sem("shifted_ready"), sem("exps_ready")
        gate_ready = sem("gate_ready")
        h_mm, h_act = sem("h_mm"), sem("h_act")
        y_mm, y_out = sem("y_mm"), sem("y_out")
        LOADS, EXPERT_LOADS = 16 * 7, 16 * 4
        READY = 4

        def attentions(eng, step):
            for n in range(2):
                for i in range(UNITS):
                    step(Group(n, 0, n), i)
            with eng.Fori(0, GROUPS // 2 - 2) as pair:
                for t in (2, 3):
                    for i in range(UNITS):
                        step(Group(pair * 2 + t, pair + t // 2, t % 2), i)
            for n in range(GROUPS - 2, GROUPS + 1):
                for i in range(UNITS):
                    step(Group(n, n // 2, n % 2), i)

        def experts(eng, group):
            with eng.Fori(0, GROUPS // 2 - 1) as pair:
                for t in range(2):
                    group(Group(pair * 2 + t, pair, t), True)
            group(Group(GROUPS - 2, GROUPS // 2 - 1, 0), True)
            group(Group(GROUPS - 1, GROUPS // 2 - 1, 1), False)

        def unit(a, i, back):
            u, j = a.plus((i - back) // UNITS), (i - back) % UNITS
            if known(u) and not 0 <= u.n < GROUPS:
                return None
            return u, j, u.n * UNITS + j

        def gates0(a, k):
            return a.n * 2 + STAGED0 + k

        def gates1(a, k):
            return a.n * 2 + STAGED1 + k

        with nc.Block() as block:
            @block.sync
            def _(sp):
                for dst, src in (
                    (wqkv[:, :, :], A["L1_ffn_w_qkv"].rearrange("i (k o) -> i k o", k=3)), (wo[:, :], A["L1_ffn_w_o"]),
                    (b1_rows[:, :], A["L1_ffn_b1"].rearrange("e (t p) -> (e t) p", p=P)),
                ) + tuple((norms[n][:, :], A["L1_ffn_" + n].partition_broadcast(S)) for n in norms):
                    sp.dma_start(dst, src).then_inc(loaded, 16)
                for dst, src in (
                    (w_gate[:, :], A["L1_ffn_w_gate"]), (b2[:, :], A["L1_ffn_b2"]),
                    (w1[:, :, :], A["L1_ffn_w1"].rearrange("e d f -> d e f")),
                    (w2[:, :, :, :], A["L1_ffn_w2"].rearrange("e (t p) d -> p e t d", p=P)),
                ):
                    sp.dma_start(dst, src).then_inc(experts_loaded, 16)

            @block.gpsimd
            def _(pool):
                def root(at):
                    pool.wait_ge(var_ready, at + 1)
                    ln.inverse_root(nc).then_inc(rstd_ready, 1)

                def stage(a, s):
                    following = a.plus(1)
                    if prepares(a) and s in (3, 5, 7, 10):
                        b = (s - 3) // 2
                        if b == 0:
                            pool.wait_ge(out[1], count1(a, "key") + 1)
                        ins = nc.gpsimd.tensor_tensor(k_bd[a.slot][:, b, :, :],
                                                      kT[:, b * S:b * S + S].unsqueeze(1).to_broadcast([D, HEADS, S]),
                                                      sh.head16[:, :].unsqueeze(2).to_broadcast([D, HEADS, S]), ALU.mult)
                        if b == GB - 1:
                            ins.then_inc(k_ready, 1)
                    if prepares(following) and s in (9, 13):
                        root(following.n * 2 + (s - 9) // 4)

                def step(a, i):
                    stage(a.plus(1), i)

                pool.memset(causal[:, :], 0.0).then_inc(made, 1)
                pool.memset(before[:, :, :], 0.0).then_inc(made, 1)
                pool.wait_ge(made, 2)
                pool.affine_select(out=causal[:, :], in_=causal[:, :], compare_op=ALU.is_ge, fill=CAUSAL, base=0,
                                   pattern=[[-1, S]], channel_multiplier=1).then_inc(made, 1)
                pool.affine_select(out=before[:, :, :], in_=before[:, :, :], compare_op=ALU.is_ge, fill=1.0, base=0,
                                   pattern=[[-1, E], [1, E]], channel_multiplier=0).then_inc(made, 1)
                root(0)
                root(1)
                for s in range(UNITS):
                    stage(Group(0, 0, 0), s)
                attentions(pool, step)
                with pool.Fori(0, GROUPS) as g:
                    root(g + 2 * GROUPS)

            @block.tensor
            def _(pe):
                def wide(bank, lhsT, rhs):
                    return nc.tensor.matmul(J[bank][:, 0:GT], lhsT, rhs, start=True, stop=True)

                def turn_tokens(bank, src):
                    for b in range(GB):
                        ins = nc.tensor.transpose(J[bank][:, b * S:b * S + S], src[:, b, :], sh.ident[0:S, 0:S])
                    return ins

                def per_batch(bank, lhsT, rhs, n):
                    for b in range(GB):
                        ins = nc.tensor.matmul(J[bank][0:S, b * n:b * n + n], lhsT[:, b * S:b * S + S], rhs, start=True, stop=True)
                    return ins

                def stage(a, s):
                    if prepares(a):
                        if s == 1:
                            pe.wait_ge(tokens, a.n + 1)
                            after(pe, out[0], count0(a, "tokens"))
                            turn_tokens(0, h).then_inc(mm[0], 1)
                        if s == 2:
                            pe.wait_ge(out[0], count0(a, "query"))
                            after(pe, out[1], count1(a, "key"))
                            wide(1, wqkv[:, 1, :], hT[:, :]).then_inc(mm[1], 1)
                            wide(0, wqkv[:, 0, :], hT[:, :]).then_inc(mm[0], 1)
                    if finishes(a):
                        if 4 <= s < 4 + GB:
                            b = s - 4
                            if b == 0:
                                pe.wait_ge(o_out, (a.n - 1) * QUARTERS)
                            pe.wait_ge(out[0], count0(a, f"back{b}"))
                            for r in range(QUARTERS):
                                ins = nc.tensor.transpose(J[0][0:S, r * P:r * P + P], oT[r][:, b * S:b * S + S], sh.ident[:, :])
                            ins.then_inc(mm[0], 1)
                        if s == 9:
                            pe.wait_ge(out[0], count0(a, "out"))
                            turn_tokens(0, o_n).then_inc(mm[0], 1)
                        if s == 11:
                            pe.wait_ge(out[0], count0(a, "out") + 1)
                            pe.wait_ge(out[1], count1(a, "Wo"))
                            per_batch(1, o_nT, wo[:, :], D).then_inc(mm[1], 1)
                    if prepares(a) and s == 12:
                        pe.wait_ge(out[1], count1(a, "value"))
                        per_batch(1, hT, wqkv[:, 2, :], D).then_inc(mm[1], 1)

                def scores(a, i, u):
                    part, b, g = i // GB, i % GB, a.slot
                    if i == 0:
                        pe.wait_ge(out[0], count0(a, "query") + 1)
                        pe.wait_ge(k_ready, a.n + 1)
                    after(pe, exp_done, u - 1)
                    bank = s_ps[i % 2][0:S, 0:UH * S]
                    nc.tensor.matmul(bank, qT[g][:, b * S:b * S + S],
                                     k_bd[g][:, b, UH * part:UH * part + UH, :].rearrange("d h k -> d (h k)"),
                                     start=True, stop=False)
                    nc.tensor.matmul(bank.rearrange("q (h k) -> q h k", h=UH), sh.ident_bf[0:S, 0:S],
                                     causal[:, :].unsqueeze(1).to_broadcast([S, UH, S]), start=False, stop=True
                                     ).then_inc(s_mm, 1)

                def transposes(a, i, u):
                    pe.wait_ge(exp_done, u + 1)
                    after(pe, t_out, u - 1)
                    for k in range(UH):
                        ins = nc.tensor.transpose(t_ps[i % 2][0:S, k * S:k * S + S], probs[i % 4][:, k, :], sh.ident[0:S, 0:S])
                    ins.then_inc(t_mm, 1)

                def outputs(a, i, u):
                    part, b, g = i // GB, i % GB, a.slot
                    if i == 0:
                        pe.wait_ge(out[1], count1(a, "value") + 1)
                    if b == 0:
                        after(pe, o_out, a.n * QUARTERS + part - 1)
                    pe.wait_ge(t_out, u + 1)
                    for k in range(UH):
                        ins = nc.tensor.matmul(o_ps[part % 2][32 * k:32 * k + SIZE + 1, b * S:b * S + S],
                                               v[g][:, b, UH * part + k, :], probsT[i % 2][:, k, :],
                                               start=True, stop=True, skip_group_check=True)
                    ins.then_inc(v_mm, 1)

                def step(a, i):
                    now, turned, used = unit(a, i, 0), unit(a, i, 2), unit(a, i, 3)
                    if now:
                        scores(*now)
                    if turned:
                        transposes(*turned)
                    if used:
                        outputs(*used)
                    stage(a.plus(1), i)

                def gates(a, k):
                    g = a.slot
                    if k == 0:
                        pe.wait_ge(inputs, a.n + 1)
                        pe.wait_ge(out[0], gates0(a, 0))
                        turn_tokens(0, h).then_inc(mm[0], 1)
                    if k == 1:
                        pe.wait_ge(out[0], gates0(a, 1))
                        pe.wait_ge(out[1], gates1(a, 0))
                        per_batch(1, xfT[g], w_gate[:, :], E).then_inc(mm[1], 1)
                    if k == 2:
                        pe.wait_ge(gate_ready, a.n + 1)
                        for b in range(GB):
                            ins = nc.tensor.transpose(J[0][0:E, b * S:b * S + S], p["gate"][g][:, b, :], sh.ident[0:S, 0:S])
                        ins.then_inc(mm[0], 1)
                    if k == 3:
                        pe.wait_ge(out[0], gates0(a, 2))
                        pe.wait_ge(out[1], gates1(a, 1))
                        per_batch(1, gateT[g], b2[:, :], D).then_inc(mm[1], 1)

                def inner(a, i):
                    e, t = i // FT, i % FT
                    if i == 0:
                        pe.wait_ge(out[0], gates0(a, 1))
                    pe.wait_ge(h_act, 1 + a.n * HIDDEN + max(i - 3, 0))
                    nc.tensor.matmul(h_ps[i % 4][:, 0:GT], w1[:, e, t * P:t * P + P], xfT[a.slot][:, :], start=True, stop=True
                                     ).then_inc(h_mm, 1)

                def outer(a, e):
                    pe.wait_ge(y_out, 1 + a.n * E + max(e - 1, 0))
                    pe.wait_ge(h_act, a.n * HIDDEN + (e + 1) * FT + 1)
                    for b in range(GB):
                        for t in range(FT):
                            ins = nc.tensor.matmul(y_ps[e % 2][0:S, b * D:b * D + D],
                                                   act_h[(e % 2) * FT + t][:, b * S:b * S + S], w2[:, e, t, :],
                                                   start=(t == 0), stop=(t == FT - 1))
                    ins.then_inc(y_mm, 1)

                def group(a, ahead):
                    for e in range(E + 1):
                        if e < E:
                            for t in range(FT):
                                inner(a, e * FT + t)
                        if ahead and e in (2, 3, 7, 8):
                            gates(a.plus(1), (2, 3, 7, 8).index(e))
                        if e > 0:
                            outer(a, e - 1)

                pe.wait_ge(loaded, LOADS)
                pe.wait_ge(made, 4)
                pe.wait_ge(ready, READY)
                nc.tensor.transpose(J[0][:, 0:HIDDEN], b1_rows[:, :], sh.ident[0:HIDDEN, 0:HIDDEN]).then_inc(b1_ready, 1)
                pe.wait_ge(b1_ready, 2)
                for s in range(UNITS):
                    stage(Group(0, 0, 0), s)
                attentions(pe, step)
                pe.wait_ge(experts_loaded, EXPERT_LOADS)
                pe.wait_ge(exp_done, GROUPS * UNITS)
                pe.wait_ge(t_out, GROUPS * UNITS)
                pe.wait_ge(o_out, GROUPS * QUARTERS)
                for k in range(4):
                    gates(Group(0, 0, 0), k)
                experts(pe, group)

            @block.scalar
            def _(act):
                def stage(a, s):
                    if prepares(a):
                        if s == 1:
                            act.wait_ge(mm[0], count0(a, "tokens") + 1)
                            if finishes(a):
                                act.wait_ge(mm[1], count1(a, "key"))
                            nc.scalar.copy(hT[:, :], J[0][:, 0:GT]).then_inc(out[0], 1)
                        if s == 2:
                            act.wait_ge(mm[0], count0(a, "query") + 1)
                            nc.scalar.copy(qT[a.slot][:, :], J[0][:, 0:GT]).then_inc(out[0], 1)
                            after(act, k_ready, a.n)
                            nc.scalar.copy(kT[:, :], J[1][:, 0:GT]).then_inc(out[1], 1)
                    if finishes(a) and s == 9:
                        act.wait_ge(mm[0], count0(a, "out") + 1)
                        nc.scalar.copy(o_nT[:, :], J[0][:, 0:GT]).then_inc(out[0], 1)
                    if prepares(a) and s == 12:
                        act.wait_ge(mm[1], count1(a, "value") + 1)
                        nc.scalar.copy(v[a.slot][:, :, :, 0:SIZE].rearrange("k b h d -> k (b h) d"),
                                       J[1][0:S, :].rearrange("k (c d) -> k c d", d=SIZE)).then_inc(out[1], 1)

                def exponentials(a, i, u):
                    act.wait_ge(top_done, u + 1)
                    after(act, t_mm, u - 3)
                    for k in range(UH):
                        ins = nc.scalar.activation(probs[i % 4][:, k, :], s_ps[i % 2][0:S, k * S:k * S + S], ACT.Exp,
                                                   bias=neg_top[i % 2][:, k:k + 1], scale=SCALE)
                    ins.then_inc(exp_done, 1)

                def transposed(a, i, u):
                    act.wait_ge(t_mm, u + 1)
                    after(act, v_mm, u - 1)
                    nc.scalar.copy(probsT[i % 2][:, :, :].rearrange("k h q -> k (h q)"), t_ps[i % 2][0:S, 0:UH * S]
                                   ).then_inc(t_out, 1)

                def quarter_out(a, i, u):
                    part = i // GB
                    act.wait_ge(v_mm, u + 1)
                    nc.scalar.copy(oT[part][:, :], o_ps[part % 2][:, 0:GT]).then_inc(o_out, 1)

                def step(a, i):
                    now, turned = unit(a, i, 0), unit(a, i, 2)
                    ended = unit(a, i, 5 if i == 8 else 4) if i in (3, 8, 11, 15) else None
                    if ended:
                        if i == 8 and finishes(a.plus(1)):
                            act.wait_ge(mm[0], count0(a.plus(1), "back3") + 1)
                        quarter_out(*ended)
                    if turned:
                        transposed(*turned)
                    if now:
                        exponentials(*now)
                    stage(a.plus(1), i)

                def gates(a, k):
                    g = a.slot
                    if k == 0:
                        act.wait_ge(mm[0], gates0(a, 1))
                        nc.scalar.copy(xfT[g][:, :], J[0][:, 0:GT]).then_inc(out[0], 1)
                    if k == 1:
                        act.wait_ge(shifted_ready, a.n + 1)
                        nc.scalar.activation(p["exps"][g][:, :, :], p["shifted"][g][:, :, :], ACT.Exp).then_inc(exps_ready, 1)
                    if k == 2:
                        act.wait_ge(mm[0], gates0(a, 2))
                        nc.scalar.copy(gateT[g][:, :], J[0][0:E, 0:GT]).then_inc(out[0], 1)

                def group(a, ahead):
                    for i in range(HIDDEN):
                        e, t = i // FT, i % FT
                        act.wait_ge(h_mm, a.n * HIDDEN + i + 1)
                        if e >= 2:
                            act.wait_ge(y_mm, a.n * E + e - 1)
                        nc.scalar.activation(act_h[i % (2 * FT)][:, :], h_ps[i % 4][:, 0:GT], ACT.Gelu_apprx_tanh,
                                             bias=b1[:, e, t:t + 1]).then_inc(h_act, 1)
                        if ahead and t == FT - 1 and e in (2, 4, 7):
                            gates(a.plus(1), (2, 4, 7).index(e))

                act.wait_ge(ready, READY)
                act.wait_ge(b1_ready, 1)
                nc.scalar.copy(b1[:, :, :].rearrange("p e t -> p (e t)"), J[0][:, 0:HIDDEN]).then_inc(b1_ready, 1)
                act.wait_ge(b1_ready, 2)
                for s in range(UNITS):
                    stage(Group(0, 0, 0), s)
                attentions(act, step)
                for k in range(3):
                    gates(Group(0, 0, 0), k)
                act.sem_inc(h_act, 1)
                experts(act, group)

            @block.vector
            def _(dve):
                NORM = 3 * GB + 3
                norms_of = Chain(dve, norm_chain, NORM)

                def normalize(at, part, dst, x, gain=None, shift=None):
                    if part == 0:
                        norms_of.begin(at)
                        norm_sums(norms_of, nc, x, ln)
                    if part == 1:
                        norm_variance(norms_of, nc, ln, LN_EPS, var_ready)
                    if part == 2:
                        dve.wait_ge(rstd_ready, at + 1)
                        for b in range(GB):
                            norms_of.count(nc.vector.tensor_scalar(dst[:, b, :], x[:, b, :], ln.mv[:, b, 0:1],
                                                                   ln.rstd[:, b:b + 1], ALU.subtract, ALU.mult))
                        norms_of.wait()
                    if part == 3:
                        if gain is None:
                            dve.sem_inc(norm_chain, 2)
                            norms_of.k += 2
                        else:
                            norms_of.link(nc.vector.tensor_tensor(dst, dst, gain[:, :].unsqueeze(1).to_broadcast([S, GB, D]), ALU.mult))
                            norms_of.link(nc.vector.tensor_tensor(dst, dst, shift[:, :].unsqueeze(1).to_broadcast([S, GB, D]), ALU.add))
                        norms_of.end()

                def of_group(t, a):
                    return t[:, bass.ds(a.n * GB, GB), :]

                def attention_input(a, k):
                    if k < 4:
                        normalize(a.n * 2, k, of_group(xi, a), of_group(sh.x, a))
                    else:
                        normalize(a.n * 2 + 1, k - 4, h[:, :, :], of_group(xi, a), norms["ln1_g"], norms["ln1_b"])
                    if k == 7:
                        dve.sem_inc(tokens, 1)

                def stage(a, s):
                    following = a.plus(1)
                    if finishes(a):
                        done = a.plus(-2)
                        if 4 <= s < 4 + GB:
                            b = s - 4
                            dve.wait_ge(mm[0], count0(a, f"back{b}") + 1)
                            m = J[0][0:S, :].rearrange("q (h d) -> q h d", d=32)
                            nc.vector.reciprocal(rden[:, :], m[:, :, SIZE]).then_inc(r_done, 1)
                            dve.wait_ge(r_done, done.n * GB + b + 1)
                            nc.vector.tensor_tensor(o_n[:, b, :].rearrange("q (h d) -> q h d", d=SIZE), m[:, :, 0:SIZE],
                                                    rden[:, :].unsqueeze(2).to_broadcast([S, HEADS, SIZE]), ALU.mult
                                                    ).then_inc(out[0], 1)
                        if s == 11:
                            dve.wait_ge(mm[1], count1(a, "Wo") + 1)
                            nc.vector.tensor_tensor(of_group(xi, done), of_group(xi, done),
                                                    J[1][0:S, :].rearrange("q (b d) -> q b d", b=GB), ALU.add).then_inc(out[1], 1)
                    if prepares(following) and s >= 8:
                        if s == 14:
                            dve.wait_ge(mm[0], count0(a, "tokens") + 1)
                        attention_input(following, s - 8)

                def maxima(a, i, u):
                    dve.wait_ge(s_mm, u + 1)
                    nc.vector.tensor_reduce(top[i % 2][:, :], s_ps[i % 2][0:S, 0:UH * S].rearrange("q (h k) -> q h k", h=UH),
                                            AX_X, ALU.max).then_inc(raw_top, 1)
                    dve.wait_ge(raw_top, u + 1)
                    nc.vector.tensor_scalar(neg_top[i % 2][:, :], top[i % 2][:, :], -SCALE, None, ALU.mult).then_inc(top_done, 1)

                def step(a, i):
                    now = unit(a, i, 0)
                    if now:
                        maxima(*now)
                    stage(a.plus(1), i)

                chain = Chain(dve, gate_chain, 2 + 3 + 2 + GB + 6 + 1)

                def wide(ap):
                    return ap.unsqueeze(2).to_broadcast([S, GB, E])

                def gates(a, k):
                    g = a.slot
                    P_ = {n: t[g][:, :, :] for n, t in p.items()}
                    O_ = {n: t[g][:, :] for n, t in one.items()}
                    if k == 0:
                        dve.wait_ge(mm[0], gates0(a, 0))
                        for part in range(4):
                            normalize(a.n + 2 * GROUPS, part, h[:, :, :], of_group(xi, a), norms["ln2_g"], norms["ln2_b"])
                        dve.sem_inc(inputs, 1)
                    if k == 1:
                        chain.begin(a.n)
                        dve.wait_ge(mm[1], gates1(a, 1))
                        logits = J[1][0:S, 0:GB * E].rearrange("q (b e) -> q b e", b=GB)
                        chain.link(nc.vector.tensor_reduce(O_["best"], logits, AX_X, ALU.max))
                        chain.link(nc.vector.tensor_tensor(P_["shifted"], logits, wide(O_["best"]), ALU.subtract))
                        dve.sem_inc(out[1], 1)
                        dve.sem_inc(shifted_ready, 1)
                    if k == 2:
                        dve.wait_ge(exps_ready, a.n + 1)
                        chain.link(nc.vector.tensor_reduce(O_["total"], P_["exps"], AX_X, ALU.add))
                        chain.link(nc.vector.reciprocal(O_["norm"], O_["total"]))
                        chain.link(nc.vector.tensor_tensor(P_["prob"], P_["exps"], wide(O_["norm"]), ALU.mult))
                        other = P_["prob"].unsqueeze(2).to_broadcast([S, GB, E, E])
                        own = P_["prob"].unsqueeze(3).to_broadcast([S, GB, E, E])
                        chain.count(nc.vector.tensor_tensor(above[:, :, :, :], other, own, ALU.is_gt))
                        chain.link(nc.vector.tensor_tensor(same[:, :, :, :], other, own, ALU.is_equal))
                        for b in range(GB):
                            chain.count(nc.vector.tensor_tensor(same[:, b, :, :], same[:, b, :, :], before[:, :, :], ALU.mult))
                        chain.wait()
                        chain.link(nc.vector.tensor_tensor(above[:, :, :, :], above[:, :, :, :], same[:, :, :, :], ALU.add))
                        chain.link(nc.vector.tensor_reduce(P_["rank"], above[:, :, :, :], AX_X, ALU.add))
                        chain.link(nc.vector.scalar_tensor_tensor(P_["kept"], P_["rank"], TOP - 0.5, P_["prob"], ALU.is_lt, ALU.mult))
                        chain.link(nc.vector.tensor_reduce(O_["kept_sum"], P_["kept"], AX_X, ALU.add))
                        chain.link(nc.vector.reciprocal(O_["norm"], O_["kept_sum"]))
                        chain.link(nc.vector.tensor_tensor(P_["gate"], P_["kept"], wide(O_["norm"]), ALU.mult))
                        dve.sem_inc(gate_ready, 1)
                    if k == 3:
                        dve.wait_ge(mm[1], gates1(a, 2))
                        chain.link(nc.vector.tensor_tensor(of_group(xi, a), of_group(xi, a),
                                                           J[1][0:S, :].rearrange("q (b d) -> q b d", b=GB), ALU.add))
                        dve.sem_inc(out[1], 1)
                        chain.end()

                added = Chain(dve, add_chain, E * GB + 1)

                def group(a, ahead):
                    added.begin(a.n)
                    if ahead:
                        gates(a.plus(1), 0)
                    for e in range(E):
                        dve.wait_ge(y_mm, a.n * E + e + 1)
                        for b in range(GB):
                            row = xi[:, a.n * GB + b, :]
                            added.count(nc.vector.scalar_tensor_tensor(row, y_ps[e % 2][0:S, b * D:b * D + D],
                                                                       p["gate"][a.slot][:, b, e:e + 1], row, ALU.mult, ALU.add))
                        added.wait()
                        dve.sem_inc(y_out, 1)
                        if ahead and e in (2, 4, 6):
                            gates(a.plus(1), e // 2)
                    added.link(nc.vector.scalar_tensor_tensor(of_group(sh.x, a), of_group(xi, a), tanh_g, of_group(sh.x, a),
                                                              ALU.mult, ALU.add))
                    added.end()

                for g in range(2):
                    nc.vector.memset(v[g][:, :, :, :], 1.0).then_inc(ready, 1)
                    nc.vector.memset(o_ps[g][:, :], 0.0).then_inc(ready, 1)
                dve.wait_ge(ready, READY)
                dve.wait_ge(loaded, LOADS)
                dve.wait_ge(made, 4)
                for k in range(8):
                    attention_input(Group(0, 0, 0), k)
                for s in range(UNITS):
                    stage(Group(0, 0, 0), s)
                attentions(dve, step)
                dve.sem_inc(y_out, 1)
                for k in range(4):
                    gates(Group(0, 0, 0), k)
                experts(dve, group)


def build_program(nc, A, out, phases=(1, 2, 3, 4)):
    nc.disable_value_cache = True
    with ExitStack() as ctx:
        sh = setup(nc, ctx, A)
        if 1 in phases:
            cross_attention(nc, ctx, sh, A, 0)
        if 2 in phases:
            cell_ffn(nc, ctx, sh, A)
        if 3 in phases:
            cross_attention(nc, ctx, sh, A, 1)
        if 4 in phases:
            moe_ffn(nc, ctx, sh, A)
        stored = ctx.enter_context(nc.semaphore("stored"))
        with nc.Block() as block:
            @block.sync
            def _(sp):
                sp.dma_start(out.rearrange("b s d -> s b d"), sh.x[:, :, :]).then_inc(stored, 16)
                sp.wait_ge(stored, 16)


def kernel(**inputs):
    import numpy as _np
    import concourse.bacc as _bacc
    from concourse import mybir as _mybir
    from concourse.bass_utils import run_bass_kernel_spmd as _run

    nc = _bacc.Bacc("TRN2", target_bir_lowering=False, num_devices=1)
    arrays, A = {}, {}
    for name, value in inputs.items():
        a = _np.ascontiguousarray(value)
        arrays[f"in_{name}"] = a
        A[name] = nc.dram_tensor(f"in_{name}", a.shape, _mybir.dt.from_np(a.dtype), kind="ExternalInput").ap()
    out = nc.dram_tensor("out_x", (B, S, D), F32, kind="ExternalOutput").ap()
    build_program(nc, A, out)
    r = _run(nc, [arrays], core_ids=[0])
    return r.results[0]["out_x"]
```
